# Optimizing a Trainium2 kernel written in Bass

```python
import numpy as np
import jax
import jax.numpy as jnp

def _softmax(x, axis=-1):
    return jax.nn.softmax(x, axis=axis)

def _gelu(x):
    return jax.nn.gelu(x, approximate=True)

def _silu(x):
    return jax.nn.silu(x)

def _sigmoid(x):
    return jax.nn.sigmoid(x)

def _layernorm(x, axis=-1, eps=1e-05):
    m = jnp.mean(x, axis=axis, keepdims=True)
    v = jnp.var(x, axis=axis, keepdims=True)
    return (x - m) / jnp.sqrt(v + eps)

def _scatter_add(tgt, idx, src, axis=0):
    return tgt.at[idx].add(src)

def _segment_sum(src, seg, n):
    return jax.ops.segment_sum(src, seg, n)
kernel_name = 'mk_prb_d2_jaxref_r8_787103'

def setup_inputs(seed: int=0):
    np.random.seed(seed)
    _w = jnp.asarray

    def _L0_attn_setup():
        import jax, jax.numpy as jnp
        import numpy as np
        import math
        B, S, D, H = (4, 256, 128, 16)
        HD = D // H
        key = jax.random.key(seed)
        ks = jax.random.split(key, 9)
        scale = 1.0 / math.sqrt(D)
        inputs = jax.random.normal(ks[0], (B, S, D), dtype=jnp.float32)
        W_q = jax.random.uniform(ks[1], (H, D, HD), minval=-scale, maxval=scale)
        b_q = jax.random.uniform(ks[2], (H, HD), minval=-scale, maxval=scale)
        W_k = jax.random.uniform(ks[3], (H, D, HD), minval=-scale, maxval=scale)
        b_k = jax.random.uniform(ks[4], (H, HD), minval=-scale, maxval=scale)
        W_v = jax.random.uniform(ks[5], (H, D, HD), minval=-scale, maxval=scale)
        b_v = jax.random.uniform(ks[6], (H, HD), minval=-scale, maxval=scale)
        W_o = jax.random.uniform(ks[7], (D, D), minval=-scale, maxval=scale)
        b_o = jax.random.uniform(ks[8], (D,), minval=-scale, maxval=scale)
        return {'inputs': inputs, 'W_q': W_q, 'b_q': b_q, 'W_k': W_k, 'b_k': b_k, 'W_v': W_v, 'b_v': b_v, 'W_o': W_o, 'b_o': b_o}
    _L0_attn_in = _L0_attn_setup()

    def _L0_ffn_setup():
        import jax, jax.numpy as jnp
        import numpy as np
        from jax import lax
        T, B, I, M, O = (32, 64, 128, 128, 128)

        def _xavier(key, shape):
            fan_out, fan_in = shape
            limit = float(np.sqrt(6.0 / (fan_in + fan_out)))
            return jax.random.uniform(key, shape, jnp.float32, -limit, limit)
        key = jax.random.key(seed)
        ks = jax.random.split(key, 9)
        x = jax.random.normal(ks[0], (T, B, I), jnp.float32)
        return {'x': x, 'wf': _xavier(ks[1], (M, I)), 'uf': _xavier(ks[2], (M, M)), 'bf': jnp.zeros((M,), jnp.float32), 'wi': _xavier(ks[3], (M, I)), 'ui': _xavier(ks[4], (M, M)), 'bi': jnp.zeros((M,), jnp.float32), 'wc': _xavier(ks[5], (M, I)), 'uc': _xavier(ks[6], (M, M)), 'bc': jnp.zeros((M,), jnp.float32), 'wo': _xavier(ks[7], (O, I)), 'uo': _xavier(ks[8], (O, M)), 'bo': jnp.zeros((O,), jnp.float32), 'in_c': jnp.zeros((M,), jnp.float32)}
    _L0_ffn_in = _L0_ffn_setup()

    def _L1_attn_setup():
        import jax, jax.numpy as jnp
        import numpy as np
        EMBED_DIM = 128
        NUM_HEADS = 16
        HEAD_DIM = EMBED_DIM // NUM_HEADS
        MAX_REL = 16
        key = jax.random.key(seed)
        ks = jax.random.split(key, 7)
        T, B, E = (128, 4, EMBED_DIM)
        scale = 1.0 / np.sqrt(E)
        return {'query': jax.random.normal(ks[0], (T, B, E), jnp.float32), 'in_proj_weight': jax.random.normal(ks[1], (3 * E, E), jnp.float32) * scale, 'in_proj_bias': jnp.zeros((3 * E,), jnp.float32), 'rel_k_table': jax.random.uniform(ks[2], (2 * MAX_REL + 1, HEAD_DIM), jnp.float32), 'rel_v_table': jax.random.uniform(ks[3], (2 * MAX_REL + 1, HEAD_DIM), jnp.float32), 'out_w': jax.random.normal(ks[4], (E, E), jnp.float32) * scale, 'out_b': jnp.zeros((E,), jnp.float32)}
    _L1_attn_in = _L1_attn_setup()

    def _L1_ffn_setup():
        import jax, jax.numpy as jnp
        import numpy as np
        S, B, H, I, E = (64, 2, 128, 352, 8)
        key = jax.random.key(seed)
        ks = jax.random.split(key, 5)
        return {'hidden_states': jax.random.normal(ks[0], (S, B, H), dtype=jnp.float32), 'router_w': jax.random.normal(ks[1], (E, H), dtype=jnp.float32) * 0.02, 'gate_w': jax.random.normal(ks[2], (E, I, H), dtype=jnp.float32) * 0.02, 'up_w': jax.random.normal(ks[3], (E, I, H), dtype=jnp.float32) * 0.02, 'down_w': jax.random.normal(ks[4], (E, H, I), dtype=jnp.float32) * 0.02}
    _L1_ffn_in = _L1_ffn_setup()
    _d = {'L0_attn_inputs': _L0_attn_in['inputs'], 'L0_attn_W_q': _L0_attn_in['W_q'], 'L0_attn_b_q': _L0_attn_in['b_q'], 'L0_attn_W_k': _L0_attn_in['W_k'], 'L0_attn_b_k': _L0_attn_in['b_k'], 'L0_attn_W_v': _L0_attn_in['W_v'], 'L0_attn_b_v': _L0_attn_in['b_v'], 'L0_attn_W_o': _L0_attn_in['W_o'], 'L0_attn_b_o': _L0_attn_in['b_o'], 'L0_ffn_wf': _L0_ffn_in['wf'], 'L0_ffn_uf': _L0_ffn_in['uf'], 'L0_ffn_bf': _L0_ffn_in['bf'], 'L0_ffn_wi': _L0_ffn_in['wi'], 'L0_ffn_ui': _L0_ffn_in['ui'], 'L0_ffn_bi': _L0_ffn_in['bi'], 'L0_ffn_wc': _L0_ffn_in['wc'], 'L0_ffn_uc': _L0_ffn_in['uc'], 'L0_ffn_bc': _L0_ffn_in['bc'], 'L0_ffn_wo': _L0_ffn_in['wo'], 'L0_ffn_uo': _L0_ffn_in['uo'], 'L0_ffn_bo': _L0_ffn_in['bo'], 'L0_ffn_in_c': _L0_ffn_in['in_c'], 'L1_attn_in_proj_weight': _L1_attn_in['in_proj_weight'], 'L1_attn_in_proj_bias': _L1_attn_in['in_proj_bias'], 'L1_attn_rel_k_table': _L1_attn_in['rel_k_table'], 'L1_attn_rel_v_table': _L1_attn_in['rel_v_table'], 'L1_attn_out_w': _L1_attn_in['out_w'], 'L1_attn_out_b': _L1_attn_in['out_b'], 'L1_ffn_router_w': _L1_ffn_in['router_w'], 'L1_ffn_gate_w': _L1_ffn_in['gate_w'], 'L1_ffn_up_w': _L1_ffn_in['up_w'], 'L1_ffn_down_w': _L1_ffn_in['down_w']}
    _x0 = _d['L0_attn_inputs']
    _d['L0_attn_inputs'] = jax.random.normal(jax.random.fold_in(jax.random.key(seed), 1), (16, 512, 128), dtype=_x0.dtype)
    del _x0
    return _d

def reference(L0_attn_inputs, L0_attn_W_q, L0_attn_b_q, L0_attn_W_k, L0_attn_b_k, L0_attn_W_v, L0_attn_b_v, L0_attn_W_o, L0_attn_b_o, L0_ffn_wf, L0_ffn_uf, L0_ffn_bf, L0_ffn_wi, L0_ffn_ui, L0_ffn_bi, L0_ffn_wc, L0_ffn_uc, L0_ffn_bc, L0_ffn_wo, L0_ffn_uo, L0_ffn_bo, L0_ffn_in_c, L1_attn_in_proj_weight, L1_attn_in_proj_bias, L1_attn_rel_k_table, L1_attn_rel_v_table, L1_attn_out_w, L1_attn_out_b, L1_ffn_router_w, L1_ffn_gate_w, L1_ffn_up_w, L1_ffn_down_w):

    def _L0_attn_ref(inputs, W_q, b_q, W_k, b_k, W_v, b_v, W_o, b_o):
        import jax, jax.numpy as jnp
        import numpy as np
        import math
        B, S, D, H = (4, 256, 128, 16)
        HD = D // H
        seq_len = inputs.shape[1]
        head_dim = W_q.shape[-1]
        q = jnp.einsum('bsd,hde->bhse', inputs, W_q) + b_q[None, :, None, :]
        k = jnp.einsum('bsd,hde->bhse', inputs, W_k) + b_k[None, :, None, :]
        v = jnp.einsum('bsd,hde->bhse', inputs, W_v) + b_v[None, :, None, :]
        scores = jnp.einsum('bhse,bhte->bhst', q, k) / math.sqrt(head_dim)
        causal = jnp.tril(jnp.ones((seq_len, seq_len), dtype=bool))
        scores = jnp.where(causal[None, None], scores, -jnp.inf)
        attn = jax.nn.softmax(scores, axis=-1)
        wv = jnp.einsum('bhst,bhte->bshe', attn, v).reshape(inputs.shape[0], seq_len, -1)
        return wv @ W_o.T + b_o

    def _L0_ffn_ref(x, wf, uf, bf, wi, ui, bi, wc, uc, bc, wo, uo, bo, in_c):
        import jax, jax.numpy as jnp
        import numpy as np
        from jax import lax
        T, B, I, M, O = (32, 64, 128, 128, 128)

        def _xavier(key, shape):
            fan_out, fan_in = shape
            limit = float(np.sqrt(6.0 / (fan_in + fan_out)))
            return jax.random.uniform(key, shape, jnp.float32, -limit, limit)
        batch = x.shape[1]
        c0 = jnp.broadcast_to(in_c, (batch, in_c.shape[0]))

        def step(c, xt):
            ft = jax.nn.sigmoid(xt @ wf.T + c @ uf.T + bf)
            it = jax.nn.sigmoid(xt @ wi.T + c @ ui.T + bi)
            gt = jnp.tanh(xt @ wc.T + c @ uc.T + bc)
            c = ft * c + it * gt
            return (c, None)
        c_final, _ = lax.scan(step, c0, x)
        h = jnp.tanh(jnp.einsum('tbi,oi->tbo', x, wo) + c_final @ uo.T + bo)
        return h

    def _L1_attn_ref(query, in_proj_weight, in_proj_bias, rel_k_table, rel_v_table, out_w, out_b):
        import jax, jax.numpy as jnp
        import numpy as np
        EMBED_DIM = 128
        NUM_HEADS = 16
        HEAD_DIM = EMBED_DIM // NUM_HEADS
        MAX_REL = 16
        T, B, E = query.shape
        H, d = (NUM_HEADS, HEAD_DIM)
        scaling = d ** (-0.5)
        qkv = jnp.einsum('tbe,fe->tbf', query, in_proj_weight) + in_proj_bias
        q, k, v = jnp.split(qkv, 3, axis=-1)
        q = q * scaling

        def to_heads(x):
            return x.reshape(T, B * H, d).transpose(1, 0, 2)
        q, k, v = (to_heads(q), to_heads(k), to_heads(v))
        pos = jnp.arange(T)
        dist = pos[None, :] - pos[:, None]
        idx = jnp.clip(dist, -MAX_REL, MAX_REL) + MAX_REL
        rel_k = rel_k_table[idx]
        rel_v = rel_v_table[idx]
        scores = jnp.einsum('nqd,nkd->nqk', q, k) + jnp.einsum('nqd,qkd->nqk', q, rel_k)
        probs = jax.nn.softmax(scores, axis=-1)
        attn = jnp.einsum('nqk,nkd->nqd', probs, v) + jnp.einsum('nqk,qkd->nqd', probs, rel_v)
        attn = attn.transpose(1, 0, 2).reshape(T, B, E)
        out = jnp.einsum('tbe,fe->tbf', attn, out_w) + out_b
        return out

    def _L1_ffn_ref(hidden_states, router_w, gate_w, up_w, down_w):
        import jax, jax.numpy as jnp
        import numpy as np
        S, B, H, I, E = (64, 2, 128, 352, 8)
        router_logits = jnp.einsum('sbh,eh->sbe', hidden_states, router_w)
        routing_indices = jnp.argmax(router_logits, axis=-1)
        out = jnp.zeros_like(hidden_states)
        for e in range(E):
            mask = (routing_indices == e)[..., None]
            xe = jnp.where(mask, hidden_states, 0.0)
            g = jnp.einsum('sbh,ih->sbi', xe, gate_w[e])
            u = jnp.einsum('sbh,ih->sbi', xe, up_w[e])
            ye = jnp.einsum('sbi,hi->sbh', jax.nn.silu(g) * u, down_w[e])
            out = out + jnp.where(mask, ye, 0.0)
        return out
    x = L0_attn_inputs
    xn = _layernorm(x, axis=-1)
    x = x + _L0_attn_ref(xn, L0_attn_W_q, L0_attn_b_q, L0_attn_W_k, L0_attn_b_k, L0_attn_W_v, L0_attn_b_v, L0_attn_W_o, L0_attn_b_o) + _L0_ffn_ref(xn, L0_ffn_wf, L0_ffn_uf, L0_ffn_bf, L0_ffn_wi, L0_ffn_ui, L0_ffn_bi, L0_ffn_wc, L0_ffn_uc, L0_ffn_bc, L0_ffn_wo, L0_ffn_uo, L0_ffn_bo, L0_ffn_in_c)
    xn = _layernorm(x, axis=-1)
    x = x + _L1_attn_ref(xn, L1_attn_in_proj_weight, L1_attn_in_proj_bias, L1_attn_rel_k_table, L1_attn_rel_v_table, L1_attn_out_w, L1_attn_out_b) + _L1_ffn_ref(xn, L1_ffn_router_w, L1_ffn_gate_w, L1_ffn_up_w, L1_ffn_down_w)
    return x

_drawn_inputs = setup_inputs


def setup_inputs(seed=0):
    import zlib

    import numpy as np

    out = dict(_drawn_inputs(seed))
    spreads = {'L0_ffn_bf': (0.0, 0.592),
     'L0_ffn_bi': (0.0, 0.594),
     'L0_ffn_bc': (0.0, 0.1),
     'L0_ffn_bo': (0.0, 0.1),
     'L0_ffn_in_c': (0.0, 0.8),
     'L1_attn_in_proj_bias': (0.0, 0.502),
     'L1_attn_out_b': (0.0, 0.533)}
    factors = {'L0_attn_W_q': 4.587,
     'L0_attn_b_q': 8.0,
     'L0_attn_W_k': 4.567,
     'L0_attn_b_k': 64.0,
     'L1_ffn_router_w': 8.0,
     'L1_ffn_gate_w': 7.911,
     'L1_ffn_up_w': 7.859,
     'L1_ffn_down_w': 7.86,
     'L1_attn_rel_k_table': 3.753,
     'L1_attn_rel_v_table': 3.549}
    for name, (base, spread) in spreads.items():
        noise = np.random.default_rng([zlib.crc32(name.encode()), seed]).standard_normal(out[name].shape)
        drawn = base * np.exp(spread * noise) if base else spread * noise
        out[name] = jnp.asarray(drawn.astype(out[name].dtype))
    for name, factor in factors.items():
        out[name] = (out[name] * factor).astype(out[name].dtype)
    return out
```

```python
from contextlib import ExitStack

import numpy as np
import concourse.bass as bass
from concourse import mybir

F32 = mybir.dt.float32
BF16 = mybir.dt.bfloat16
I32 = mybir.dt.int32
U32 = mybir.dt.uint32
ALU = mybir.AluOpType
ACT = mybir.ActivationFunctionType
AX = mybir.AxisListType

P = 128
B = 16
S = 512
D = 128
NST = S // P
NH = 16
HD = D // NH
HG = 4
NG = NH // HG
GW = HG * HD
NREL = 33
MAXREL = 16
NE = 8
FI = 352
FC = [128, 128, 96]
NTILE = B * NST
NBLK = NTILE + NE
EPS = 1e-5
SCALE = float(HD) ** -0.5
NEG = -1.0e30
NWIN = B + HD

UNITS = [[(3, 0)], [(2, 0), (0, 3 * P)], [(1, 0)]]
NU = 2 * HG * len(UNITS)
GU = NU // 2
LAG_T = 3
LAG_V = 5
RING_S, RING_P, RING_T = 3, 4, 3


def wait_apart(eng, signal, value):
    eng.wait_ge(signal, value)
    eng.sem_inc(APART[0], 1)


APART = []


def linker(eng, signal):
    state = {"base": 0, "n": 0}

    def link(ins, apart=False):
        state["n"] += 1
        ins.then_inc(signal, 1)
        (wait_apart if apart else type(eng).wait_ge)(eng, signal, state["base"] + state["n"])

    def at(base):
        state["base"], state["n"] = base, 0

    return link, at, lambda: state["n"]


def layer_norm(nc, link, stats, mv, rstd, var_ready, wait_rstd, src, dst):
    for t in range(4):
        ins = nc.vector.bn_stats(stats[:, t, :], src(t))
    link(ins, apart=True)
    for t in range(4):
        ins = nc.vector.bn_aggr(mv[:, t, :], stats[:, t, :])
    link(ins)
    nc.vector.tensor_scalar(rstd[:, 0, :], mv[:, :, 1], EPS, None, ALU.add).then_inc(var_ready, 1)
    wait_rstd()
    for t in range(4):
        ins = nc.vector.tensor_scalar(dst(t), src(t), mv[:, t, 0:1], rstd[:, 1, t:t + 1], ALU.subtract, ALU.mult)
    return ins


def program(nc, a, out):
    with ExitStack() as ctx:
        def sem(name):
            return ctx.enter_context(nc.semaphore(name))

        def sb(where, name, shape, dt=F32):
            return where.enter_context(nc.sbuf_tensor(name, shape, dt))

        def ps(where, name, shape, dt=F32):
            return where.enter_context(nc.psum_tensor(name, shape, dt))

        APART[:] = [sem("apart")]
        q_parts = nc.dram_tensor("q_parts", [B * NG, 3, GW, S], BF16, kind="Internal").ap()
        k_parts = nc.dram_tensor("k_parts", [B * NG, 3, GW, S], BF16, kind="Internal").ap()
        sorted_x = nc.dram_tensor("sorted_x", [NBLK * P, D], F32, kind="Internal").ap()
        sorted_y = nc.dram_tensor("sorted_y", [NBLK * P, D], F32, kind="Internal").ap()

        ident = sb(ctx, "ident", [P, P])
        X = sb(ctx, "X", [P, B, NST, D])
        HX = sb(ctx, "HX", [P, B, NST, D])
        BIG = sb(ctx, "BIG", [P, 3, B * S])
        C2 = sb(ctx, "C2", [P, S])
        uo_h = sb(ctx, "uo_h", [P, D])
        stats = sb(ctx, "stats", [P, 4, 6])
        mv = sb(ctx, "mv", [P, 4, 2])
        rstd = sb(ctx, "rstd", [P, 3, 4])
        LOG = sb(ctx, "LOG", [P, NTILE, NE])
        pos = sb(ctx, "pos", [P, NTILE], I32)
        eb = sb(ctx, "eb", [1, NBLK], I32)
        attn_space = ExitStack()
        O_all = sb(attn_space, "O_all", [P, B * NG, NST, GW])
        V_all = BIG[:, 0, :].rearrange("p (i k c) -> p i k c", i=B * NG, k=NST)

        carved = [B * S]

        def carve(shape, dt=F32):
            n = int(np.prod(shape[1:])) * (1 if dt == F32 else 2) // (1 if dt == F32 else 4)
            at = carved[0]
            carved[0] += n
            assert carved[0] <= 3 * B * S
            v = BIG[:, :, :].rearrange("p a n -> p (a n)")[:, at:at + n]
            if dt != F32:
                v = v.bitcast(dt)
            names = " ".join(f"d{n}" for n in range(len(shape) - 1))
            return v.rearrange(f"p ({names}) -> p {names}", **{f"d{n}": shape[n + 1] for n in range(len(shape) - 2)})

        pa = ExitStack()
        WN = ("wq", "wk", "wv", "wf", "wi", "wc", "wo", "uf", "ui", "uc", "uo")
        W = {n: carve([P, D]) for n in WN}
        bias_cols = carve([P, 6])
        bias_half = carve([P, 4])
        bv_row, bo_row = carve([P, D]), carve([P, D])
        U2 = carve([P, 3, D])
        XN, XNT = carve([P, 2, 4, D]), carve([P, 2, S])
        QK = carve([P, 2, 2, S])
        RES = carve([P, 2, S])
        PARTS = carve([P, 2, 2, 3, S], BF16)
        TG, CA = carve([P, 3, S]), carve([P, 2, S])
        NZ = 4
        zero = carve([P, NBLK * D // NZ])
        psT = ps(pa, "psT", [P, S])
        psQ = ps(pa, "psQ", [P, 2, S])
        psV, psH = ps(pa, "psV", [P, 4, D]), ps(pa, "psH", [P, 4, D])
        psG = ps(pa, "psG", [P, 3, S])

        weights_in, x_in, zeroed, zero_out, halved = (sem(n) for n in (
            "weights_in", "x_in", "zeroed", "zero_out", "halved"))
        xn_ready, xnT_ps, xnT_ready = sem("xn_ready"), sem("xnT_ps"), sem("xnT_ready")
        q_ps, k_ps, v_ps, h_ps, g_ps = (sem(n) for n in ("q_ps", "k_ps", "v_ps", "h_ps", "g_ps"))
        qk_sb, v_out, h_out, gates_ready, c_ready, parts_ready, parts_stored = (sem(n) for n in (
            "qk_sb", "v_out", "h_out", "gates_ready", "c_ready", "parts_ready", "parts_stored"))
        a_dve, a_pool = sem("a_dve"), sem("a_pool")
        var_ready, rstd_ready = sem("var_ready"), sem("rstd_ready")

        def power(eng, n):
            eng.wait_ge(var_ready, n + 1)
            nc.gpsimd.tensor_tensor(rstd[:, 1, :], rstd[:, 0, :], rstd[:, 2, :], ALU.pow).then_inc(rstd_ready, 1)
        NWA = len(WN) + 6 + 3

        def two_steps(eng, body):
            with eng.Fori(0, B // 2 - 1) as i:
                body(i * 2, 0, False)
                body(i * 2 + 1, 1, False)
            body(B - 2, 0, False)
            body(B - 1, 1, True)

        def b_tiles(t, b):
            return t[:, bass.ds(b, 1)].rearrange("p a n d -> p (a n) d")

        with nc.Block() as block:
            @block.sync
            def _(sp):
                for n in WN:
                    sp.dma_start(W[n], a[n]).then_inc(weights_in, 16)
                for c, n in enumerate(("bq", "bk", "bf", "bi", "bc", "in_c")):
                    sp.dma_start(bias_cols[:, c:c + 1], a[n]).then_inc(weights_in, 16)
                sp.dma_start(bv_row, a["bv"].to_broadcast([P, D])).then_inc(weights_in, 16)
                sp.dma_start(bo_row, a["ffn_bo"].to_broadcast([P, D])).then_inc(weights_in, 16)
                sp.dma_start(ident[:, :], a["ident"]).then_inc(weights_in, 16)

                def load_x(b):
                    sp.dma_start(b_tiles(X, b), a["x"][bass.ds(b, 1)].rearrange("a (n p) d -> p (a n) d", p=P))\
                      .then_inc(x_in, 16)
                    sp.wait_ge(x_in, b * 16 + 16)
                load_x(0)

                def body(b, s, last):
                    if not last:
                        load_x(b + 1)
                    for n, parts in enumerate((q_parts, k_parts)):
                        sp.wait_ge(parts_ready, b * 2 + (n + 5))
                        for g in range(NG):
                            sp.dma_start(parts[bass.ds(b * NG + g, 1)].rearrange("g t r s -> (g r) t s"),
                                         PARTS[g * GW:(g + 1) * GW, s, n]).then_inc(parts_stored, 16)
                    wait_apart(sp, parts_stored, b * 128 + (128 + 256))
                two_steps(sp, body)

            @block.scalar
            def _(act):
                act.wait_ge(zeroed, 1)
                zx = sorted_x.rearrange("(z p r) d -> z p (r d)", z=NZ, p=P)
                for z in range(NZ):
                    act.dma_start(zx[z], zero).then_inc(zero_out, 16)
                act.sem_inc(qk_sb, 2)
                act.sem_inc(gates_ready, 1)
                act.wait_ge(weights_in, 16 * NWA)
                nc.scalar.mul(bias_half[:, 0:1], bias_cols[:, 0:1], SCALE)
                nc.scalar.mul(bias_half[:, 1:3], bias_cols[:, 2:4], 0.5)
                for n, w in enumerate(("uf", "ui", "uc")):
                    nc.scalar.mul(U2[:, n, :], W[w], 0.5)
                nc.scalar.mul(uo_h[:, :], W["uo"], 0.5).then_inc(halved, 1)
                act.wait_ge(halved, 1)

                def body(b, s, last):
                    act.wait_ge(xnT_ps, b + 1)
                    nc.scalar.copy(XNT[:, s, :], psT[:, :]).then_inc(xnT_ready, 1)
                    act.wait_ge(q_ps, b + 1)
                    act.wait_ge(parts_ready, b * 2 + 2)
                    nc.scalar.activation(QK[:, s, 0, :], psQ[:, 0, :], ACT.Identity,
                                         bias=bias_half[:, 0:1], scale=SCALE).then_inc(qk_sb, 1)
                    act.wait_ge(k_ps, b + 1)
                    nc.scalar.activation(QK[:, s, 1, :], psQ[:, 1, :], ACT.Identity,
                                         bias=bias_cols[:, 1:2]).then_inc(qk_sb, 1)
                    act.wait_ge(g_ps, b + 1)
                    act.wait_ge(c_ready, b + 1)
                    nc.scalar.activation(TG[:, 0, :], psG[:, 0, :], ACT.Tanh, bias=bias_half[:, 1:2], scale=0.5)
                    nc.scalar.activation(TG[:, 1, :], psG[:, 1, :], ACT.Tanh, bias=bias_half[:, 2:3], scale=0.5)
                    nc.scalar.activation(TG[:, 2, :], psG[:, 2, :], ACT.Tanh,
                                         bias=bias_cols[:, 4:5]).then_inc(gates_ready, 1)
                two_steps(act, body)
                act.wait_ge(zero_out, 16 * NZ)

            @block.vector
            def _(dve):
                link, at, count = linker(dve, a_dve)
                nc.vector.memset(zero, 0.0).then_inc(zeroed, 1)
                dve.sem_inc(v_out, 1)
                dve.sem_inc(h_out, 1)
                dve.wait_ge(weights_in, 16 * NWA)
                link(nc.vector.memset(C2[:, :], 0.0))
                nc.vector.tensor_scalar(C2[:, :], C2[:, :], bias_cols[:, 5:6], 2.0, ALU.add, ALU.mult)\
                    .then_inc(c_ready, 1)

                def norm(b, s):
                    dve.wait_ge(x_in, b * 16 + 16)
                    layer_norm(nc, link, stats, mv, rstd, var_ready, lambda: dve.wait_ge(rstd_ready, b + 1),
                               lambda t: b_tiles(X, b)[:, t, :], lambda t: XN[:, s, t, :]).then_inc(xn_ready, 1)
                norm(0, 0)
                first, per = count(), 3

                def body(b, s, last):
                    at(b * per + first)
                    dve.wait_ge(v_ps, b + 1)
                    for t in range(NST):
                        ins = nc.vector.tensor_tensor(V_all[:, bass.ds(b * NG, NG), t, :],
                                                      psV[:, t, :].rearrange("p (g c) -> p g c", g=NG),
                                                      bv_row.rearrange("p (g c) -> p g c", g=NG), ALU.add)
                    ins.then_inc(v_out, 1)
                    dve.wait_ge(h_ps, b + 1)
                    nc.vector.tensor_tensor(b_tiles(HX, b), psH[:, :, :],
                                            bo_row.unsqueeze(1).to_broadcast([P, NST, D]), ALU.add).then_inc(h_out, 1)
                    if not last:
                        norm(b + 1, 1 - s)
                    dve.wait_ge(gates_ready, b + 2)
                    nc.vector.scalar_tensor_tensor(CA[:, 0, :], TG[:, 0, :], 1.0, C2[:, :], ALU.add, ALU.mult)
                    link(nc.vector.scalar_tensor_tensor(CA[:, 1, :], TG[:, 1, :], 1.0, TG[:, 2, :], ALU.add, ALU.mult))
                    nc.vector.scalar_tensor_tensor(C2[:, :], CA[:, 0, :], 0.5, CA[:, 1, :], ALU.mult, ALU.add)\
                        .then_inc(c_ready, 1)
                    dve.wait_ge(c_ready, b + 2)
                    assert last or count() == per
                two_steps(dve, body)

            @block.gpsimd
            def _(pool):
                pool.sem_inc(parts_ready, 4)
                pool.sem_inc(parts_stored, 256)

                nc.gpsimd.memset(rstd[:, 2, :], -0.5).then_inc(a_pool, 1)
                pool.wait_ge(a_pool, 1)
                power(pool, 0)

                def body(b, s, last):
                    pool.wait_ge(parts_stored, b * 128 + 128)
                    for n in range(2):
                        c = b * 6 + (n * 3 + 1)
                        wait_apart(pool, qk_sb, b * 2 + (n + 3))
                        src, part = QK[:, s, n, :], PARTS[:, s, n]
                        nc.gpsimd.tensor_copy(part[:, 0, :], src).then_inc(a_pool, 1)
                        pool.wait_ge(a_pool, c + 1)
                        nc.gpsimd.tensor_tensor(RES[:, n, :], src, part[:, 0, :], ALU.subtract).then_inc(a_pool, 1)
                        wait_apart(pool, a_pool, c + 2)
                        nc.gpsimd.tensor_copy(part[:, 1, :], RES[:, n, :]).then_inc(a_pool, 1)
                        pool.wait_ge(a_pool, c + 3)
                        nc.gpsimd.tensor_tensor(part[:, 2, :], RES[:, n, :], part[:, 1, :], ALU.subtract)\
                            .then_inc(parts_ready, 1)
                        if n == 0 and not last:
                            power(pool, b + 1)
                two_steps(pool, body)

            @block.tensor
            def _(pe):
                pe.wait_ge(weights_in, 16 * NWA)
                pe.wait_ge(halved, 1)

                def body(b, s, last):
                    pe.wait_ge(xn_ready, b + 1)
                    for t in range(4):
                        ins = nc.tensor.transpose(psT[:, t * P:(t + 1) * P], XN[:, s, t, :], ident[:, :])
                    ins.then_inc(xnT_ps, 1)
                    pe.wait_ge(xnT_ready, b + 1)
                    xT = XNT[:, s, :]
                    pe.wait_ge(qk_sb, b * 2 + 2)
                    nc.tensor.matmul(psQ[:, 0, :], W["wq"], xT, start=True, stop=True).then_inc(q_ps, 1)
                    nc.tensor.matmul(psQ[:, 1, :], W["wk"], xT, start=True, stop=True).then_inc(k_ps, 1)
                    pe.wait_ge(v_out, b + 1)
                    for t in range(4):
                        ins = nc.tensor.matmul(psV[:, t, :], xT[:, t * P:(t + 1) * P], W["wv"], start=True, stop=True)
                    ins.then_inc(v_ps, 1)
                    pe.wait_ge(h_out, b + 1)
                    for t in range(4):
                        ins = nc.tensor.matmul(psH[:, t, :], xT[:, t * P:(t + 1) * P], W["wo"], start=True, stop=True)
                    ins.then_inc(h_ps, 1)
                    pe.wait_ge(gates_ready, b + 1)
                    for n, w in enumerate(("wf", "wi", "wc")):
                        nc.tensor.matmul(psG[:, n, :], W[w], xT, start=True, stop=False)
                    pe.wait_ge(c_ready, b + 1)
                    for n in range(3):
                        ins = nc.tensor.matmul(psG[:, n, :], U2[:, n, :], C2[:, :], start=False, stop=True)
                    ins.then_inc(g_ps, 1)
                two_steps(pe, body)
        pa.close()

        pb = ExitStack()
        carved[0] = B * S
        STEPS = B * NG // 2
        maskb, identb = carve([P, P], BF16), carve([P, P], BF16)
        maskf = carve([P, P])
        QS, KS = carve([P, 2, HG, S], BF16), carve([P, 2, HG, S], BF16)
        VG = carve([P, 2, NST, GW])
        NM = carve([P, 8, 2])
        RS = carve([P, 2, NST, HG])
        RI = carve([P, 2, NST, HG])
        PR = carve([P, RING_P, S])
        PT = carve([P, RING_P, S])
        psS = ps(pb, "psS", [P, RING_S, S])
        psP = ps(pb, "psP", [P, RING_T, S])
        psO_banks = ps(pb, "psO", [P, 2, S])
        psO = psO_banks[:, :, 0:NST * GW].rearrange("p g (q c) -> p g q c", q=NST)

        mask_in, b_const, stack_clear = sem("mask_in"), sem("b_const"), sem("stack_clear")
        stack_in = [sem("stack_in0"), sem("stack_in1")]
        stack_free = [sem("stack_free0"), sem("stack_free1")]
        s_done, max_done, exp_done, t_done = sem("s_done"), sem("max_done"), sem("exp_done"), sem("t_done")
        evac_act, evac_dve, pv_done = sem("evac_act"), sem("evac_dve"), sem("pv_done")
        vg_ready, o_done, b_dve = sem("vg_ready"), sem("o_done"), sem("b_dve")

        def by_act(u):
            return u % 3 == 2 or u % 12 == 4
        NA = sum(by_act(u) for u in range(NU))
        ND = NU - NA

        def evacuated(u):
            n = sum(by_act(v) == by_act(u) for v in range(u % NU + 1))
            return (evac_act, NA, n) if by_act(u) else (evac_dve, ND, n)

        def skewed(eng, body):
            for u in range(NU):
                body(0, u, lambda lag, u=u: u - lag >= 0)
            with eng.Fori(1, STEPS) as i:
                for u in range(NU):
                    body(i, u, lambda lag: True)
            for u in range(LAG_V):
                body(STEPS, u, lambda lag, u=u: u - lag < 0 and lag > 0)

        def blocks(unit):
            return [(qb, c0, [(kb, c0 + kb * P) for kb in range(qb + 1)]) for qb, c0 in unit]

        with nc.Block() as block:
            @block.sync
            def _(sp):
                sp.dma_start(maskf, a["mask"]).then_inc(mask_in, 16)
                sp.wait_ge(stack_clear, 1)
                rows = [(QS, q_parts, [(0, 0, 3), (3 * HD, 1, 2), (5 * HD, 2, 1)]),
                        (KS, k_parts, [(0, None, 3), (3 * HD, None, 2), (5 * HD, None, 1)])]
                with sp.Fori(0, STEPS) as i:
                    for g in range(2):
                        sp.wait_ge(stack_free[g], i + 1)
                        for stack, parts, dmas in rows:
                            src = parts[bass.ds(i * 2 + g, 1)].rearrange("a t (d h) s -> (a t) d (h s)", d=HD)
                            for r0, part, n in dmas:
                                for m in range(n):
                                    t = part if part is not None else m
                                    sp.dma_start(stack[r0 + m * HD:r0 + (m + 1) * HD, g].rearrange("p h s -> p (h s)"),
                                                 src[t]).then_inc(stack_in[g], 16)

            @block.gpsimd
            def _(pool):
                nc.gpsimd.memset(QS, 0.0)
                nc.gpsimd.memset(KS, 0.0).then_inc(stack_clear, 1)
                pool.wait_ge(mask_in, 16)
                nc.gpsimd.tensor_copy(maskb, maskf)
                nc.gpsimd.tensor_copy(identb, ident[:, :]).then_inc(b_const, 1)
                pool.sem_inc(pv_done, 2 * GU)

                with pool.Fori(0, STEPS) as i:
                    for g in range(2):
                        wait_apart(pool, pv_done, i * NU + (g + 1) * GU)
                        nc.gpsimd.tensor_copy(VG[:, g], V_all[:, bass.ds(i * 2 + g, 1)].rearrange("p a k c -> p (a k) c"))\
                            .then_inc(vg_ready, 1)

            @block.tensor
            def _(pe):
                pe.wait_ge(b_const, 1)
                for g in range(2):
                    pe.sem_inc(stack_free[g], 1)
                last = {}

                def body(i, u, has):
                    if has(0):
                        g, h = u // GU, u % GU // 3
                        if u % GU == 0:
                            pe.wait_ge(stack_in[g], i * 192 + 192)
                        pe.wait_ge(exp_done, i * NU + (u + 1))
                        bank = psS[:, u % RING_S, :]
                        for qb, c0, keys in blocks(UNITS[u % 3]):
                            nc.tensor.matmul(bank[:, c0:c0 + (qb + 1) * P], QS[:, g, h, qb * P:(qb + 1) * P],
                                             KS[:, g, h, 0:(qb + 1) * P], start=True, stop=False)
                            ins = nc.tensor.matmul(bank[:, c0 + qb * P:c0 + (qb + 1) * P], identb, maskb,
                                                   start=False, stop=True)
                        ins.then_inc(s_done, 1)
                        if u % GU == GU - 1:
                            pe.wait_ge(s_done, i * NU + (u + 1))
                            pe.sem_inc(stack_free[g], 1)
                    if has(LAG_T):
                        v = u - LAG_T
                        pe.wait_ge(exp_done, i * NU + (v + RING_S + 1))
                        w = v - RING_T
                        if has(LAG_T + RING_T):
                            sig, per, n = evacuated(w % NU)
                            pe.wait_ge(sig, (i if w >= 0 else i - 1) * per + n)
                        for qb, c0, keys in blocks(UNITS[v % 3]):
                            for kb, c in keys:
                                ins = nc.tensor.transpose(psP[:, v % RING_T, c:c + P], PR[:, v % RING_P, c:c + P],
                                                          ident[:, :])
                        ins.then_inc(t_done, 1)
                    if has(LAG_V):
                        v = u - LAG_V
                        vu = v % NU
                        g, h = vu // GU, vu % GU // 3
                        sig, per, n = evacuated(vu)
                        pe.wait_ge(sig, (i if v >= 0 else i - 1) * per + n)
                        if vu % GU == 0:
                            pe.wait_ge(vg_ready, (i if v >= 0 else i - 1) * 2 + (g + 1))
                            pe.wait_ge(o_done, (i if v >= 0 else i - 1) * 2 + (g + 1))
                        for qb, c0, keys in blocks(UNITS[vu % 3]):
                            for kb, c in keys:
                                ins = nc.tensor.matmul(psO[:, g, qb, h * HD:(h + 1) * HD], PT[:, vu % RING_P, c:c + P],
                                                       VG[:, g, kb, h * HD:(h + 1) * HD], start=(kb == 0), stop=(kb == qb))
                        ins.then_inc(pv_done, 1)
                skewed(pe, body)

            def width(v):
                return {0: S, 1: S, 2: 2 * P}[v % 3]

            @block.scalar
            def _(act):
                act.sem_inc(exp_done, RING_S)

                def body(i, u, has):
                    if has(0):
                        g, h = u // GU, u % GU // 3
                        act.wait_ge(max_done, i * NU + (u + 1))
                        if has(RING_P):
                            act.wait_ge(t_done, i * NU + (u - RING_P + 1))
                        if u % GU == 0 and has(GU * 2):
                            act.wait_ge(o_done, i * 2 + (g + 1))
                        for n, (qb, c0, keys) in enumerate(blocks(UNITS[u % 3])):
                            w = (qb + 1) * P
                            ins = nc.scalar.activation(PR[:, u % RING_P, c0:c0 + w], psS[:, u % RING_S, c0:c0 + w],
                                                       ACT.Exp, bias=NM[:, u % 8, n:n + 1],
                                                       accum_out=RS[:, g, qb, h:h + 1])
                        ins.then_inc(exp_done, 1)
                    if has(LAG_T) and by_act((u - LAG_T) % NU):
                        v = u - LAG_T
                        act.wait_ge(t_done, i * NU + (v + 1))
                        act.wait_ge(pv_done, i * NU + (v + 1 - RING_P + 2 * GU))
                        nc.scalar.copy(PT[:, v % RING_P, 0:width(v)], psP[:, v % RING_T, 0:width(v)]).then_inc(evac_act, 1)
                skewed(act, body)

            @block.vector
            def _(dve):
                dve.sem_inc(o_done, 2)

                def body(i, u, has):
                    if has(0):
                        dve.wait_ge(s_done, i * NU + (u + 1))
                        for n, (qb, c0, keys) in enumerate(blocks(UNITS[u % 3])):
                            w = (qb + 1) * P
                            ins = nc.vector.tensor_reduce(NM[:, u % 8, n:n + 1], psS[:, u % RING_S, c0:c0 + w],
                                                          AX.X, ALU.max, negate=True)
                        ins.then_inc(max_done, 1)
                    if has(LAG_T) and not by_act((u - LAG_T) % NU):
                        v = u - LAG_T
                        dve.wait_ge(t_done, i * NU + (v + 1))
                        dve.wait_ge(pv_done, i * NU + (v + 1 - RING_P + 2 * GU))
                        nc.vector.tensor_copy(PT[:, v % RING_P, 0:width(v)], psP[:, v % RING_T, 0:width(v)])\
                            .then_inc(evac_dve, 1)
                    if has(LAG_V) and (u - LAG_V) % GU == GU - 1:
                        v = u - LAG_V
                        g = v % NU // GU
                        j = i if v >= 0 else i - 1
                        dve.wait_ge(pv_done, i * NU + (v + 1 + 2 * GU))
                        nc.vector.reciprocal(RI[:, g], RS[:, g]).then_inc(b_dve, 1)
                        dve.wait_ge(b_dve, j * 2 + (g + 1))
                        nc.vector.tensor_tensor(
                            O_all[:, bass.ds(j * 2 + g, 1)].rearrange("p a q (h e) -> p (a q h) e", e=HD),
                            psO[:, g].rearrange("p q (h e) -> p (q h) e", e=HD),
                            RI[:, g].rearrange("p q h -> p (q h)").unsqueeze(2).to_broadcast([P, NST * HG, HD]),
                            ALU.mult).then_inc(o_done, 1)
                skewed(dve, body)
        pb.close()

        pc = ExitStack()
        q1T, k1T, v1T = (BIG[:, n, :].rearrange("p (t s) -> p t s", t=B) for n in range(3))
        WC = sb(pc, "WC", [P, 4, D])
        rw = sb(pc, "rw", [P, NE])
        bc1 = sb(pc, "bc1", [P, 4])
        ab_row = sb(pc, "ab_row", [P, D])
        CU = C2[:, :].rearrange("p (n d) -> p n d", n=NST)
        OST, HS = sb(pc, "OST", [P, 4, D]), sb(pc, "HS", [P, 4, D])
        c_in, cu_ps, cu_sb = sem("c_in"), sem("cu_ps"), sem("cu_sb")
        ost_ready, oT_ps, oT_sb, y_ps, x1_ready, hs_pre, hs_ready, xs_ready, xT_ps, xT_sb = (sem(n) for n in (
            "ost_ready", "oT_ps", "oT_sb", "y_ps", "x1_ready", "hs_pre", "hs_ready", "xs_ready", "xT_ps", "xT_sb"))
        q1_ps, r_ps, q1_sb, v1_sb, log_sb, xs_copied, c_dve, c_pool, c_act = (sem(n) for n in (
            "q1_ps", "r_ps", "q1_sb", "v1_sb", "log_sb", "xs_copied", "c_dve", "c_pool", "c_act"))
        psA, psB = ps(pc, "psA", [P, 4, D]), ps(pc, "psB", [P, 4, D])
        psA2 = ps(pc, "psA2", [P, 4, D])
        psQ1 = ps(pc, "psQ1", [P, 3, S])
        psR = ps(pc, "psR", [P, 4, NE])
        psCU = ps(pc, "psCU", [P, NST, D])
        OT = sb(pc, "OT", [P, S])
        XS, XT = HS, OT

        with nc.Block() as block:
            @block.sync
            def _(sp):
                sp.dma_start(WC[:, 0, :], a["attn_wo"]).then_inc(c_in, 16)
                sp.dma_start(WC[:, 1:4, :], a["in_proj"].rearrange("p (n d) -> p n d", n=3)).then_inc(c_in, 16)
                sp.dma_start(rw[:, :], a["router"]).then_inc(c_in, 16)
                sp.dma_start(bc1[:, 0:3], a["in_bias"]).then_inc(c_in, 16)
                sp.dma_start(ab_row[:, :], a["attn_bo"].to_broadcast([P, D])).then_inc(c_in, 16)

            @block.gpsimd
            def _(pool):
                pool.wait_ge(c_in, 80)
                with pool.Fori(0, B) as b:
                    wait_apart(pool, oT_ps, b + 1)
                    for g in range(NG):
                        ins = nc.gpsimd.tensor_copy(OST[:, :, g * GW:(g + 1) * GW],
                                                    O_all[:, bass.ds(b * NG + g, 1)].rearrange("p a q c -> p (a q) c"))
                    ins.then_inc(ost_ready, 1)
                    nc.gpsimd.tensor_tensor(b_tiles(X, b), b_tiles(X, b),
                                            ab_row[:, :].unsqueeze(1).to_broadcast([P, NST, D]), ALU.add).then_inc(c_pool, 1)
                    power(pool, b + B)
                    wait_apart(pool, xs_ready, b + 1)
                    nc.gpsimd.tensor_copy(b_tiles(HX, b), XS[:, :, :]).then_inc(xs_copied, 1)

            @block.tensor
            def _(pe):
                pe.wait_ge(c_in, 80)
                for t in range(NST):
                    ins = nc.tensor.matmul(psCU[:, t, :], C2[:, t * P:(t + 1) * P], uo_h[:, :], start=True, stop=True)
                ins.then_inc(cu_ps, 1)
                pe.sem_inc(oT_ps, 1)
                with pe.Fori(0, B) as b:
                    pe.wait_ge(ost_ready, b + 1)
                    for t in range(4):
                        ins = nc.tensor.transpose(psA[:, t, :], OST[:, t, :], ident[:, :])
                    ins.then_inc(oT_ps, 1)
                    pe.wait_ge(oT_sb, b + 1)
                    pe.wait_ge(x1_ready, b + 1)
                    for t in range(4):
                        ins = nc.tensor.matmul(psB[:, t, :], OT[:, t * P:(t + 1) * P], WC[:, 0, :], start=True, stop=True)
                    ins.then_inc(y_ps, 1)
                    pe.wait_ge(xs_ready, b + 1)
                    for t in range(4):
                        ins = nc.tensor.transpose(psA2[:, t, :], XS[:, t, :], ident[:, :])
                    ins.then_inc(xT_ps, 1)
                    pe.wait_ge(xT_sb, b + 1)
                    pe.wait_ge(log_sb, b + 1)
                    for t in range(4):
                        ins = nc.tensor.matmul(psR[:, t, :], XT[:, t * P:(t + 1) * P], rw[:, :], start=True, stop=True)
                    ins.then_inc(r_ps, 1)
                    pe.wait_ge(q1_sb, b * 2 + 2)
                    pe.wait_ge(v1_sb, b + 1)
                    for n in range(3):
                        nc.tensor.matmul(psQ1[:, n, :], WC[:, 1 + n, :], XT[:, :], start=True, stop=True).then_inc(q1_ps, 1)

            @block.scalar
            def _(act):
                act.sem_inc(q1_sb, 2)
                act.wait_ge(c_in, 80)
                nc.scalar.mul(bc1[:, 3:4], bc1[:, 0:1], SCALE).then_inc(c_act, 1)
                act.wait_ge(c_act, 1)
                with act.Fori(0, B) as b:
                    act.wait_ge(oT_ps, b + 2)
                    act.wait_ge(q1_ps, b * 3 + 3)
                    nc.scalar.copy(OT[:, :], psA[:, :, :].rearrange("p t d -> p (t d)")).then_inc(oT_sb, 1)
                    act.wait_ge(hs_pre, b + 1)
                    nc.scalar.activation(HS[:, :, :], HS[:, :, :], ACT.Tanh).then_inc(hs_ready, 1)
                    act.wait_ge(xT_ps, b + 1)
                    nc.scalar.copy(XT[:, :], psA2[:, :, :].rearrange("p t d -> p (t d)")).then_inc(xT_sb, 1)
                    act.wait_ge(q1_ps, b * 3 + 4)
                    nc.scalar.activation(q1T[:, bass.ds(b, 1), :].rearrange("p a s -> p (a s)"), psQ1[:, 0, :],
                                         ACT.Identity, bias=bc1[:, 3:4], scale=SCALE).then_inc(q1_sb, 1)
                    act.wait_ge(q1_ps, b * 3 + 5)
                    nc.scalar.activation(k1T[:, bass.ds(b, 1), :].rearrange("p a s -> p (a s)"), psQ1[:, 1, :],
                                         ACT.Identity, bias=bc1[:, 1:2]).then_inc(q1_sb, 1)

            @block.vector
            def _(dve):
                link, at, count = linker(dve, c_dve)
                dve.sem_inc(x1_ready, 1)
                dve.sem_inc(log_sb, 1)
                dve.sem_inc(v1_sb, 1)
                dve.sem_inc(q1_ps, 3)
                dve.wait_ge(c_in, 80)
                dve.wait_ge(cu_ps, 1)
                link(nc.vector.tensor_copy(CU[:, :, :], psCU[:, :, :]))
                per = 4
                with dve.Fori(0, B) as b:
                    at(b * per + 1)
                    nc.vector.tensor_tensor(HS[:, :, :], b_tiles(HX, b), CU[:, :, :], ALU.add).then_inc(hs_pre, 1)
                    dve.wait_ge(c_pool, b + 1)
                    dve.wait_ge(y_ps, b + 1)
                    link(nc.vector.tensor_tensor(b_tiles(X, b), psB[:, :, :], b_tiles(X, b), ALU.add))
                    dve.wait_ge(hs_ready, b + 1)
                    link(nc.vector.tensor_tensor(b_tiles(X, b), b_tiles(X, b), HS[:, :, :], ALU.add))
                    dve.sem_inc(x1_ready, 1)
                    layer_norm(nc, link, stats, mv, rstd, var_ready, lambda: dve.wait_ge(rstd_ready, b + (B + 1)),
                               lambda t: b_tiles(X, b)[:, t, :], lambda t: XS[:, t, :]).then_inc(xs_ready, 1)
                    dve.wait_ge(r_ps, b + 1)
                    nc.vector.tensor_copy(LOG[:, bass.ds(b * NST, NST), :], psR[:, :, :]).then_inc(log_sb, 1)
                    dve.wait_ge(q1_ps, b * 3 + 6)
                    nc.vector.tensor_scalar(v1T[:, bass.ds(b, 1), :].rearrange("p a s -> p (a s)"), psQ1[:, 2, :],
                                            bc1[:, 2:3], None, ALU.add).then_inc(v1_sb, 1)
                    dve.wait_ge(xs_copied, b + 1)
                    assert count() == per
        pc.close()
        attn_space.close()

        pr = ExitStack()

        def rsb(shape, dt=F32):
            rsb.n += 1
            return sb(pr, f"r{rsb.n}", shape, dt)[:]
        rsb.n = 0
        OH, ET = rsb([P, NTILE, NE]), rsb([P, NTILE, NE])
        TOT, INC = rsb([P, NE, NTILE]), rsb([P, NE, NTILE])
        ones64, iota64 = rsb([P, NTILE]), rsb([P, NTILE])
        mxl, idx, posf = rsb([P, NTILE]), rsb([P, NTILE]), rsb([P, NTILE])
        iota8 = rsb([P, NE])
        nblk, incb, baseb = rsb([P, NE]), rsb([P, NE]), rsb([P, NE])
        onesm, before = rsb([P, P]), rsb([P, P])
        iotab, ebf, ebc = rsb([P, NBLK]), rsb([P, NBLK]), rsb([P, NBLK, NE])
        psRT = ps(pr, "psRT", [P, 2, NTILE * NE])
        psRank, psTot = (psRT[:, n, :].rearrange("p (j e) -> p j e", e=NE) for n in range(2))
        e_const, e_oh, e_rank, pos_ready, scattered, e_dve = (sem(n) for n in (
            "e_const", "e_oh", "e_rank", "pos_ready", "scattered", "e_dve"))

        with nc.Block() as block:
            @block.sync
            def _(sp):
                sp.dma_start(onesm, a["ones"]).then_inc(e_const, 16)
                sp.dma_start(before, a["before"]).then_inc(e_const, 16)
                sp.dma_start(iota8, a["iota8"].to_broadcast([P, NE])).then_inc(e_const, 16)
                sp.dma_start(iota64, a["iota64"].to_broadcast([P, NTILE])).then_inc(e_const, 16)
                sp.dma_start(iotab, a["iotab"].to_broadcast([P, NBLK])).then_inc(e_const, 16)

            @block.vector
            def _(dve):
                link, at, count = linker(dve, e_dve)
                link(nc.vector.memset(ones64, 1.0))
                dve.wait_ge(e_const, 80)
                link(nc.vector.tensor_reduce(mxl, LOG[:, :, :], AX.X, ALU.max))
                link(nc.vector.tensor_tensor(ET, LOG[:, :, :], mxl.unsqueeze(2).to_broadcast([P, NTILE, NE]), ALU.is_equal))
                io = iota8.unsqueeze(1).to_broadcast([P, NTILE, NE])
                link(nc.vector.tensor_tensor(ET, ET, io, ALU.mult))
                link(nc.vector.tensor_reduce(idx, ET, AX.X, ALU.min))
                nc.vector.tensor_tensor(OH, idx.unsqueeze(2).to_broadcast([P, NTILE, NE]), io, ALU.is_equal).then_inc(e_oh, 1)
                dve.wait_ge(e_rank, 1)
                link(nc.vector.tensor_copy(TOT, psTot.rearrange("p j e -> p e j")))
                for e in range(NE):
                    ins = nc.vector.tensor_tensor_scan(INC[:, e, :], ones64, TOT[:, e, :], 0.0, ALU.mult, ALU.add)
                link(ins)
                for e in range(NE):
                    ins = nc.vector.tensor_scalar(ET.rearrange("p j e -> p (j e)")[:, e * NTILE:(e + 1) * NTILE], iota64,
                                                  INC[:, e, NTILE - 1:NTILE], None, ALU.is_lt)
                link(ins)
                link(nc.vector.tensor_reduce(nblk, ET.rearrange("p j e -> p (j e)").rearrange("p (e n) -> p e n", e=NE),
                                             AX.X, ALU.add))
                link(nc.vector.tensor_tensor_scan(incb, ones64[:, 0:NE], nblk, 0.0, ALU.mult, ALU.add))
                link(nc.vector.tensor_tensor(baseb, incb, nblk, ALU.subtract))
                link(nc.vector.tensor_scalar(baseb, baseb, float(P), None, ALU.mult))
                link(nc.vector.tensor_tensor(INC, INC, TOT, ALU.subtract))
                link(nc.vector.tensor_tensor(INC, INC, baseb.unsqueeze(2).to_broadcast([P, NE, NTILE]), ALU.add))
                link(nc.vector.tensor_tensor(ET, psRank, INC.rearrange("p e j -> p j e"), ALU.add))
                link(nc.vector.tensor_tensor(ET, ET, OH, ALU.mult))
                link(nc.vector.tensor_reduce(posf, ET, AX.X, ALU.add))
                link(nc.vector.tensor_copy(pos[:, :], posf))
                link(nc.vector.tensor_tensor(ebc, incb.unsqueeze(1).to_broadcast([P, NBLK, NE]),
                                             iotab.unsqueeze(2).to_broadcast([P, NBLK, NE]), ALU.is_le))
                link(nc.vector.tensor_reduce(ebf, ebc, AX.X, ALU.add))
                link(nc.vector.tensor_scalar(ebf, ebf, float(NE - 1), None, ALU.min))
                nc.vector.tensor_copy(eb[0:1, :], ebf[0:1, :]).then_inc(pos_ready, 1)

            @block.tensor
            def _(pe):
                pe.wait_ge(e_const, 80)
                pe.wait_ge(e_oh, 1)
                oh = OH.rearrange("p j e -> p (j e)")
                nc.tensor.matmul(psRT[:, 0, :], before, oh, start=True, stop=True)
                nc.tensor.matmul(psRT[:, 1, :], onesm, oh, start=True, stop=True).then_inc(e_rank, 1)

            @block.gpsimd
            def _(pool):
                pool.wait_ge(pos_ready, 1)
                for b in range(B):
                    for st in range(NST):
                        j = b * NST + st
                        pool.indirect_dma_start(sorted_x, bass.IndirectOffsetOnAxis(pos[:, j:j + 1], 0),
                                                HX[:, b, st, :], None).then_inc(scattered, 16)
                pool.wait_ge(scattered, 16 * NTILE)
        pr.close()

        pd = ExitStack()
        relk = sb(pd, "relk", [P, NREL, NH])
        relv = sb(pd, "relv", [P, NREL, NH])
        relrow = sb(pd, "relrow", [P, 2, NREL])
        sel = sb(pd, "sel", [P, NH])
        wout = sb(pd, "wout", [P, D])
        ones_row = sb(pd, "ones_row", [1, P])
        bout_row = sb(pd, "bout_row", [1, D])
        RW = sb(pd, "RW", [P, NWIN * D])
        QD = sb(pd, "QD", [P, 4, P])
        hx = HX[:, :, :, :].rearrange("p a n d -> p (a n) d")
        PROD = hx[:, 0:2 * B, :].rearrange("p (a t) s -> p a t s", a=2)
        PV = hx[:, 2 * B:3 * B, :]
        PD = hx[:, 3 * B:4 * B, :].rearrange("p (a t) x -> p a t x", a=2)
        EP = sb(pd, "EP", [P, 2, 2, B, NH])
        MX = sb(pd, "MX", [P, 2, 2, 2, NH])
        OD = sb(pd, "OD", [P, 2, P])
        PTS = sb(pd, "PTS", [P, 2, 2, 2, P])
        psS1 = ps(pd, "psS1", [P, 2, 2, B * NH])
        psX = ps(pd, "psX", [P, 2, 2, 4, P])
        psT1 = ps(pd, "psT1", [P, 2, 2, P])
        psO1 = ps(pd, "psO1", [P, 4, P])
        d_in, d_const, rw_ps, rw_sb = sem("d_in"), sem("d_const"), sem("rw_ps"), sem("rw_sb")
        qd_sb, prod_ready, s1_done, e_ready, p_exp, p_ready = (sem(n) for n in (
            "qd_sb", "prod_ready", "s1_done", "e_ready", "p_exp", "p_ready"))
        t1_ps, t1_sb, px_ps, pv_sb, od_ready, o1_ps, x2_done = (sem(n) for n in (
            "t1_ps", "t1_sb", "px_ps", "pv_sb", "od_ready", "o1_ps", "x2_done"))
        d_dve, z_ready, pd_sb = sem("d_dve"), sem("z_ready"), sem("pd_sb")
        NSTEP = NST * B // 4

        with nc.Block() as block:
            @block.sync
            def _(sp):
                for n, name in enumerate(("relk", "relv")):
                    for h in range(NH):
                        sp.dma_start(relrow[h * HD:(h + 1) * HD, n, :], a[name]).then_inc(d_in, 16)
                sp.dma_start(sel[:, :], a["sel"]).then_inc(d_in, 16)
                sp.dma_start(wout[:, :], a["out_w"]).then_inc(d_in, 16)
                sp.dma_start(bout_row[:, :], a["out_b"]).then_inc(d_in, 16)
            NDI = 16 * (2 * NH + 3)

            def steps(eng, body):
                with eng.Fori(0, NST) as st:
                    with eng.Fori(0, B // 4) as q4:
                        body(st, q4, st * 4 + q4)

            def s_cols(t, st):
                return t[:, :, bass.ds(st * P, P)]

            @block.gpsimd
            def _(pool):
                nc.gpsimd.memset(ones_row[:, :], 1.0)
                pool.wait_ge(d_in, NDI)
                for n, rel in enumerate((relk, relv)):
                    ins = nc.gpsimd.tensor_tensor(rel[:, :, :], relrow[:, n, :].unsqueeze(2).to_broadcast([P, NREL, NH]),
                                                  sel[:, :].unsqueeze(1).to_broadcast([P, NREL, NH]), ALU.mult)
                ins.then_inc(d_const, 1)
                pool.sem_inc(s1_done, 2)

                def body(st, q4, i):
                    for n in range(4):
                        pool.wait_ge(s1_done, i * 4 + (n + 1))
                        q = q1T[:, bass.ds(q4 * 4 + n, 1), bass.ds(st * P, P)]
                        nc.gpsimd.tensor_tensor(PROD[:, n % 2], s_cols(k1T, st), q.to_broadcast([P, B, P]), ALU.mult)\
                            .then_inc(prod_ready, 1)
                    for pair in range(2):
                        pool.wait_ge(z_ready, i * 2 + (pair + 1))
                        for m in range(2):
                            ins = nc.gpsimd.tensor_tensor(EP[:, pair, m], EP[:, pair, m],
                                                          MX[:, pair, 1, m, :].unsqueeze(1).to_broadcast([P, B, NH]),
                                                          ALU.mult)
                        ins.then_inc(p_ready, 1)
                steps(pool, body)

            @block.tensor
            def _(pe):
                pe.wait_ge(d_const, 1)
                for w in range(NWIN):
                    if w >= 16 and w % 4 == 0:
                        pe.wait_ge(rw_sb, w // 4 - 3)
                    ins = nc.tensor.matmul(psX[:, w // 8 % 2, w // 4 % 2, w % 4, :],
                                           relv[:, 1 + w:1 + w + HD, :].rearrange("p r h -> p (r h)"), wout[:, :],
                                           start=True, stop=True)
                    if w % 4 == 3:
                        ins.then_inc(rw_ps, 1)
                pe.wait_ge(rw_sb, NWIN // 4)
                pe.sem_inc(px_ps, 2)

                def body(st, q4, i):
                    for n in range(4):
                        pair, m = n // 2, n % 2
                        pe.wait_ge(qd_sb, i * 4 + (n + 1))
                        wait_apart(pe, e_ready, i * 2 + (pair + 1))
                        nc.tensor.matmul(psS1[:, pair, m, :], QD[:, n, :],
                                         relk[:, bass.ds(MAXREL - n - q4 * 4, B), :].rearrange("p r h -> p (r h)"),
                                         start=True, stop=False)
                        pe.wait_ge(prod_ready, i * 4 + (n + 1))
                        for t in range(B):
                            ins = nc.tensor.matmul(psS1[:, pair, m, t * NH:(t + 1) * NH], PROD[:, n % 2, t, :], sel[:, :],
                                                   start=False, stop=(t == B - 1))
                        ins.then_inc(s1_done, 1)
                    for n in range(4):
                        pair, m = n // 2, n % 2
                        if m == 0:
                            pe.wait_ge(p_ready, i * 2 + (pair + 1))
                            pe.wait_ge(t1_sb, i * 2 + (pair + 1))
                            for mm in range(2):
                                for c in range(2):
                                    ins = nc.tensor.transpose(
                                        psT1[:, mm, c, :],
                                        EP[:, pair, mm, c * HD:(c + 1) * HD, :].rearrange("p t h -> p (t h)"), ident[:, :])
                            ins.then_inc(t1_ps, 1)
                        for half in range(2):
                            pe.wait_ge(pv_sb, i * 8 + (n * 2 + half + 1))
                            pe.wait_ge(pd_sb, i * 8 + (n * 2 + half + 1))
                            for t in range(8):
                                ins = nc.tensor.transpose(psX[:, half, t // 4, t % 4, :], PD[:, half, t, :], ident[:, :])
                            ins.then_inc(px_ps, 1)
                        if m == 1:
                            pe.wait_ge(t1_sb, i * 2 + (pair + 2))
                            if pair == 0:
                                pe.wait_ge(x2_done, i + 1)
                            for mm in range(2):
                                q = pair * 2 + mm
                                pe.wait_ge(od_ready, i * 4 + (q + 1))
                                nc.tensor.matmul(psO1[:, q, :], OD[:, mm, :], wout[:, :], start=True, stop=False)
                                for c in range(2):
                                    nc.tensor.matmul(psO1[:, q, :], PTS[:, pair, mm, c, :],
                                                     RW[:, bass.ds((8 * c + 15 - q - q4 * 4) * D, D)], start=False, stop=False)
                                ins = nc.tensor.matmul(psO1[:, q, :], ones_row[:, :], bout_row[:, :], start=False, stop=True)
                            ins.then_inc(o1_ps, 1)
                steps(pe, body)

            @block.scalar
            def _(act):
                for r in range(NWIN // 4):
                    act.wait_ge(rw_ps, r + 1)
                    nc.scalar.copy(RW[:, r * 4 * D:(r * 4 + 4) * D],
                                   psX[:, r // 2 % 2, r % 2, :, :].rearrange("p a b -> p (a b)")).then_inc(rw_sb, 1)
                act.sem_inc(t1_sb, 1)

                def body(st, q4, i):
                    for n in range(4):
                        if n == 0:
                            act.wait_ge(s1_done, i * 4 + 2)
                        q = q1T[:, bass.ds(q4 * 4 + n, 1), bass.ds(st * P, P)].rearrange("p a s -> p (a s)")
                        nc.scalar.copy(QD[:, n, :], q).then_inc(qd_sb, 1)
                    for pair in range(2):
                        act.wait_ge(e_ready, i * 2 + (pair + 3))
                        ep = EP[:, pair].rearrange("p m t h -> p (m t h)")
                        nc.scalar.activation(ep, ep, ACT.Exp).then_inc(p_exp, 1)
                    for pair in range(2):
                        act.wait_ge(t1_ps, i * 2 + (pair + 1))
                        act.wait_ge(x2_done, i + 1)
                        nc.scalar.copy(PTS[:, pair].rearrange("p m c s -> p (m c s)"),
                                       psT1[:, :, :, :].rearrange("p m c s -> p (m c s)")).then_inc(t1_sb, 1)
                        for m in range(2):
                            for half in range(2):
                                act.wait_ge(px_ps, i * 8 + (pair * 4 + m * 2 + half + 1))
                                nc.scalar.copy(PD[:, half].rearrange("p t (h e) -> p (t h) e", e=HD),
                                               EP[:, pair, m, half * 8:half * 8 + 8, :].rearrange("p t h -> p (t h)")
                                               .unsqueeze(2).to_broadcast([P, 8 * NH, HD])).then_inc(pd_sb, 1)
                steps(act, body)

            @block.vector
            def _(dve):
                link, at, count = linker(dve, d_dve)
                dve.sem_inc(e_ready, 2)
                dve.sem_inc(pv_sb, 2)
                dve.sem_inc(x2_done, 1)
                per = 2 + 2 + 4

                def body(st, q4, i):
                    at(i * per)
                    for pair in range(2):
                        dve.wait_ge(s1_done, i * 4 + (2 * pair + 4))
                        sc = psS1[:, pair].rearrange("p m (t h) -> p m h t", h=NH)
                        link(nc.vector.tensor_reduce(MX[:, pair, 0], sc, AX.X, ALU.max))
                        for m in range(2):
                            ins = nc.vector.tensor_tensor(
                                EP[:, pair, m], psS1[:, pair, m].rearrange("p (t h) -> p t h", h=NH),
                                MX[:, pair, 0, m, :].unsqueeze(1).to_broadcast([P, B, NH]), ALU.subtract)
                        ins.then_inc(e_ready, 1)
                    for pair in range(2):
                        dve.wait_ge(p_exp, i * 2 + (pair + 1))
                        link(nc.vector.tensor_reduce(MX[:, pair, 0], EP[:, pair].rearrange("p m t h -> p m h t"),
                                                     AX.X, ALU.add))
                        nc.vector.reciprocal(MX[:, pair, 1], MX[:, pair, 0]).then_inc(z_ready, 1)
                    for n in range(4):
                        for half in range(2):
                            dve.wait_ge(px_ps, i * 8 + (n * 2 + half + 3))
                            ins = nc.vector.tensor_tensor(
                                PV[:, half * 8:half * 8 + 8, :], psX[:, half].rearrange("p a b s -> p (a b) s"),
                                v1T[:, half * 8:half * 8 + 8, bass.ds(st * P, P)], ALU.mult)
                            ins.then_inc(pv_sb, 1)
                        dve.wait_ge(pv_sb, i * 8 + (n * 2 + 4))
                        if n == 2:
                            dve.wait_ge(o1_ps, i * 2 + 1)
                        link(nc.vector.tensor_reduce(OD[:, n % 2, :], PV[:, :, :].rearrange("p t s -> p s t"),
                                                     AX.X, ALU.add))
                        dve.sem_inc(od_ready, 1)
                    dve.wait_ge(o1_ps, i * 2 + 2)
                    xv = X[:, bass.ds(q4 * 4, 4), bass.ds(st, 1), :].rearrange("p t a d -> p t (a d)")
                    nc.vector.tensor_tensor(xv, psO1[:, :, :], xv, ALU.add).then_inc(x2_done, 1)
                    assert count() == per
                steps(dve, body)
        pd.close()

        pe_ = ExitStack()
        carved[0] = 0
        GUW = carve([P, NE, 2 * FI])
        DW = carve([P, NE, len(FC), D])
        GUWf, DWf = GUW.rearrange("p e f -> p (e f)"), DW.rearrange("p e c d -> p (e c d)")
        XB, XBT = carve([P, 2, P]), carve([P, 2, P])
        TH, HH = carve([P, 2, FI]), carve([P, 2, FI])
        HT, YB = carve([P, 2, 3 * P]), carve([P, 2, D])
        psGU = ps(pe_, "psGU", [P, 2, 2, S])
        psXB = ps(pe_, "psXB", [P, S])
        psHT = ps(pe_, "psHT", [P, 3, P])
        psY = ps(pe_, "psY", [P, 2, S])
        ew_in = sem("ew_in")
        xb_in = [sem("xb_in0"), sem("xb_in1")]
        y2_out = [sem("y2_out0"), sem("y2_out1")]
        e_silu = sem("e_silu")
        xb_ps, xb_sb, gu_ps, th_sb, hh_sb, ht_ps, ht_sb, y2_ps, y2_sb = (sem(n) for n in (
            "xb_ps", "xb_sb", "gu_ps", "th_sb", "hh_sb", "ht_ps", "ht_sb", "y2_ps", "y2_sb"))
        a_add, out_done = sem("a_add"), sem("out_done")
        gathered = [sem(f"gathered{b}") for b in range(B)]

        def blocks_behind(eng, first, second):
            first(0, 0)
            with eng.Fori(0, NBLK // 2 - 1) as i:
                for s in range(2):
                    first(i * 2 + (s + 1), 1 - s)
                    second(i * 2 + s, s, i)
            first(NBLK - 1, 1)
            second(NBLK - 2, 0, NBLK // 2 - 1)
            second(NBLK - 1, 1, NBLK // 2 - 1)

        with nc.Block() as block:
            @block.sync
            def _(sp):
                sp.dma_start(GUW, a["gate_up"].rearrange("p (e f) -> p e f", e=NE)).then_inc(ew_in, 16)
                for c, w in enumerate(FC):
                    sp.dma_start(DW[0:w, :, c, :], a["down"][c * P:c * P + w, :].rearrange("p (e d) -> p e d", e=NE))\
                      .then_inc(ew_in, 16)
                sp.sem_inc(xb_ps, 2)
                sp.sem_inc(y2_out[0], 16)
                sp.sem_inc(y2_out[1], 16)

                def load(n, s):
                    sp.wait_ge(xb_ps, n + 1)
                    sp.dma_start(XB[:, s, :], sorted_x[bass.ds(n * P, P), :]).then_inc(xb_in[s], 16)

                def store(n, s):
                    sp.wait_ge(y2_sb, n + 3)
                    sp.dma_start(sorted_y[bass.ds(n * P, P), :], YB[:, s, :]).then_inc(y2_out[s], 16)
                for n in range(3):
                    load(n, n % 2)
                with sp.Fori(0, NBLK // 2 - 2) as i:
                    for s in range(2):
                        load(i * 2 + (s + 3), 1 - s)
                        store(i * 2 + s, s)
                load(NBLK - 1, 1)
                for n in range(NBLK - 4, NBLK):
                    store(n, n % 2)
                for b in range(B):
                    sp.wait_ge(a_add, b + 1)
                    sp.dma_start(out[b].rearrange("(n p) d -> p n d", p=P), X[:, b]).then_inc(out_done, 16)
                sp.wait_ge(out_done, 16 * B)

            @block.vector
            def _(dve):
                def first(n, s):
                    dve.wait_ge(th_sb, n + 1)
                    nc.vector.scalar_tensor_tensor(TH[:, s, :], TH[:, s, :], 1.0, psGU[:, s, 0, 0:FI],
                                                   ALU.add, ALU.mult).then_inc(e_silu, 1)
                    dve.wait_ge(e_silu, n + 1)
                    nc.vector.scalar_tensor_tensor(HH[:, s, :], TH[:, s, :], 0.5, psGU[:, s, 1, 0:FI],
                                                   ALU.mult, ALU.mult).then_inc(hh_sb, 1)

                def second(n, s, i):
                    dve.wait_ge(y2_ps, n + 1)
                    dve.wait_ge(y2_out[s], i * 16 + 16)
                    nc.vector.tensor_copy(YB[:, s, :], psY[:, s, 0:D]).then_inc(y2_sb, 1)
                dve.sem_inc(y2_sb, 2)
                blocks_behind(dve, first, second)
                for b in range(B):
                    dve.wait_ge(gathered[b], 16 * NST)
                    nc.vector.tensor_tensor(X[:, b], X[:, b], HX[:, b], ALU.add).then_inc(a_add, 1)

            @block.scalar
            def _(act):
                def first(n, s):
                    act.wait_ge(xb_ps, n + 3)
                    nc.scalar.copy(XBT[:, s, :], psXB[:, 0:P]).then_inc(xb_sb, 1)
                    act.wait_ge(gu_ps, n + 1)
                    nc.scalar.activation(TH[:, s, :], psGU[:, s, 0, 0:FI], ACT.Tanh, scale=0.5).then_inc(th_sb, 1)

                def second(n, s, i):
                    act.wait_ge(ht_ps, n + 1)
                    nc.scalar.copy(HT[:, s, 0:2 * P], psHT[:, 0:2, :].rearrange("p c s -> p (c s)"))
                    nc.scalar.copy(HT[0:FC[2], s, 2 * P:3 * P], psHT[0:FC[2], 2, :]).then_inc(ht_sb, 1)
                blocks_behind(act, first, second)

            @block.tensor
            def _(pe):
                pe.wait_ge(ew_in, 64)

                def expert(n):
                    return pe.value_load(eb[0:1, bass.ds(n, 1)], min_val=0, max_val=NE - 1)

                def first(n, s):
                    pe.wait_ge(xb_in[s], n * 8 + (16 if s == 0 else 8))
                    nc.tensor.transpose(psXB[:, 0:P], XB[:, s, :], ident[:, :]).then_inc(xb_ps, 1)
                    wait_apart(pe, xb_sb, n + 1)
                    e = expert(n)
                    for c in range(2):
                        ins = nc.tensor.matmul(psGU[:, s, c, 0:FI], XBT[:, s, :], GUWf[:, bass.ds(e * (2 * FI) + c * FI, FI)],
                                               start=True, stop=True)
                    ins.then_inc(gu_ps, 1)

                def second(n, s, i):
                    pe.wait_ge(hh_sb, n + 1)
                    for c, w in enumerate(FC):
                        ins = nc.tensor.transpose(psHT[0:w, c, :], HH[:, s, c * P:c * P + w], ident[:, :])
                    ins.then_inc(ht_ps, 1)
                    pe.wait_ge(ht_sb, n + 1)
                    wait_apart(pe, y2_sb, n + 1)
                    e = expert(n)
                    for c, w in enumerate(FC):
                        ins = nc.tensor.matmul(psY[:, s, 0:D], HT[0:w, s, c * P:(c + 1) * P],
                                               DWf[0:w, bass.ds(e * (3 * D) + c * D, D)], start=(c == 0), stop=(c == 2))
                    ins.then_inc(y2_ps, 1)
                blocks_behind(pe, first, second)

            @block.gpsimd
            def _(pool):
                for s in range(2):
                    pool.wait_ge(y2_out[s], 16 * (NBLK // 2 + 1))
                for b in range(B):
                    for st in range(NST):
                        j = b * NST + st
                        pool.indirect_dma_start(HX[:, b, st, :], None, sorted_y,
                                                bass.IndirectOffsetOnAxis(pos[:, j:j + 1], 0)).then_inc(gathered[b], 16)
        pe_.close()


def kernel(**inputs):
    import numpy as _np
    import concourse.bacc as _bacc
    from concourse import mybir as _mybir
    from concourse.bass_utils import run_bass_kernel_spmd as _run

    v = {k: _np.asarray(x) for k, x in inputs.items()}

    def heads_inner(w):
        w = _np.moveaxis(w, 0, -2)
        w = w.reshape(w.shape[:-2] + (NG, HG, HD))
        return _np.swapaxes(w, -1, -2).reshape(w.shape[:-3] + (D,))

    eye = _np.eye(P, dtype=_np.float32)
    n = _np.arange(P)
    arrays = {
        "x": v["L0_attn_inputs"],
        "wq": heads_inner(v["L0_attn_W_q"]), "wk": heads_inner(v["L0_attn_W_k"]),
        "wv": v["L0_attn_W_v"].transpose(1, 0, 2).reshape(D, D),
        "bq": heads_inner(v["L0_attn_b_q"]).reshape(D, 1), "bk": heads_inner(v["L0_attn_b_k"]).reshape(D, 1),
        "bv": v["L0_attn_b_v"].reshape(1, D),
        "attn_wo": v["L0_attn_W_o"].T, "attn_bo": v["L0_attn_b_o"].reshape(1, D),
        "in_c": v["L0_ffn_in_c"].reshape(D, 1), "ffn_bo": v["L0_ffn_bo"].reshape(1, D),
        "in_proj": v["L1_attn_in_proj_weight"].T, "in_bias": v["L1_attn_in_proj_bias"].reshape(3, D).T,
        "relk": v["L1_attn_rel_k_table"].T, "relv": v["L1_attn_rel_v_table"].T,
        "out_w": v["L1_attn_out_w"].T, "out_b": v["L1_attn_out_b"].reshape(1, D),
        "router": v["L1_ffn_router_w"].T,
        "gate_up": _np.concatenate([v["L1_ffn_gate_w"], v["L1_ffn_up_w"]], axis=1).transpose(2, 0, 1).reshape(D, NE * 2 * FI),
        "down": v["L1_ffn_down_w"].transpose(2, 0, 1).reshape(FI, NE * D),
        "ident": eye, "ones": _np.ones((P, P), _np.float32),
        "before": (n[:, None] < n[None, :]).astype(_np.float32),
        "mask": _np.where(n[None, :] > n[:, None], NEG, 0.0).astype(_np.float32),
        "sel": (n[:, None] // HD == _np.arange(NH)[None, :]).astype(_np.float32),
        "iota8": _np.arange(NE, dtype=_np.float32).reshape(1, NE) - NE,
        "iota64": _np.arange(NTILE, dtype=_np.float32).reshape(1, NTILE) * P,
        "iotab": _np.arange(NBLK, dtype=_np.float32).reshape(1, NBLK),
    }
    for w in ("wf", "wi", "wc", "wo", "uf", "ui", "uc", "uo"):
        arrays[w] = v["L0_ffn_" + w].T
    for b in ("bf", "bi", "bc"):
        arrays[b] = v["L0_ffn_" + b].reshape(D, 1)

    nc = _bacc.Bacc("TRN2", target_bir_lowering=False, num_devices=1)
    aps = {}
    arrays = {k: _np.ascontiguousarray(x) for k, x in arrays.items()}
    for k, x in arrays.items():
        aps[k] = nc.dram_tensor(f"in_{k}", x.shape, _mybir.dt.from_np(x.dtype), kind="ExternalInput").ap()
    out = nc.dram_tensor("out", (B, S, D), F32, kind="ExternalOutput").ap()
    program(nc, aps, out)
    r = _run(nc, [{f"in_{k}": x for k, x in arrays.items()}], core_ids=[0])
    return r.results[0]["out"]
```

```python
import math
from contextlib import ExitStack

import numpy as np
import concourse.bass as bass
from concourse import mybir

F32 = mybir.dt.float32
BF16 = mybir.dt.bfloat16
F16 = mybir.dt.float16
I32 = mybir.dt.int32
U32 = mybir.dt.uint32
ALU = mybir.AluOpType
ACT = mybir.ActivationFunctionType
AX = mybir.AxisListType

P = 128
B = 16
S = 512
D = 128
NST = S // P
NH = 16
HD = D // NH
HG = 4
NG = NH // HG
GW = HG * HD
NREL = 33
MAXREL = 16
NE = 8
FI = 352
FC = [128, 128, 96]
NTILE = B * NST
NBLK = NTILE + NE
EPS = 1e-5
SCALE = float(HD) ** -0.5
NEG = -1.0e30
NWIN = B + HD

UNITS = [[(3, 0)], [(2, 0), (0, 3 * P)], [(1, 0)]]
GU = HG * len(UNITS)
NU = NG * GU
LAG_T = 2
LAG_S = 19
LAG_V = 23
LAG_F = 28
LAG_NORM = 29
RING = 4
GAIN = 10 * math.log(2)


def wait_apart(eng, signal, value):
    eng.wait_ge(signal, value)
    eng.sem_inc(APART[0], 1)


APART = []


def linker(eng, signal):
    state = {"base": 0, "n": 0}

    def link(ins, apart=False):
        state["n"] += 1
        ins.then_inc(signal, 1)
        (wait_apart if apart else type(eng).wait_ge)(eng, signal, state["base"] + state["n"])

    def at(base):
        state["base"], state["n"] = base, 0

    return link, at, lambda: state["n"]


def layer_norm(nc, link, stats, mv, rstd, var_ready, wait_rstd, src, dst):
    for t in range(4):
        ins = nc.vector.bn_stats(stats[:, t, :], src(t))
    link(ins, apart=True)
    for t in range(4):
        ins = nc.vector.bn_aggr(mv[:, t, :], stats[:, t, :])
    link(ins)
    nc.vector.tensor_scalar(rstd[:, 0, :], mv[:, :, 1], EPS, None, ALU.add).then_inc(var_ready, 1)
    wait_rstd()
    for t in range(4):
        ins = nc.vector.tensor_scalar(dst(t), src(t), mv[:, t, 0:1], rstd[:, 1, t:t + 1], ALU.subtract, ALU.mult)
    return ins


def program(nc, a, out):
    with ExitStack() as ctx:
        def sem(name):
            return ctx.enter_context(nc.semaphore(name))

        def sb(where, name, shape, dt=F32):
            return where.enter_context(nc.sbuf_tensor(name, shape, dt))

        def ps(where, name, shape, dt=F32):
            return where.enter_context(nc.psum_tensor(name, shape, dt))

        APART[:] = [sem("apart")]
        q_parts = nc.dram_tensor("q_parts", [B * NG, 3, GW, S], BF16, kind="Internal").ap()
        k_parts = nc.dram_tensor("k_parts", [B * NG, 3, GW, S], BF16, kind="Internal").ap()
        sorted_x = nc.dram_tensor("sorted_x", [NBLK * P, D], F32, kind="Internal").ap()
        sorted_y = nc.dram_tensor("sorted_y", [NBLK * P, D], F32, kind="Internal").ap()

        ident = sb(ctx, "ident", [P, P])
        X = sb(ctx, "X", [P, B, NST, D])
        HX = sb(ctx, "HX", [P, B, NST, D])
        BIG = sb(ctx, "BIG", [P, 3, B * S])
        C2 = sb(ctx, "C2", [P, S])
        uo_h = sb(ctx, "uo_h", [P, D])
        stats = sb(ctx, "stats", [P, 4, 6])
        mv = sb(ctx, "mv", [P, 4, 2])
        rstd = sb(ctx, "rstd", [P, 3, 4])
        LOG = sb(ctx, "LOG", [P, NTILE, NE])
        pos = sb(ctx, "pos", [P, NTILE], I32)
        eb = sb(ctx, "eb", [1, NBLK], I32)
        attn_space = ExitStack()
        O_all = sb(attn_space, "O_all", [P, B * NG, NST, GW])
        V_all = BIG[:, 0, :].rearrange("p (i k c) -> p i k c", i=B * NG, k=NST)

        carved = [B * S]

        def carve(shape, dt=F32):
            n = int(np.prod(shape[1:])) * (1 if dt == F32 else 2) // (1 if dt == F32 else 4)
            at = carved[0]
            carved[0] += n
            assert carved[0] <= 3 * B * S
            v = BIG[:, :, :].rearrange("p a n -> p (a n)")[:, at:at + n]
            if dt != F32:
                v = v.bitcast(dt)
            names = " ".join(f"d{n}" for n in range(len(shape) - 1))
            return v.rearrange(f"p ({names}) -> p {names}", **{f"d{n}": shape[n + 1] for n in range(len(shape) - 2)})

        pa = ExitStack()
        WN = ("wq", "wk", "wv", "wf", "wi", "wc", "wo", "uf", "ui", "uc", "uo")
        W = {n: carve([P, D]) for n in WN}
        bias_cols = carve([P, 6])
        bias_half = carve([P, 4])
        bv_row, bo_row = carve([P, D]), carve([P, D])
        U2 = carve([P, 3, D])
        XN, XNT = carve([P, 2, 4, D]), carve([P, 2, S])
        QK = carve([P, 2, 2, S])
        RES = carve([P, 2, S])
        PARTS = carve([P, 2, 2, 3, S], BF16)
        TG, CA = carve([P, 3, S]), carve([P, 2, S])
        NZ = 4
        zero = carve([P, NBLK * D // NZ])
        psT = ps(pa, "psT", [P, S])
        psQ = ps(pa, "psQ", [P, 2, S])
        psV, psH = ps(pa, "psV", [P, 4, D]), ps(pa, "psH", [P, 4, D])
        psG = ps(pa, "psG", [P, 3, S])

        weights_in, x_in, zeroed, zero_out, halved = (sem(n) for n in (
            "weights_in", "x_in", "zeroed", "zero_out", "halved"))
        xn_ready, xnT_ps, xnT_ready = sem("xn_ready"), sem("xnT_ps"), sem("xnT_ready")
        q_ps, k_ps, v_ps, h_ps, g_ps = (sem(n) for n in ("q_ps", "k_ps", "v_ps", "h_ps", "g_ps"))
        qk_sb, v_out, h_out, gates_ready, c_ready, parts_ready, parts_stored = (sem(n) for n in (
            "qk_sb", "v_out", "h_out", "gates_ready", "c_ready", "parts_ready", "parts_stored"))
        a_dve, a_pool = sem("a_dve"), sem("a_pool")
        var_ready, rstd_ready = sem("var_ready"), sem("rstd_ready")

        def power(eng, n):
            eng.wait_ge(var_ready, n + 1)
            nc.gpsimd.tensor_tensor(rstd[:, 1, :], rstd[:, 0, :], rstd[:, 2, :], ALU.pow).then_inc(rstd_ready, 1)
        NWA = len(WN) + 6 + 3

        def two_steps(eng, body):
            with eng.Fori(0, B // 2 - 1) as i:
                body(i * 2, 0, False)
                body(i * 2 + 1, 1, False)
            body(B - 2, 0, False)
            body(B - 1, 1, True)

        def b_tiles(t, b):
            return t[:, bass.ds(b, 1)].rearrange("p a n d -> p (a n) d")

        with nc.Block() as block:
            @block.sync
            def _(sp):
                for n in WN:
                    sp.dma_start(W[n], a[n]).then_inc(weights_in, 16)
                for c, n in enumerate(("bq", "bk", "bf", "bi", "bc", "in_c")):
                    sp.dma_start(bias_cols[:, c:c + 1], a[n]).then_inc(weights_in, 16)
                sp.dma_start(bv_row, a["bv"].to_broadcast([P, D])).then_inc(weights_in, 16)
                sp.dma_start(bo_row, a["ffn_bo"].to_broadcast([P, D])).then_inc(weights_in, 16)
                sp.dma_start(ident[:, :], a["ident"]).then_inc(weights_in, 16)

                def load_x(b):
                    sp.dma_start(b_tiles(X, b), a["x"][bass.ds(b, 1)].rearrange("a (n p) d -> p (a n) d", p=P))\
                      .then_inc(x_in, 16)
                    sp.wait_ge(x_in, b * 16 + 16)
                load_x(0)

                def body(b, s, last):
                    if not last:
                        load_x(b + 1)
                    for n, parts in enumerate((q_parts, k_parts)):
                        sp.wait_ge(parts_ready, b * 2 + (n + 5))
                        for g in range(NG):
                            sp.dma_start(parts[bass.ds(b * NG + g, 1)].rearrange("g t r s -> (g r) t s"),
                                         PARTS[g * GW:(g + 1) * GW, s, n]).then_inc(parts_stored, 16)
                    wait_apart(sp, parts_stored, b * 128 + (128 + 256))
                two_steps(sp, body)

            @block.scalar
            def _(act):
                act.wait_ge(zeroed, 1)
                zx = sorted_x.rearrange("(z p r) d -> z p (r d)", z=NZ, p=P)
                for z in range(NZ):
                    act.dma_start(zx[z], zero).then_inc(zero_out, 16)
                act.sem_inc(qk_sb, 2)
                act.sem_inc(gates_ready, 1)
                act.wait_ge(weights_in, 16 * NWA)
                nc.scalar.mul(bias_half[:, 0:1], bias_cols[:, 0:1], SCALE)
                nc.scalar.mul(bias_half[:, 1:3], bias_cols[:, 2:4], 0.5)
                for n, w in enumerate(("uf", "ui", "uc")):
                    nc.scalar.mul(U2[:, n, :], W[w], 0.5)
                nc.scalar.mul(uo_h[:, :], W["uo"], 0.5).then_inc(halved, 1)
                act.wait_ge(halved, 1)

                def body(b, s, last):
                    act.wait_ge(xnT_ps, b + 1)
                    nc.scalar.copy(XNT[:, s, :], psT[:, :]).then_inc(xnT_ready, 1)
                    act.wait_ge(q_ps, b + 1)
                    act.wait_ge(parts_ready, b * 2 + 2)
                    nc.scalar.activation(QK[:, s, 0, :], psQ[:, 0, :], ACT.Identity,
                                         bias=bias_half[:, 0:1], scale=SCALE).then_inc(qk_sb, 1)
                    act.wait_ge(k_ps, b + 1)
                    nc.scalar.activation(QK[:, s, 1, :], psQ[:, 1, :], ACT.Identity,
                                         bias=bias_cols[:, 1:2]).then_inc(qk_sb, 1)
                    act.wait_ge(g_ps, b + 1)
                    act.wait_ge(c_ready, b + 1)
                    nc.scalar.activation(TG[:, 0, :], psG[:, 0, :], ACT.Tanh, bias=bias_half[:, 1:2], scale=0.5)
                    nc.scalar.activation(TG[:, 1, :], psG[:, 1, :], ACT.Tanh, bias=bias_half[:, 2:3], scale=0.5)
                    nc.scalar.activation(TG[:, 2, :], psG[:, 2, :], ACT.Tanh,
                                         bias=bias_cols[:, 4:5]).then_inc(gates_ready, 1)
                two_steps(act, body)
                act.wait_ge(zero_out, 16 * NZ)

            @block.vector
            def _(dve):
                link, at, count = linker(dve, a_dve)
                nc.vector.memset(zero, 0.0).then_inc(zeroed, 1)
                dve.sem_inc(v_out, 1)
                dve.sem_inc(h_out, 1)
                dve.wait_ge(weights_in, 16 * NWA)
                link(nc.vector.memset(C2[:, :], 0.0))
                nc.vector.tensor_scalar(C2[:, :], C2[:, :], bias_cols[:, 5:6], 2.0, ALU.add, ALU.mult)\
                    .then_inc(c_ready, 1)

                def norm(b, s):
                    dve.wait_ge(x_in, b * 16 + 16)
                    layer_norm(nc, link, stats, mv, rstd, var_ready, lambda: dve.wait_ge(rstd_ready, b + 1),
                               lambda t: b_tiles(X, b)[:, t, :], lambda t: XN[:, s, t, :]).then_inc(xn_ready, 1)
                norm(0, 0)
                first, per = count(), 3

                def body(b, s, last):
                    at(b * per + first)
                    dve.wait_ge(v_ps, b + 1)
                    for t in range(NST):
                        ins = nc.vector.tensor_tensor(V_all[:, bass.ds(b * NG, NG), t, :],
                                                      psV[:, t, :].rearrange("p (g c) -> p g c", g=NG),
                                                      bv_row.rearrange("p (g c) -> p g c", g=NG), ALU.add)
                    ins.then_inc(v_out, 1)
                    dve.wait_ge(h_ps, b + 1)
                    nc.vector.tensor_tensor(b_tiles(HX, b), psH[:, :, :],
                                            bo_row.unsqueeze(1).to_broadcast([P, NST, D]), ALU.add).then_inc(h_out, 1)
                    if not last:
                        norm(b + 1, 1 - s)
                    dve.wait_ge(gates_ready, b + 2)
                    nc.vector.scalar_tensor_tensor(CA[:, 0, :], TG[:, 0, :], 1.0, C2[:, :], ALU.add, ALU.mult)
                    link(nc.vector.scalar_tensor_tensor(CA[:, 1, :], TG[:, 1, :], 1.0, TG[:, 2, :], ALU.add, ALU.mult))
                    nc.vector.scalar_tensor_tensor(C2[:, :], CA[:, 0, :], 0.5, CA[:, 1, :], ALU.mult, ALU.add)\
                        .then_inc(c_ready, 1)
                    dve.wait_ge(c_ready, b + 2)
                    assert last or count() == per
                two_steps(dve, body)

            @block.gpsimd
            def _(pool):
                pool.sem_inc(parts_ready, 4)
                pool.sem_inc(parts_stored, 256)

                nc.gpsimd.memset(rstd[:, 2, :], -0.5).then_inc(a_pool, 1)
                pool.wait_ge(a_pool, 1)
                power(pool, 0)

                def body(b, s, last):
                    pool.wait_ge(parts_stored, b * 128 + 128)
                    for n in range(2):
                        c = b * 6 + (n * 3 + 1)
                        wait_apart(pool, qk_sb, b * 2 + (n + 3))
                        src, part = QK[:, s, n, :], PARTS[:, s, n]
                        nc.gpsimd.tensor_copy(part[:, 0, :], src).then_inc(a_pool, 1)
                        pool.wait_ge(a_pool, c + 1)
                        nc.gpsimd.tensor_tensor(RES[:, n, :], src, part[:, 0, :], ALU.subtract).then_inc(a_pool, 1)
                        wait_apart(pool, a_pool, c + 2)
                        nc.gpsimd.tensor_copy(part[:, 1, :], RES[:, n, :]).then_inc(a_pool, 1)
                        pool.wait_ge(a_pool, c + 3)
                        nc.gpsimd.tensor_tensor(part[:, 2, :], RES[:, n, :], part[:, 1, :], ALU.subtract)\
                            .then_inc(parts_ready, 1)
                        if n == 0 and not last:
                            power(pool, b + 1)
                two_steps(pool, body)

            @block.tensor
            def _(pe):
                pe.wait_ge(weights_in, 16 * NWA)
                pe.wait_ge(halved, 1)

                def body(b, s, last):
                    pe.wait_ge(xn_ready, b + 1)
                    for t in range(4):
                        ins = nc.tensor.transpose(psT[:, t * P:(t + 1) * P], XN[:, s, t, :], ident[:, :])
                    ins.then_inc(xnT_ps, 1)
                    pe.wait_ge(xnT_ready, b + 1)
                    xT = XNT[:, s, :]
                    pe.wait_ge(qk_sb, b * 2 + 2)
                    nc.tensor.matmul(psQ[:, 0, :], W["wq"], xT, start=True, stop=True).then_inc(q_ps, 1)
                    nc.tensor.matmul(psQ[:, 1, :], W["wk"], xT, start=True, stop=True).then_inc(k_ps, 1)
                    pe.wait_ge(v_out, b + 1)
                    for t in range(4):
                        ins = nc.tensor.matmul(psV[:, t, :], xT[:, t * P:(t + 1) * P], W["wv"], start=True, stop=True)
                    ins.then_inc(v_ps, 1)
                    pe.wait_ge(h_out, b + 1)
                    for t in range(4):
                        ins = nc.tensor.matmul(psH[:, t, :], xT[:, t * P:(t + 1) * P], W["wo"], start=True, stop=True)
                    ins.then_inc(h_ps, 1)
                    pe.wait_ge(gates_ready, b + 1)
                    for n, w in enumerate(("wf", "wi", "wc")):
                        nc.tensor.matmul(psG[:, n, :], W[w], xT, start=True, stop=False)
                    pe.wait_ge(c_ready, b + 1)
                    for n in range(3):
                        ins = nc.tensor.matmul(psG[:, n, :], U2[:, n, :], C2[:, :], start=False, stop=True)
                    ins.then_inc(g_ps, 1)
                two_steps(pe, body)
        pa.close()

        pb = ExitStack()
        carved[0] = B * S
        maskb, identb = carve([P, P], BF16), carve([P, P], BF16)
        QS, KS = carve([P, NG, HG, S], BF16), carve([P, NG, HG, S], BF16)
        PR = carve([P, RING, S])
        P1, P2 = carve([P, RING, S], F16), carve([P, RING, S], F16)
        VG = carve([P, 2, NST, HG * (P + GW)], BF16)
        VG_heads = VG.rearrange("p g k (h x) -> p g k h x", h=HG)
        V1 = 3 * HD
        NROW = 6 * HD
        OS = sb(pb, "OS", [P, 2, S])
        maskf, pick = sb(pb, "maskf", [P, P]), sb(pb, "pick", [P, HG * (HD + 1)])
        NM = sb(pb, "NM", [P, 2, HG * NST])
        NR = sb(pb, "NR", [HG * NST, P])
        NP = sb(pb, "NP", [HG * NST, 3, P], BF16)
        VR = sb(pb, "VR", [P, NST, GW])
        RI = sb(pb, "RI", [P, 2, NST * HG])
        psS = ps(pb, "psS", [P, 2, S])
        psST = ps(pb, "psST", [P, 3, S])
        psO = ps(pb, "psO", [P, 2, S])
        psM = ps(pb, "psM", [P, S])
        psN = psM[0:HG * NST, 0:P]
        psF = psM[:, P:P + NST * HG * (HD + 1)].rearrange("p (q x) -> p q x", q=NST)

        mask_in, b_const, stack_clear = sem("mask_in"), sem("b_const"), sem("stack_clear")
        stack_in = [sem(f"stack_in{g}") for g in range(NG)]
        max_in = [sem(f"max_in{g}") for g in range(NG)]
        s_done, max_done, nt_done, n_split, v_split = (sem(n) for n in ("s_done", "max_done", "nt_done", "n_split", "v_split"))
        st_done, exp_done, p1_act, p1_dve, p2_done, pv_done = (sem(n) for n in (
            "st_done", "exp_done", "p1_act", "p1_dve", "p2_done", "pv_done"))
        o_evac, post_done, b_dve, norm_done = sem("o_evac"), sem("post_done"), sem("b_dve"), sem("norm_done")

        def keys_of(v):
            return {0: [(0, 0, 0, S)], 1: [(1, P, 0, 3 * P), (3, 3 * P, 3 * P, S)], 2: [(2, 2 * P, 0, 2 * P)]}[v % 3]

        def width(v):
            return 2 * P if v % 3 == 2 else S

        def skewed(eng, body):
            for u in range(NU):
                body(0, u, lambda lag, u=u: u - lag >= 0)
            with eng.Fori(1, B) as i:
                for u in range(NU):
                    body(i, u, lambda lag: True)
            for u in range(LAG_NORM + 1):
                body(B, u, lambda lag, u=u: u - lag < 0 and lag > 0)

        def group(i, v):
            return i * NG + v // GU

        with nc.Block() as block:
            @block.sync
            def _(sp):
                sp.dma_start(maskf[:, :], a["mask"]).then_inc(mask_in, 16)
                sp.dma_start(pick[:, :], a["pick"]).then_inc(mask_in, 16)
                sp.wait_ge(stack_clear, 1)

                def load(j, g):
                    for stack, parts, order in ((QS, q_parts, (0, 0, 0, 1, 1, 2)), (KS, k_parts, (0, 1, 2, 0, 1, 0))):
                        rows = parts[bass.ds(j, 1)].rearrange("a t (d h) s -> (a t) d (h s)", d=HD)
                        for r, t in enumerate(order):
                            sp.dma_start(stack[r * HD:(r + 1) * HD, g].rearrange("p h s -> p (h s)"),
                                         rows[t]).then_inc(stack_in[g], 16)

                def put_maxima(j, g):
                    sp.wait_ge(n_split, j * 4 + 4)
                    for t in range(3):
                        sp.dma_start(QS[NROW + t:NROW + t + 1, g].rearrange("p h (q s) -> p (h q) s", q=NST),
                                     NP[:, t, :]).then_inc(max_in[g], 16)
                for g in range(3):
                    load(g, g)
                with sp.Fori(0, B - 1) as i:
                    for g in range(NG):
                        put_maxima(i * NG + g, g)
                        wait_apart(sp, exp_done, i * NU + (g * GU + 3))
                        load(i * NG + (g + 3), (g + 3) % NG)
                for g in range(NG):
                    put_maxima((B - 1) * NG + g, g)
                    if g == 0:
                        sp.wait_ge(exp_done, (B - 1) * NU + 3)
                        load(B * NG - 1, NG - 1)

            @block.gpsimd
            def _(pool):
                nc.gpsimd.memset(KS[0:2 * GW], 1.0).then_inc(stack_clear, 1)
                pool.wait_ge(mask_in, 32)
                nc.gpsimd.tensor_copy(maskb, maskf[:, :])
                nc.gpsimd.tensor_copy(identb, ident[:, :])
                nc.gpsimd.memset(VG, 0.0).then_inc(b_const, 1)
                pool.wait_ge(b_const, 1)
                for g in range(2):
                    ins = nc.gpsimd.memset(VG_heads[:, g, :, :, V1:V1 + 1], 1.0)
                ins.then_inc(b_const, 1)
                pool.sem_inc(p2_done, RING)

                with pool.Fori(0, B * NG) as j:
                    for v in range(GU):
                        n = v // 3
                        if v % 3 == 1:
                            pool.wait_ge(p1_dve, j * HG + (n + 1))
                        else:
                            pool.wait_ge(p1_act, j * 2 * HG + (2 * n + 1 + v % 3 // 2))
                        w = width(v)
                        nc.gpsimd.tensor_tensor(P2[:, v % RING, 0:w], PR[:, v % RING, 0:w], P1[:, v % RING, 0:w],
                                                ALU.subtract).then_inc(p2_done, 1)

            @block.tensor
            def _(pe):
                pe.wait_ge(b_const, 2)
                pe.wait_ge(mask_in, 32)
                pe.sem_inc(pv_done, RING)

                def body(i, u, has):
                    if has(0):
                        g, h = u // GU, u % GU // 3
                        if u % GU == 0:
                            pe.wait_ge(stack_in[g], i * 192 + 192)
                        pe.wait_ge(max_done, i * NU + (u + 1))
                        bank = psS[:, u % 2, :]
                        for qb, c0 in UNITS[u % 3]:
                            nc.tensor.matmul(bank[:, c0:c0 + (qb + 1) * P], QS[0:NROW, g, h, qb * P:(qb + 1) * P],
                                             KS[0:NROW, g, h, 0:(qb + 1) * P], start=True, stop=False)
                            ins = nc.tensor.matmul(bank[:, c0 + qb * P:c0 + (qb + 1) * P], identb, maskb,
                                                   start=False, stop=True)
                        ins.then_inc(s_done, 1)
                    if has(LAG_T) and (u - LAG_T) % GU == GU - 1:
                        v = u - LAG_T
                        pe.wait_ge(max_done, i * NU + (v + 3))
                        pe.wait_ge(norm_done, group(i, v))
                        nc.tensor.transpose(psN, NM[:, v // GU % 2, :], ident[:, :]).then_inc(nt_done, 1)
                    if has(LAG_S):
                        v = u - LAG_S
                        g, h = v // GU % NG, v % GU // 3
                        if v % GU == 0:
                            pe.wait_ge(max_in[g], (i + v // NU) * 48 + 48)
                        pe.wait_ge(exp_done, i * NU + (v + 1))
                        bank = psST[:, v % 3, :]
                        for kb, q0, c0, c1 in keys_of(v):
                            nc.tensor.matmul(bank[:, c0:c1], KS[0:NROW + 3, g, h, kb * P:(kb + 1) * P],
                                             QS[0:NROW + 3, g, h, q0:S], start=True, stop=False)
                            ins = nc.tensor.matmul(bank[:, c0:c0 + P], maskb, identb, start=False, stop=True)
                        ins.then_inc(st_done, 1)
                    if has(LAG_V):
                        v = u - LAG_V
                        g, h = v // GU % 2, v % GU // 3
                        if v % GU == 0:
                            pe.wait_ge(v_split, group(i, v) * 4 + 4)
                            pe.wait_ge(o_evac, group(i, v) + 1)
                        pe.wait_ge(p2_done, i * NU + (v + (1 + RING)))
                        for kb, q0, c0, c1 in keys_of(v):
                            for n, part in enumerate((P1, P2)):
                                ins = nc.tensor.matmul(psO[:, g, q0:S], VG[:, g, kb, h * P:(h + 1) * P],
                                                       part[:, v % RING, c0:c1], start=(v % GU == 0 and n == 0),
                                                       stop=(v % GU == GU - 1 and n == 1))
                        ins.then_inc(pv_done, 1)
                    if has(LAG_F) and (u - LAG_F) % GU == GU - 1:
                        v = u - LAG_F
                        pe.wait_ge(o_evac, group(i, v) + 3)
                        n = group(i, v) + 3
                        pe.wait_ge(n_split, (min(n, B * NG) if isinstance(n, int) else n) * 4 - 2)
                        for qb in range(NST):
                            ins = nc.tensor.matmul(psF[:, qb, :], OS[:, v // GU % 2, qb * P:(qb + 1) * P], pick[:, :],
                                                   start=True, stop=True)
                        ins.then_inc(post_done, 1)
                skewed(pe, body)

            @block.scalar
            def _(act):
                act.sem_inc(exp_done, 3)
                act.sem_inc(o_evac, 2)

                def body(i, u, has):
                    if has(LAG_S):
                        v = u - LAG_S
                        w = width(v)
                        act.wait_ge(st_done, i * NU + (v + 1))
                        act.wait_ge(p2_done, i * NU + (v + 1))
                        nc.scalar.activation(PR[:, v % RING, 0:w], psST[:, v % 3, 0:w], ACT.Exp).then_inc(exp_done, 1)
                    if has(LAG_S + 1) and (u - LAG_S - 1) % 3 != 1:
                        v = u - LAG_S - 1
                        w = width(v)
                        act.wait_ge(exp_done, i * NU + (v + 4))
                        act.wait_ge(pv_done, i * NU + (v + 1))
                        nc.scalar.copy(P1[:, v % RING, 0:w], PR[:, v % RING, 0:w]).then_inc(p1_act, 1)
                    if has(LAG_V + 1) and (u - LAG_V - 1) % GU == GU - 1:
                        v = u - LAG_V - 1
                        act.wait_ge(pv_done, i * NU + (v + (1 + RING)))
                        act.wait_ge(post_done, group(i, v) + 1)
                        nc.scalar.copy(OS[:, v // GU % 2, :], psO[:, v // GU % 2, :]).then_inc(o_evac, 1)
                skewed(act, body)

            @block.vector
            def _(dve):
                dve.sem_inc(max_done, 2)
                dve.sem_inc(norm_done, 2)
                dve.sem_inc(post_done, 2)
                dve.wait_ge(b_const, 2)

                def body(i, u, has):
                    if has(0):
                        g, h = u // GU, u % GU // 3
                        dve.wait_ge(s_done, i * NU + (u + 1))
                        for qb, c0 in UNITS[u % 3]:
                            ins = nc.vector.tensor_reduce(NM[:, g % 2, h * NST + qb:h * NST + qb + 1],
                                                          psS[:, u % 2, c0:c0 + (qb + 1) * P], AX.X, ALU.max, negate=True)
                        ins.then_inc(max_done, 1)
                    if has(LAG_S + 1) and (u - LAG_S - 1) % 3 == 1:
                        v = u - LAG_S - 1
                        dve.wait_ge(exp_done, i * NU + (v + 4))
                        dve.wait_ge(pv_done, i * NU + (v + 1))
                        nc.vector.tensor_copy(P1[:, v % RING, :], PR[:, v % RING, :]).then_inc(p1_dve, 1)
                    if has(GU) and (u - GU) % GU in (2, 3):
                        v = u - GU
                        j, n, g = group(i, v), v % GU, v // GU % NG
                        if n == 2:
                            dve.wait_ge(nt_done, j + 1)
                            if has(2 * GU):
                                dve.wait_ge(max_in[(g - 1) % NG], (i + v // NU) * 48 + (48 if g else 0))
                            nc.vector.tensor_scalar(NP[:, 0, :], psN, GAIN, None, ALU.add).then_inc(n_split, 1)
                            dve.wait_ge(n_split, j * 4 + 1)
                            nc.vector.scalar_tensor_tensor(NR[:, :], psN, GAIN, NP[:, 0, :],
                                                           ALU.add, ALU.subtract).then_inc(n_split, 1)
                        else:
                            dve.wait_ge(n_split, j * 4 + 2)
                            nc.vector.tensor_copy(NP[:, 1, :], NR[:, :]).then_inc(n_split, 1)
                            dve.wait_ge(n_split, j * 4 + 3)
                            nc.vector.tensor_tensor(NP[:, 2, :], NR[:, :], NP[:, 1, :], ALU.subtract).then_inc(n_split, 1)
                    if has(GU) and (u - GU) % GU in (4, 5, 6, 7):
                        v = u - GU
                        j, n, g = group(i, v), v % GU - 4, v // GU % 2
                        rest = VR[:, :, :].rearrange("p k (h e) -> p k h e", e=HD)
                        part = [VG_heads[:, g, :, :, t * HD:(t + 1) * HD] for t in range(3)]
                        if n == 0:
                            if has(2 * GU):
                                dve.wait_ge(pv_done, i * NU + (v // GU * GU - GU + RING))
                            src = V_all[:, bass.ds(j, 1)].rearrange("p a k (h e) -> p (a k) h e", e=HD)
                            nc.vector.tensor_copy(part[0], src).then_inc(v_split, 1)
                        elif n == 1:
                            dve.wait_ge(v_split, j * 4 + 1)
                            src = V_all[:, bass.ds(j, 1)].rearrange("p a k (h e) -> p (a k) h e", e=HD)
                            nc.vector.tensor_tensor(rest, src, part[0], ALU.subtract).then_inc(v_split, 1)
                        elif n == 2:
                            dve.wait_ge(v_split, j * 4 + 2)
                            nc.vector.tensor_copy(part[1], rest).then_inc(v_split, 1)
                        else:
                            dve.wait_ge(v_split, j * 4 + 3)
                            nc.vector.tensor_tensor(part[2], rest, part[1], ALU.subtract).then_inc(v_split, 1)
                    if has(LAG_NORM) and (u - LAG_NORM) % GU == GU - 1:
                        v = u - LAG_NORM
                        j, g = group(i, v), v // GU % 2
                        heads = psF.rearrange("p q (h x) -> p (q h) x", x=HD + 1)
                        dve.wait_ge(post_done, j + 3)
                        nc.vector.reciprocal(RI[:, g], heads[:, :, HD:HD + 1].rearrange("p n a -> p (n a)")).then_inc(b_dve, 1)
                        dve.wait_ge(b_dve, j + 1)
                        nc.vector.tensor_tensor(
                            O_all[:, bass.ds(j, 1)].rearrange("p a q (h e) -> p (a q h) e", e=HD), heads[:, :, 0:HD],
                            RI[:, g].unsqueeze(2).to_broadcast([P, NST * HG, HD]), ALU.mult).then_inc(norm_done, 1)
                skewed(dve, body)
        pb.close()

        pc = ExitStack()
        q1T, k1T, v1T = (BIG[:, n, :].rearrange("p (t s) -> p t s", t=B) for n in range(3))
        WC = sb(pc, "WC", [P, 4, D])
        rw = sb(pc, "rw", [P, NE])
        bc1 = sb(pc, "bc1", [P, 4])
        ab_row = sb(pc, "ab_row", [P, D])
        CU = C2[:, :].rearrange("p (n d) -> p n d", n=NST)
        OST, HS = sb(pc, "OST", [P, 4, D]), sb(pc, "HS", [P, 4, D])
        c_in, cu_ps, cu_sb = sem("c_in"), sem("cu_ps"), sem("cu_sb")
        ost_ready, oT_ps, oT_sb, y_ps, x1_ready, hs_pre, hs_ready, xs_ready, xT_ps, xT_sb = (sem(n) for n in (
            "ost_ready", "oT_ps", "oT_sb", "y_ps", "x1_ready", "hs_pre", "hs_ready", "xs_ready", "xT_ps", "xT_sb"))
        q1_ps, r_ps, q1_sb, v1_sb, log_sb, xs_copied, c_dve, c_pool, c_act = (sem(n) for n in (
            "q1_ps", "r_ps", "q1_sb", "v1_sb", "log_sb", "xs_copied", "c_dve", "c_pool", "c_act"))
        psA, psB = ps(pc, "psA", [P, 4, D]), ps(pc, "psB", [P, 4, D])
        psA2 = ps(pc, "psA2", [P, 4, D])
        psQ1 = ps(pc, "psQ1", [P, 3, S])
        psR = ps(pc, "psR", [P, 4, NE])
        psCU = ps(pc, "psCU", [P, NST, D])
        OT = sb(pc, "OT", [P, S])
        XS, XT = HS, OT

        with nc.Block() as block:
            @block.sync
            def _(sp):
                sp.dma_start(WC[:, 0, :], a["attn_wo"]).then_inc(c_in, 16)
                sp.dma_start(WC[:, 1:4, :], a["in_proj"].rearrange("p (n d) -> p n d", n=3)).then_inc(c_in, 16)
                sp.dma_start(rw[:, :], a["router"]).then_inc(c_in, 16)
                sp.dma_start(bc1[:, 0:3], a["in_bias"]).then_inc(c_in, 16)
                sp.dma_start(ab_row[:, :], a["attn_bo"].to_broadcast([P, D])).then_inc(c_in, 16)

            @block.gpsimd
            def _(pool):
                pool.wait_ge(c_in, 80)
                with pool.Fori(0, B) as b:
                    wait_apart(pool, oT_ps, b + 1)
                    for g in range(NG):
                        ins = nc.gpsimd.tensor_copy(OST[:, :, g * GW:(g + 1) * GW],
                                                    O_all[:, bass.ds(b * NG + g, 1)].rearrange("p a q c -> p (a q) c"))
                    ins.then_inc(ost_ready, 1)
                    nc.gpsimd.tensor_tensor(b_tiles(X, b), b_tiles(X, b),
                                            ab_row[:, :].unsqueeze(1).to_broadcast([P, NST, D]), ALU.add).then_inc(c_pool, 1)
                    power(pool, b + B)
                    wait_apart(pool, xs_ready, b + 1)
                    nc.gpsimd.tensor_copy(b_tiles(HX, b), XS[:, :, :]).then_inc(xs_copied, 1)

            @block.tensor
            def _(pe):
                pe.wait_ge(c_in, 80)
                for t in range(NST):
                    ins = nc.tensor.matmul(psCU[:, t, :], C2[:, t * P:(t + 1) * P], uo_h[:, :], start=True, stop=True)
                ins.then_inc(cu_ps, 1)
                pe.sem_inc(oT_ps, 1)
                with pe.Fori(0, B) as b:
                    pe.wait_ge(ost_ready, b + 1)
                    for t in range(4):
                        ins = nc.tensor.transpose(psA[:, t, :], OST[:, t, :], ident[:, :])
                    ins.then_inc(oT_ps, 1)
                    pe.wait_ge(oT_sb, b + 1)
                    pe.wait_ge(x1_ready, b + 1)
                    for t in range(4):
                        ins = nc.tensor.matmul(psB[:, t, :], OT[:, t * P:(t + 1) * P], WC[:, 0, :], start=True, stop=True)
                    ins.then_inc(y_ps, 1)
                    pe.wait_ge(xs_ready, b + 1)
                    for t in range(4):
                        ins = nc.tensor.transpose(psA2[:, t, :], XS[:, t, :], ident[:, :])
                    ins.then_inc(xT_ps, 1)
                    pe.wait_ge(xT_sb, b + 1)
                    pe.wait_ge(log_sb, b + 1)
                    for t in range(4):
                        ins = nc.tensor.matmul(psR[:, t, :], XT[:, t * P:(t + 1) * P], rw[:, :], start=True, stop=True)
                    ins.then_inc(r_ps, 1)
                    pe.wait_ge(q1_sb, b * 2 + 2)
                    pe.wait_ge(v1_sb, b + 1)
                    for n in range(3):
                        nc.tensor.matmul(psQ1[:, n, :], WC[:, 1 + n, :], XT[:, :], start=True, stop=True).then_inc(q1_ps, 1)

            @block.scalar
            def _(act):
                act.sem_inc(q1_sb, 2)
                act.wait_ge(c_in, 80)
                nc.scalar.mul(bc1[:, 3:4], bc1[:, 0:1], SCALE).then_inc(c_act, 1)
                act.wait_ge(c_act, 1)
                with act.Fori(0, B) as b:
                    act.wait_ge(oT_ps, b + 2)
                    act.wait_ge(q1_ps, b * 3 + 3)
                    nc.scalar.copy(OT[:, :], psA[:, :, :].rearrange("p t d -> p (t d)")).then_inc(oT_sb, 1)
                    act.wait_ge(hs_pre, b + 1)
                    nc.scalar.activation(HS[:, :, :], HS[:, :, :], ACT.Tanh).then_inc(hs_ready, 1)
                    act.wait_ge(xT_ps, b + 1)
                    nc.scalar.copy(XT[:, :], psA2[:, :, :].rearrange("p t d -> p (t d)")).then_inc(xT_sb, 1)
                    act.wait_ge(q1_ps, b * 3 + 4)
                    nc.scalar.activation(q1T[:, bass.ds(b, 1), :].rearrange("p a s -> p (a s)"), psQ1[:, 0, :],
                                         ACT.Identity, bias=bc1[:, 3:4], scale=SCALE).then_inc(q1_sb, 1)
                    act.wait_ge(q1_ps, b * 3 + 5)
                    nc.scalar.activation(k1T[:, bass.ds(b, 1), :].rearrange("p a s -> p (a s)"), psQ1[:, 1, :],
                                         ACT.Identity, bias=bc1[:, 1:2]).then_inc(q1_sb, 1)

            @block.vector
            def _(dve):
                link, at, count = linker(dve, c_dve)
                dve.sem_inc(x1_ready, 1)
                dve.sem_inc(log_sb, 1)
                dve.sem_inc(v1_sb, 1)
                dve.sem_inc(q1_ps, 3)
                dve.wait_ge(c_in, 80)
                dve.wait_ge(cu_ps, 1)
                link(nc.vector.tensor_copy(CU[:, :, :], psCU[:, :, :]))
                per = 4
                with dve.Fori(0, B) as b:
                    at(b * per + 1)
                    nc.vector.tensor_tensor(HS[:, :, :], b_tiles(HX, b), CU[:, :, :], ALU.add).then_inc(hs_pre, 1)
                    dve.wait_ge(c_pool, b + 1)
                    dve.wait_ge(y_ps, b + 1)
                    link(nc.vector.tensor_tensor(b_tiles(X, b), psB[:, :, :], b_tiles(X, b), ALU.add))
                    dve.wait_ge(hs_ready, b + 1)
                    link(nc.vector.tensor_tensor(b_tiles(X, b), b_tiles(X, b), HS[:, :, :], ALU.add))
                    dve.sem_inc(x1_ready, 1)
                    layer_norm(nc, link, stats, mv, rstd, var_ready, lambda: dve.wait_ge(rstd_ready, b + (B + 1)),
                               lambda t: b_tiles(X, b)[:, t, :], lambda t: XS[:, t, :]).then_inc(xs_ready, 1)
                    dve.wait_ge(r_ps, b + 1)
                    nc.vector.tensor_copy(LOG[:, bass.ds(b * NST, NST), :], psR[:, :, :]).then_inc(log_sb, 1)
                    dve.wait_ge(q1_ps, b * 3 + 6)
                    nc.vector.tensor_scalar(v1T[:, bass.ds(b, 1), :].rearrange("p a s -> p (a s)"), psQ1[:, 2, :],
                                            bc1[:, 2:3], None, ALU.add).then_inc(v1_sb, 1)
                    dve.wait_ge(xs_copied, b + 1)
                    assert count() == per
        pc.close()
        attn_space.close()

        pr = ExitStack()

        def rsb(shape, dt=F32):
            rsb.n += 1
            return sb(pr, f"r{rsb.n}", shape, dt)[:]
        rsb.n = 0
        OH, ET = rsb([P, NTILE, NE]), rsb([P, NTILE, NE])
        TOT, INC = rsb([P, NE, NTILE]), rsb([P, NE, NTILE])
        ones64, iota64 = rsb([P, NTILE]), rsb([P, NTILE])
        mxl, idx, posf = rsb([P, NTILE]), rsb([P, NTILE]), rsb([P, NTILE])
        iota8 = rsb([P, NE])
        nblk, incb, baseb = rsb([P, NE]), rsb([P, NE]), rsb([P, NE])
        onesm, before = rsb([P, P]), rsb([P, P])
        iotab, ebf, ebc = rsb([P, NBLK]), rsb([P, NBLK]), rsb([P, NBLK, NE])
        psRT = ps(pr, "psRT", [P, 2, NTILE * NE])
        psRank, psTot = (psRT[:, n, :].rearrange("p (j e) -> p j e", e=NE) for n in range(2))
        e_const, e_oh, e_rank, pos_ready, scattered, e_dve = (sem(n) for n in (
            "e_const", "e_oh", "e_rank", "pos_ready", "scattered", "e_dve"))

        with nc.Block() as block:
            @block.sync
            def _(sp):
                sp.dma_start(onesm, a["ones"]).then_inc(e_const, 16)
                sp.dma_start(before, a["before"]).then_inc(e_const, 16)
                sp.dma_start(iota8, a["iota8"].to_broadcast([P, NE])).then_inc(e_const, 16)
                sp.dma_start(iota64, a["iota64"].to_broadcast([P, NTILE])).then_inc(e_const, 16)
                sp.dma_start(iotab, a["iotab"].to_broadcast([P, NBLK])).then_inc(e_const, 16)

            @block.vector
            def _(dve):
                link, at, count = linker(dve, e_dve)
                link(nc.vector.memset(ones64, 1.0))
                dve.wait_ge(e_const, 80)
                link(nc.vector.tensor_reduce(mxl, LOG[:, :, :], AX.X, ALU.max))
                link(nc.vector.tensor_tensor(ET, LOG[:, :, :], mxl.unsqueeze(2).to_broadcast([P, NTILE, NE]), ALU.is_equal))
                io = iota8.unsqueeze(1).to_broadcast([P, NTILE, NE])
                link(nc.vector.tensor_tensor(ET, ET, io, ALU.mult))
                link(nc.vector.tensor_reduce(idx, ET, AX.X, ALU.min))
                nc.vector.tensor_tensor(OH, idx.unsqueeze(2).to_broadcast([P, NTILE, NE]), io, ALU.is_equal).then_inc(e_oh, 1)
                dve.wait_ge(e_rank, 1)
                link(nc.vector.tensor_copy(TOT, psTot.rearrange("p j e -> p e j")))
                for e in range(NE):
                    ins = nc.vector.tensor_tensor_scan(INC[:, e, :], ones64, TOT[:, e, :], 0.0, ALU.mult, ALU.add)
                link(ins)
                for e in range(NE):
                    ins = nc.vector.tensor_scalar(ET.rearrange("p j e -> p (j e)")[:, e * NTILE:(e + 1) * NTILE], iota64,
                                                  INC[:, e, NTILE - 1:NTILE], None, ALU.is_lt)
                link(ins)
                link(nc.vector.tensor_reduce(nblk, ET.rearrange("p j e -> p (j e)").rearrange("p (e n) -> p e n", e=NE),
                                             AX.X, ALU.add))
                link(nc.vector.tensor_tensor_scan(incb, ones64[:, 0:NE], nblk, 0.0, ALU.mult, ALU.add))
                link(nc.vector.tensor_tensor(baseb, incb, nblk, ALU.subtract))
                link(nc.vector.tensor_scalar(baseb, baseb, float(P), None, ALU.mult))
                link(nc.vector.tensor_tensor(INC, INC, TOT, ALU.subtract))
                link(nc.vector.tensor_tensor(INC, INC, baseb.unsqueeze(2).to_broadcast([P, NE, NTILE]), ALU.add))
                link(nc.vector.tensor_tensor(ET, psRank, INC.rearrange("p e j -> p j e"), ALU.add))
                link(nc.vector.tensor_tensor(ET, ET, OH, ALU.mult))
                link(nc.vector.tensor_reduce(posf, ET, AX.X, ALU.add))
                link(nc.vector.tensor_copy(pos[:, :], posf))
                link(nc.vector.tensor_tensor(ebc, incb.unsqueeze(1).to_broadcast([P, NBLK, NE]),
                                             iotab.unsqueeze(2).to_broadcast([P, NBLK, NE]), ALU.is_le))
                link(nc.vector.tensor_reduce(ebf, ebc, AX.X, ALU.add))
                link(nc.vector.tensor_scalar(ebf, ebf, float(NE - 1), None, ALU.min))
                nc.vector.tensor_copy(eb[0:1, :], ebf[0:1, :]).then_inc(pos_ready, 1)

            @block.tensor
            def _(pe):
                pe.wait_ge(e_const, 80)
                pe.wait_ge(e_oh, 1)
                oh = OH.rearrange("p j e -> p (j e)")
                nc.tensor.matmul(psRT[:, 0, :], before, oh, start=True, stop=True)
                nc.tensor.matmul(psRT[:, 1, :], onesm, oh, start=True, stop=True).then_inc(e_rank, 1)

            @block.gpsimd
            def _(pool):
                pool.wait_ge(pos_ready, 1)
                for b in range(B):
                    for st in range(NST):
                        j = b * NST + st
                        pool.indirect_dma_start(sorted_x, bass.IndirectOffsetOnAxis(pos[:, j:j + 1], 0),
                                                HX[:, b, st, :], None).then_inc(scattered, 16)
                pool.wait_ge(scattered, 16 * NTILE)
        pr.close()

        pd = ExitStack()
        relk = sb(pd, "relk", [P, NREL, NH])
        relv = sb(pd, "relv", [P, NREL, NH])
        relrow = sb(pd, "relrow", [P, 2, NREL])
        sel = sb(pd, "sel", [P, NH])
        wout = sb(pd, "wout", [P, D])
        ones_row = sb(pd, "ones_row", [1, P])
        bout_row = sb(pd, "bout_row", [1, D])
        RW = sb(pd, "RW", [P, NWIN * D])
        QD = sb(pd, "QD", [P, 4, P])
        hx = HX[:, :, :, :].rearrange("p a n d -> p (a n) d")
        PROD = hx[:, 0:2 * B, :].rearrange("p (a t) s -> p a t s", a=2)
        PV = hx[:, 2 * B:3 * B, :]
        PD = hx[:, 3 * B:4 * B, :].rearrange("p (a t) x -> p a t x", a=2)
        EP = sb(pd, "EP", [P, 2, 2, B, NH])
        MX = sb(pd, "MX", [P, 2, 2, 2, NH])
        OD = sb(pd, "OD", [P, 2, P])
        PTS = sb(pd, "PTS", [P, 2, 2, 2, P])
        psS1 = ps(pd, "psS1", [P, 2, 2, B * NH])
        psX = ps(pd, "psX", [P, 2, 2, 4, P])
        psT1 = ps(pd, "psT1", [P, 2, 2, P])
        psO1 = ps(pd, "psO1", [P, 4, P])
        d_in, d_const, rw_ps, rw_sb = sem("d_in"), sem("d_const"), sem("rw_ps"), sem("rw_sb")
        qd_sb, prod_ready, s1_done, e_ready, p_exp, p_ready = (sem(n) for n in (
            "qd_sb", "prod_ready", "s1_done", "e_ready", "p_exp", "p_ready"))
        t1_ps, t1_sb, px_ps, pv_sb, od_ready, o1_ps, x2_done = (sem(n) for n in (
            "t1_ps", "t1_sb", "px_ps", "pv_sb", "od_ready", "o1_ps", "x2_done"))
        d_dve, z_ready, pd_sb = sem("d_dve"), sem("z_ready"), sem("pd_sb")
        NSTEP = NST * B // 4

        with nc.Block() as block:
            @block.sync
            def _(sp):
                for n, name in enumerate(("relk", "relv")):
                    for h in range(NH):
                        sp.dma_start(relrow[h * HD:(h + 1) * HD, n, :], a[name]).then_inc(d_in, 16)
                sp.dma_start(sel[:, :], a["sel"]).then_inc(d_in, 16)
                sp.dma_start(wout[:, :], a["out_w"]).then_inc(d_in, 16)
                sp.dma_start(bout_row[:, :], a["out_b"]).then_inc(d_in, 16)
            NDI = 16 * (2 * NH + 3)

            def steps(eng, body):
                with eng.Fori(0, NST) as st:
                    with eng.Fori(0, B // 4) as q4:
                        body(st, q4, st * 4 + q4)

            def s_cols(t, st):
                return t[:, :, bass.ds(st * P, P)]

            @block.gpsimd
            def _(pool):
                nc.gpsimd.memset(ones_row[:, :], 1.0)
                pool.wait_ge(d_in, NDI)
                for n, rel in enumerate((relk, relv)):
                    ins = nc.gpsimd.tensor_tensor(rel[:, :, :], relrow[:, n, :].unsqueeze(2).to_broadcast([P, NREL, NH]),
                                                  sel[:, :].unsqueeze(1).to_broadcast([P, NREL, NH]), ALU.mult)
                ins.then_inc(d_const, 1)
                pool.sem_inc(s1_done, 2)

                def body(st, q4, i):
                    for n in range(4):
                        pool.wait_ge(s1_done, i * 4 + (n + 1))
                        q = q1T[:, bass.ds(q4 * 4 + n, 1), bass.ds(st * P, P)]
                        nc.gpsimd.tensor_tensor(PROD[:, n % 2], s_cols(k1T, st), q.to_broadcast([P, B, P]), ALU.mult)\
                            .then_inc(prod_ready, 1)
                    for pair in range(2):
                        pool.wait_ge(z_ready, i * 2 + (pair + 1))
                        for m in range(2):
                            ins = nc.gpsimd.tensor_tensor(EP[:, pair, m], EP[:, pair, m],
                                                          MX[:, pair, 1, m, :].unsqueeze(1).to_broadcast([P, B, NH]),
                                                          ALU.mult)
                        ins.then_inc(p_ready, 1)
                steps(pool, body)

            @block.tensor
            def _(pe):
                pe.wait_ge(d_const, 1)
                for w in range(NWIN):
                    if w >= 16 and w % 4 == 0:
                        pe.wait_ge(rw_sb, w // 4 - 3)
                    ins = nc.tensor.matmul(psX[:, w // 8 % 2, w // 4 % 2, w % 4, :],
                                           relv[:, 1 + w:1 + w + HD, :].rearrange("p r h -> p (r h)"), wout[:, :],
                                           start=True, stop=True)
                    if w % 4 == 3:
                        ins.then_inc(rw_ps, 1)
                pe.wait_ge(rw_sb, NWIN // 4)
                pe.sem_inc(px_ps, 2)

                def body(st, q4, i):
                    for n in range(4):
                        pair, m = n // 2, n % 2
                        pe.wait_ge(qd_sb, i * 4 + (n + 1))
                        wait_apart(pe, e_ready, i * 2 + (pair + 1))
                        nc.tensor.matmul(psS1[:, pair, m, :], QD[:, n, :],
                                         relk[:, bass.ds(MAXREL - n - q4 * 4, B), :].rearrange("p r h -> p (r h)"),
                                         start=True, stop=False)
                        pe.wait_ge(prod_ready, i * 4 + (n + 1))
                        for t in range(B):
                            ins = nc.tensor.matmul(psS1[:, pair, m, t * NH:(t + 1) * NH], PROD[:, n % 2, t, :], sel[:, :],
                                                   start=False, stop=(t == B - 1))
                        ins.then_inc(s1_done, 1)
                    for n in range(4):
                        pair, m = n // 2, n % 2
                        if m == 0:
                            pe.wait_ge(p_ready, i * 2 + (pair + 1))
                            pe.wait_ge(t1_sb, i * 2 + (pair + 1))
                            for mm in range(2):
                                for c in range(2):
                                    ins = nc.tensor.transpose(
                                        psT1[:, mm, c, :],
                                        EP[:, pair, mm, c * HD:(c + 1) * HD, :].rearrange("p t h -> p (t h)"), ident[:, :])
                            ins.then_inc(t1_ps, 1)
                        for half in range(2):
                            pe.wait_ge(pv_sb, i * 8 + (n * 2 + half + 1))
                            pe.wait_ge(pd_sb, i * 8 + (n * 2 + half + 1))
                            for t in range(8):
                                ins = nc.tensor.transpose(psX[:, half, t // 4, t % 4, :], PD[:, half, t, :], ident[:, :])
                            ins.then_inc(px_ps, 1)
                        if m == 1:
                            pe.wait_ge(t1_sb, i * 2 + (pair + 2))
                            if pair == 0:
                                pe.wait_ge(x2_done, i + 1)
                            for mm in range(2):
                                q = pair * 2 + mm
                                pe.wait_ge(od_ready, i * 4 + (q + 1))
                                nc.tensor.matmul(psO1[:, q, :], OD[:, mm, :], wout[:, :], start=True, stop=False)
                                for c in range(2):
                                    nc.tensor.matmul(psO1[:, q, :], PTS[:, pair, mm, c, :],
                                                     RW[:, bass.ds((8 * c + 15 - q - q4 * 4) * D, D)], start=False, stop=False)
                                ins = nc.tensor.matmul(psO1[:, q, :], ones_row[:, :], bout_row[:, :], start=False, stop=True)
                            ins.then_inc(o1_ps, 1)
                steps(pe, body)

            @block.scalar
            def _(act):
                for r in range(NWIN // 4):
                    act.wait_ge(rw_ps, r + 1)
                    nc.scalar.copy(RW[:, r * 4 * D:(r * 4 + 4) * D],
                                   psX[:, r // 2 % 2, r % 2, :, :].rearrange("p a b -> p (a b)")).then_inc(rw_sb, 1)
                act.sem_inc(t1_sb, 1)

                def body(st, q4, i):
                    for n in range(4):
                        if n == 0:
                            act.wait_ge(s1_done, i * 4 + 2)
                        q = q1T[:, bass.ds(q4 * 4 + n, 1), bass.ds(st * P, P)].rearrange("p a s -> p (a s)")
                        nc.scalar.copy(QD[:, n, :], q).then_inc(qd_sb, 1)
                    for pair in range(2):
                        act.wait_ge(e_ready, i * 2 + (pair + 3))
                        ep = EP[:, pair].rearrange("p m t h -> p (m t h)")
                        nc.scalar.activation(ep, ep, ACT.Exp).then_inc(p_exp, 1)
                    for pair in range(2):
                        act.wait_ge(t1_ps, i * 2 + (pair + 1))
                        act.wait_ge(x2_done, i + 1)
                        nc.scalar.copy(PTS[:, pair].rearrange("p m c s -> p (m c s)"),
                                       psT1[:, :, :, :].rearrange("p m c s -> p (m c s)")).then_inc(t1_sb, 1)
                        for m in range(2):
                            for half in range(2):
                                act.wait_ge(px_ps, i * 8 + (pair * 4 + m * 2 + half + 1))
                                nc.scalar.copy(PD[:, half].rearrange("p t (h e) -> p (t h) e", e=HD),
                                               EP[:, pair, m, half * 8:half * 8 + 8, :].rearrange("p t h -> p (t h)")
                                               .unsqueeze(2).to_broadcast([P, 8 * NH, HD])).then_inc(pd_sb, 1)
                steps(act, body)

            @block.vector
            def _(dve):
                link, at, count = linker(dve, d_dve)
                dve.sem_inc(e_ready, 2)
                dve.sem_inc(pv_sb, 2)
                dve.sem_inc(x2_done, 1)
                per = 2 + 2 + 4

                def body(st, q4, i):
                    at(i * per)
                    for pair in range(2):
                        dve.wait_ge(s1_done, i * 4 + (2 * pair + 4))
                        sc = psS1[:, pair].rearrange("p m (t h) -> p m h t", h=NH)
                        link(nc.vector.tensor_reduce(MX[:, pair, 0], sc, AX.X, ALU.max))
                        for m in range(2):
                            ins = nc.vector.tensor_tensor(
                                EP[:, pair, m], psS1[:, pair, m].rearrange("p (t h) -> p t h", h=NH),
                                MX[:, pair, 0, m, :].unsqueeze(1).to_broadcast([P, B, NH]), ALU.subtract)
                        ins.then_inc(e_ready, 1)
                    for pair in range(2):
                        dve.wait_ge(p_exp, i * 2 + (pair + 1))
                        link(nc.vector.tensor_reduce(MX[:, pair, 0], EP[:, pair].rearrange("p m t h -> p m h t"),
                                                     AX.X, ALU.add))
                        nc.vector.reciprocal(MX[:, pair, 1], MX[:, pair, 0]).then_inc(z_ready, 1)
                    for n in range(4):
                        for half in range(2):
                            dve.wait_ge(px_ps, i * 8 + (n * 2 + half + 3))
                            ins = nc.vector.tensor_tensor(
                                PV[:, half * 8:half * 8 + 8, :], psX[:, half].rearrange("p a b s -> p (a b) s"),
                                v1T[:, half * 8:half * 8 + 8, bass.ds(st * P, P)], ALU.mult)
                            ins.then_inc(pv_sb, 1)
                        dve.wait_ge(pv_sb, i * 8 + (n * 2 + 4))
                        if n == 2:
                            dve.wait_ge(o1_ps, i * 2 + 1)
                        link(nc.vector.tensor_reduce(OD[:, n % 2, :], PV[:, :, :].rearrange("p t s -> p s t"),
                                                     AX.X, ALU.add))
                        dve.sem_inc(od_ready, 1)
                    dve.wait_ge(o1_ps, i * 2 + 2)
                    xv = X[:, bass.ds(q4 * 4, 4), bass.ds(st, 1), :].rearrange("p t a d -> p t (a d)")
                    nc.vector.tensor_tensor(xv, psO1[:, :, :], xv, ALU.add).then_inc(x2_done, 1)
                    assert count() == per
                steps(dve, body)
        pd.close()

        pe_ = ExitStack()
        carved[0] = 0
        GUW = carve([P, NE, 2 * FI])
        DW = carve([P, NE, len(FC), D])
        GUWf, DWf = GUW.rearrange("p e f -> p (e f)"), DW.rearrange("p e c d -> p (e c d)")
        XB, XBT = carve([P, 2, P]), carve([P, 2, P])
        TH, HH = carve([P, 2, FI]), carve([P, 2, FI])
        HT, YB = carve([P, 2, 3 * P]), carve([P, 2, D])
        psGU = ps(pe_, "psGU", [P, 2, 2, S])
        psXB = ps(pe_, "psXB", [P, S])
        psHT = ps(pe_, "psHT", [P, 3, P])
        psY = ps(pe_, "psY", [P, 2, S])
        ew_in = sem("ew_in")
        xb_in = [sem("xb_in0"), sem("xb_in1")]
        y2_out = [sem("y2_out0"), sem("y2_out1")]
        e_silu = sem("e_silu")
        xb_ps, xb_sb, gu_ps, th_sb, hh_sb, ht_ps, ht_sb, y2_ps, y2_sb = (sem(n) for n in (
            "xb_ps", "xb_sb", "gu_ps", "th_sb", "hh_sb", "ht_ps", "ht_sb", "y2_ps", "y2_sb"))
        a_add, out_done = sem("a_add"), sem("out_done")
        gathered = [sem(f"gathered{b}") for b in range(B)]

        def blocks_behind(eng, first, second):
            first(0, 0)
            with eng.Fori(0, NBLK // 2 - 1) as i:
                for s in range(2):
                    first(i * 2 + (s + 1), 1 - s)
                    second(i * 2 + s, s, i)
            first(NBLK - 1, 1)
            second(NBLK - 2, 0, NBLK // 2 - 1)
            second(NBLK - 1, 1, NBLK // 2 - 1)

        with nc.Block() as block:
            @block.sync
            def _(sp):
                sp.dma_start(GUW, a["gate_up"].rearrange("p (e f) -> p e f", e=NE)).then_inc(ew_in, 16)
                for c, w in enumerate(FC):
                    sp.dma_start(DW[0:w, :, c, :], a["down"][c * P:c * P + w, :].rearrange("p (e d) -> p e d", e=NE))\
                      .then_inc(ew_in, 16)
                sp.sem_inc(xb_ps, 2)
                sp.sem_inc(y2_out[0], 16)
                sp.sem_inc(y2_out[1], 16)

                def load(n, s):
                    sp.wait_ge(xb_ps, n + 1)
                    sp.dma_start(XB[:, s, :], sorted_x[bass.ds(n * P, P), :]).then_inc(xb_in[s], 16)

                def store(n, s):
                    sp.wait_ge(y2_sb, n + 3)
                    sp.dma_start(sorted_y[bass.ds(n * P, P), :], YB[:, s, :]).then_inc(y2_out[s], 16)
                for n in range(3):
                    load(n, n % 2)
                with sp.Fori(0, NBLK // 2 - 2) as i:
                    for s in range(2):
                        load(i * 2 + (s + 3), 1 - s)
                        store(i * 2 + s, s)
                load(NBLK - 1, 1)
                for n in range(NBLK - 4, NBLK):
                    store(n, n % 2)
                for b in range(B):
                    sp.wait_ge(a_add, b + 1)
                    sp.dma_start(out[b].rearrange("(n p) d -> p n d", p=P), X[:, b]).then_inc(out_done, 16)
                sp.wait_ge(out_done, 16 * B)

            @block.vector
            def _(dve):
                def first(n, s):
                    dve.wait_ge(th_sb, n + 1)
                    nc.vector.scalar_tensor_tensor(TH[:, s, :], TH[:, s, :], 1.0, psGU[:, s, 0, 0:FI],
                                                   ALU.add, ALU.mult).then_inc(e_silu, 1)
                    dve.wait_ge(e_silu, n + 1)
                    nc.vector.scalar_tensor_tensor(HH[:, s, :], TH[:, s, :], 0.5, psGU[:, s, 1, 0:FI],
                                                   ALU.mult, ALU.mult).then_inc(hh_sb, 1)

                def second(n, s, i):
                    dve.wait_ge(y2_ps, n + 1)
                    dve.wait_ge(y2_out[s], i * 16 + 16)
                    nc.vector.tensor_copy(YB[:, s, :], psY[:, s, 0:D]).then_inc(y2_sb, 1)
                dve.sem_inc(y2_sb, 2)
                blocks_behind(dve, first, second)
                for b in range(B):
                    dve.wait_ge(gathered[b], 16 * NST)
                    nc.vector.tensor_tensor(X[:, b], X[:, b], HX[:, b], ALU.add).then_inc(a_add, 1)

            @block.scalar
            def _(act):
                def first(n, s):
                    act.wait_ge(xb_ps, n + 3)
                    nc.scalar.copy(XBT[:, s, :], psXB[:, 0:P]).then_inc(xb_sb, 1)
                    act.wait_ge(gu_ps, n + 1)
                    nc.scalar.activation(TH[:, s, :], psGU[:, s, 0, 0:FI], ACT.Tanh, scale=0.5).then_inc(th_sb, 1)

                def second(n, s, i):
                    act.wait_ge(ht_ps, n + 1)
                    nc.scalar.copy(HT[:, s, 0:2 * P], psHT[:, 0:2, :].rearrange("p c s -> p (c s)"))
                    nc.scalar.copy(HT[0:FC[2], s, 2 * P:3 * P], psHT[0:FC[2], 2, :]).then_inc(ht_sb, 1)
                blocks_behind(act, first, second)

            @block.tensor
            def _(pe):
                pe.wait_ge(ew_in, 64)

                def expert(n):
                    return pe.value_load(eb[0:1, bass.ds(n, 1)], min_val=0, max_val=NE - 1)

                def first(n, s):
                    pe.wait_ge(xb_in[s], n * 8 + (16 if s == 0 else 8))
                    nc.tensor.transpose(psXB[:, 0:P], XB[:, s, :], ident[:, :]).then_inc(xb_ps, 1)
                    wait_apart(pe, xb_sb, n + 1)
                    e = expert(n)
                    for c in range(2):
                        ins = nc.tensor.matmul(psGU[:, s, c, 0:FI], XBT[:, s, :], GUWf[:, bass.ds(e * (2 * FI) + c * FI, FI)],
                                               start=True, stop=True)
                    ins.then_inc(gu_ps, 1)

                def second(n, s, i):
                    pe.wait_ge(hh_sb, n + 1)
                    for c, w in enumerate(FC):
                        ins = nc.tensor.transpose(psHT[0:w, c, :], HH[:, s, c * P:c * P + w], ident[:, :])
                    ins.then_inc(ht_ps, 1)
                    pe.wait_ge(ht_sb, n + 1)
                    wait_apart(pe, y2_sb, n + 1)
                    e = expert(n)
                    for c, w in enumerate(FC):
                        ins = nc.tensor.matmul(psY[:, s, 0:D], HT[0:w, s, c * P:(c + 1) * P],
                                               DWf[0:w, bass.ds(e * (3 * D) + c * D, D)], start=(c == 0), stop=(c == 2))
                    ins.then_inc(y2_ps, 1)
                blocks_behind(pe, first, second)

            @block.gpsimd
            def _(pool):
                for s in range(2):
                    pool.wait_ge(y2_out[s], 16 * (NBLK // 2 + 1))
                for b in range(B):
                    for st in range(NST):
                        j = b * NST + st
                        pool.indirect_dma_start(HX[:, b, st, :], None, sorted_y,
                                                bass.IndirectOffsetOnAxis(pos[:, j:j + 1], 0)).then_inc(gathered[b], 16)
        pe_.close()


def kernel(**inputs):
    import numpy as _np
    import concourse.bacc as _bacc
    from concourse import mybir as _mybir
    from concourse.bass_utils import run_bass_kernel_spmd as _run

    v = {k: _np.asarray(x) for k, x in inputs.items()}

    def heads_inner(w):
        w = _np.moveaxis(w, 0, -2)
        w = w.reshape(w.shape[:-2] + (NG, HG, HD))
        return _np.swapaxes(w, -1, -2).reshape(w.shape[:-3] + (D,))

    eye = _np.eye(P, dtype=_np.float32)
    n = _np.arange(P)
    arrays = {
        "x": v["L0_attn_inputs"],
        "wq": heads_inner(v["L0_attn_W_q"]), "wk": heads_inner(v["L0_attn_W_k"]),
        "wv": v["L0_attn_W_v"].transpose(1, 0, 2).reshape(D, D),
        "bq": heads_inner(v["L0_attn_b_q"]).reshape(D, 1), "bk": heads_inner(v["L0_attn_b_k"]).reshape(D, 1),
        "bv": v["L0_attn_b_v"].reshape(1, D),
        "attn_wo": v["L0_attn_W_o"].T, "attn_bo": v["L0_attn_b_o"].reshape(1, D),
        "in_c": v["L0_ffn_in_c"].reshape(D, 1), "ffn_bo": v["L0_ffn_bo"].reshape(1, D),
        "in_proj": v["L1_attn_in_proj_weight"].T, "in_bias": v["L1_attn_in_proj_bias"].reshape(3, D).T,
        "relk": v["L1_attn_rel_k_table"].T, "relv": v["L1_attn_rel_v_table"].T,
        "out_w": v["L1_attn_out_w"].T, "out_b": v["L1_attn_out_b"].reshape(1, D),
        "router": v["L1_ffn_router_w"].T,
        "gate_up": _np.concatenate([v["L1_ffn_gate_w"], v["L1_ffn_up_w"]], axis=1).transpose(2, 0, 1).reshape(D, NE * 2 * FI),
        "down": v["L1_ffn_down_w"].transpose(2, 0, 1).reshape(FI, NE * D),
        "ident": eye, "ones": _np.ones((P, P), _np.float32),
        "before": (n[:, None] < n[None, :]).astype(_np.float32),
        "mask": _np.where(n[None, :] > n[:, None], NEG, 0.0).astype(_np.float32),
        "sel": (n[:, None] // HD == _np.arange(NH)[None, :]).astype(_np.float32),
        "pick": _np.stack([(n // GW == h) & ((n % GW == 3 * HD) if e == HD else (n % GW < 3 * HD) & (n % HD == e))
                           for h in range(HG) for e in range(HD + 1)], axis=1).astype(_np.float32),
        "iota8": _np.arange(NE, dtype=_np.float32).reshape(1, NE) - NE,
        "iota64": _np.arange(NTILE, dtype=_np.float32).reshape(1, NTILE) * P,
        "iotab": _np.arange(NBLK, dtype=_np.float32).reshape(1, NBLK),
    }
    for w in ("wf", "wi", "wc", "wo", "uf", "ui", "uc", "uo"):
        arrays[w] = v["L0_ffn_" + w].T
    for b in ("bf", "bi", "bc"):
        arrays[b] = v["L0_ffn_" + b].reshape(D, 1)

    nc = _bacc.Bacc("TRN2", target_bir_lowering=False, num_devices=1)
    aps = {}
    arrays = {k: _np.ascontiguousarray(x) for k, x in arrays.items()}
    for k, x in arrays.items():
        aps[k] = nc.dram_tensor(f"in_{k}", x.shape, _mybir.dt.from_np(x.dtype), kind="ExternalInput").ap()
    out = nc.dram_tensor("out", (B, S, D), F32, kind="ExternalOutput").ap()
    program(nc, aps, out)
    r = _run(nc, [{f"in_{k}": x for k, x in arrays.items()}], core_ids=[0])
    return r.results[0]["out"]
```

```python
import math
from contextlib import ExitStack

import numpy as np
import concourse.bass as bass
from concourse import mybir

F32 = mybir.dt.float32
BF16 = mybir.dt.bfloat16
F16 = mybir.dt.float16
I32 = mybir.dt.int32
ALU = mybir.AluOpType
ACT = mybir.ActivationFunctionType
AX = mybir.AxisListType

P = 128
B = 16
S = 512
D = 128
NST = S // P
NH = 16
HD = D // NH
HG = 4
NG = NH // HG
GW = HG * HD
NREL = 33
MAXREL = 16
NE = 8
FI = 352
FC = [128, 128, 96]
NTILE = B * NST
NBLK = NTILE + NE
EPS = 1e-5
SCALE = float(HD) ** -0.5
NEG = -1.0e30
BS = 8
NBT = P // BS
NPAIR = NH // 2
GW1 = 2 * HD
NG1 = NST * NPAIR

UNITS = [[(3, 0)], [(2, 0), (0, 3 * P)], [(1, 0)]]
GU = HG * len(UNITS)
NU = NG * GU
LAG_T = 2
LAG_S = 22
LAG_V = 26
LAG_F = 31
LAG_NORM = 32
RING = 4
GAIN = 10 * math.log(2)


def wait_apart(eng, signal, value):
    eng.wait_ge(signal, value)
    eng.sem_inc(APART[0], 1)


APART = []


def linker(eng, signal):
    state = {"base": 0, "n": 0}

    def link(ins, apart=False):
        state["n"] += 1
        ins.then_inc(signal, 1)
        (wait_apart if apart else type(eng).wait_ge)(eng, signal, state["base"] + state["n"])

    def at(base):
        state["base"], state["n"] = base, 0

    return link, at, lambda: state["n"]


def layer_norm(nc, link, stats, mv, rstd, var_ready, wait_rstd, src, dst):
    for t in range(4):
        ins = nc.vector.bn_stats(stats[:, t, :], src(t))
    link(ins, apart=True)
    for t in range(4):
        ins = nc.vector.bn_aggr(mv[:, t, :], stats[:, t, :])
    link(ins)
    nc.vector.tensor_scalar(rstd[:, 0, :], mv[:, :, 1], EPS, None, ALU.add).then_inc(var_ready, 1)
    wait_rstd()
    for t in range(4):
        ins = nc.vector.tensor_scalar(dst(t), src(t), mv[:, t, 0:1], rstd[:, 1, t:t + 1], ALU.subtract, ALU.mult)
    return ins


def program(nc, a, out):
    with ExitStack() as ctx:
        def sem(name):
            return ctx.enter_context(nc.semaphore(name))

        def sb(where, name, shape, dt=F32):
            return where.enter_context(nc.sbuf_tensor(name, shape, dt))

        def ps(where, name, shape, dt=F32):
            return where.enter_context(nc.psum_tensor(name, shape, dt))

        APART[:] = [sem("apart")]
        q_parts = nc.dram_tensor("q_parts", [B * NG, 3, GW, S], BF16, kind="Internal").ap()
        k_parts = nc.dram_tensor("k_parts", [B * NG, 3, GW, S], BF16, kind="Internal").ap()
        q1_parts = nc.dram_tensor("q1_parts", [NST, 3, D, NBT * P], BF16, kind="Internal").ap()
        k1_parts = nc.dram_tensor("k1_parts", [NST, 3, D, NBT * P], BF16, kind="Internal").ap()
        r1_parts = nc.dram_tensor("r1_parts", [NST, 3, 2, P, NBT * P], BF16, kind="Internal").ap()
        sorted_x = nc.dram_tensor("sorted_x", [NBLK * P, D], F32, kind="Internal").ap()
        sorted_y = nc.dram_tensor("sorted_y", [NBLK * P, D], F32, kind="Internal").ap()

        ident = sb(ctx, "ident", [P, P])
        X = sb(ctx, "X", [P, B, NST, D])
        HX = sb(ctx, "HX", [P, B, NST, D])
        BIG = sb(ctx, "BIG", [P, 3, B * S])
        C2 = sb(ctx, "C2", [P, S])
        uo_h = sb(ctx, "uo_h", [P, D])
        stats = sb(ctx, "stats", [P, 4, 6])
        mv = sb(ctx, "mv", [P, 4, 2])
        rstd = sb(ctx, "rstd", [P, 3, 4])
        LOG = sb(ctx, "LOG", [P, NTILE, NE])
        pos = sb(ctx, "pos", [P, NTILE], I32)
        eb = sb(ctx, "eb", [1, NBLK], I32)
        attn_space = ExitStack()
        O_all = sb(attn_space, "O_all", [P, B * NG, NST, GW])
        V_all = BIG[:, 0, :].rearrange("p (i k c) -> p i k c", i=B * NG, k=NST)

        carved = [B * S]

        def carve(shape, dt=F32):
            n = int(np.prod(shape[1:])) * (1 if dt == F32 else 2) // (1 if dt == F32 else 4)
            at = carved[0]
            carved[0] += n
            assert carved[0] <= 3 * B * S
            v = BIG[:, :, :].rearrange("p a n -> p (a n)")[:, at:at + n]
            if dt != F32:
                v = v.bitcast(dt)
            names = " ".join(f"d{n}" for n in range(len(shape) - 1))
            return v.rearrange(f"p ({names}) -> p {names}", **{f"d{n}": shape[n + 1] for n in range(len(shape) - 2)})

        pa = ExitStack()
        WN = ("wq", "wk", "wv", "wf", "wi", "wc", "wo", "uf", "ui", "uc", "uo")
        W_all = carve([P, len(WN), D])
        W = {n: W_all[:, i, :] for i, n in enumerate(WN)}
        bias_cols = carve([P, 6])
        bias_half = carve([P, 4])
        bv_row, bo_row = carve([P, D]), carve([P, D])
        U2 = carve([P, 3, D])
        XN, XNT = carve([P, 2, 4, D]), carve([P, 2, S])
        QK = carve([P, 2, 2, S])
        RES = carve([P, 2, S])
        PARTS = carve([P, 2, 2, 3, S], BF16)
        TG, CA = carve([P, 3, S]), carve([P, 2, S])
        NZ = 4
        zero = carve([P, NBLK * D // NZ])
        psT = ps(pa, "psT", [P, S])
        psQ = ps(pa, "psQ", [P, 2, S])
        psV, psH = ps(pa, "psV", [P, 4, D]), ps(pa, "psH", [P, 4, D])
        psG = ps(pa, "psG", [P, 3, S])

        weights_in, zeroed, zero_out, halved = (sem(n) for n in ("weights_in", "zeroed", "zero_out", "halved"))
        x_in, parts_stored = [sem("x_in0"), sem("x_in1")], [sem("parts_stored0"), sem("parts_stored1")]
        xn_ready, xnT_ps, xnT_ready = sem("xn_ready"), sem("xnT_ps"), sem("xnT_ready")
        q_ps, k_ps, v_ps, h_ps, g_ps = (sem(n) for n in ("q_ps", "k_ps", "v_ps", "h_ps", "g_ps"))
        qk_sb, v_out, h_out, gates_ready, c_ready, second_ready, parts_ready = (sem(n) for n in (
            "qk_sb", "v_out", "h_out", "gates_ready", "c_ready", "second_ready", "parts_ready"))
        a_dve, a_pool = sem("a_dve"), sem("a_pool")
        var_ready, rstd_ready = sem("var_ready"), sem("rstd_ready")

        def power(eng, n):
            eng.wait_ge(var_ready, n + 1)
            nc.gpsimd.tensor_tensor(rstd[:, 1, :], rstd[:, 0, :], rstd[:, 2, :], ALU.pow).then_inc(rstd_ready, 1)
        NWA = 5

        def two_steps(eng, body):
            with eng.Fori(0, B // 2 - 1) as i:
                body(i * 2, 0, False)
                body(i * 2 + 1, 1, False)
            body(B - 2, 0, False)
            body(B - 1, 1, True)

        def b_tiles(t, b):
            return t[:, bass.ds(b, 1)].rearrange("p a n d -> p (a n) d")

        with nc.Block() as block:
            @block.sync
            def _(sp):
                def load_x(b, s):
                    sp.dma_start(b_tiles(X, b), a["x"][bass.ds(b, 1)].rearrange("a (n p) d -> p (a n) d", p=P))\
                      .then_inc(x_in[s], 16)
                load_x(0, 0)
                sp.dma_start(ident[:, :], a["ident"]).then_inc(weights_in, 16)
                sp.dma_start(bias_cols[:, :], a["bias_cols"]).then_inc(weights_in, 16)
                sp.dma_start(W_all, a["weights"].rearrange("p (n d) -> p n d", n=len(WN))).then_inc(weights_in, 16)
                sp.dma_start(bv_row, a["bv"].to_broadcast([P, D])).then_inc(weights_in, 16)
                sp.dma_start(bo_row, a["ffn_bo"].to_broadcast([P, D])).then_inc(weights_in, 16)
                load_x(1, 1)

                def body(b, s, last):
                    if not isinstance(b, int):
                        wait_apart(sp, x_in[s], b * 8 + (16 - 8 * s))
                        load_x(b + 2, s)
                    for n, parts in enumerate((q_parts, k_parts)):
                        sp.wait_ge(parts_ready, b * 2 + (n + 5))
                        for g in range(NG):
                            sp.dma_start(parts[bass.ds(b * NG + g, 1)].rearrange("g t r s -> (g r) t s"),
                                         PARTS[g * GW:(g + 1) * GW, s, n]).then_inc(parts_stored[s], 16)
                two_steps(sp, body)
                for s in range(2):
                    sp.wait_ge(parts_stored[s], 128 + 128 * (B // 2))

            @block.scalar
            def _(act):
                act.wait_ge(zeroed, 1)
                zx = sorted_x.rearrange("(z p r) d -> z p (r d)", z=NZ, p=P)
                for z in range(NZ):
                    act.dma_start(zx[z], zero).then_inc(zero_out, 16)
                act.sem_inc(qk_sb, 2)
                act.sem_inc(gates_ready, 1)
                act.wait_ge(weights_in, 16 * NWA)
                nc.scalar.mul(bias_half[:, 0:1], bias_cols[:, 0:1], SCALE)
                nc.scalar.mul(bias_half[:, 1:3], bias_cols[:, 2:4], 0.5)
                for n, w in enumerate(("uf", "ui", "uc")):
                    nc.scalar.mul(U2[:, n, :], W[w], 0.5)
                nc.scalar.mul(uo_h[:, :], W["uo"], 0.5).then_inc(halved, 1)
                act.wait_ge(halved, 1)

                def transposed(n, s):
                    act.wait_ge(xnT_ps, n + 1)
                    nc.scalar.copy(XNT[:, s, :], psT[:, :]).then_inc(xnT_ready, 1)
                transposed(0, 0)

                def body(b, s, last):
                    act.wait_ge(parts_stored[s], b * 64 + (128 - 64 * s))
                    for n in range(2):
                        act.wait_ge((q_ps, k_ps)[n], b + 1)
                        if n == 0:
                            act.wait_ge(parts_ready, b * 2 + 2)
                        args = (dict(bias=bias_half[:, 0:1], scale=SCALE), dict(bias=bias_cols[:, 1:2]))[n]
                        nc.scalar.activation(QK[:, s, n, :], psQ[:, n, :], ACT.Identity, **args)
                        nc.scalar.activation(PARTS[:, s, n, 0, :], psQ[:, n, :], ACT.Identity, **args).then_inc(qk_sb, 1)
                    if not last:
                        transposed(b + 1, 1 - s)
                    act.wait_ge(g_ps, b + 1)
                    act.wait_ge(c_ready, b + 1)
                    nc.scalar.activation(TG[:, 0, :], psG[:, 0, :], ACT.Tanh, bias=bias_half[:, 1:2], scale=0.5)
                    nc.scalar.activation(TG[:, 1, :], psG[:, 1, :], ACT.Tanh, bias=bias_half[:, 2:3], scale=0.5)
                    nc.scalar.activation(TG[:, 2, :], psG[:, 2, :], ACT.Tanh,
                                         bias=bias_cols[:, 4:5]).then_inc(gates_ready, 1)
                    for n in range(2):
                        act.wait_ge(a_pool, b * 2 + (n + 2))
                        nc.scalar.copy(PARTS[:, s, n, 1, :], RES[:, n, :]).then_inc(second_ready, 1)
                two_steps(act, body)
                act.wait_ge(zero_out, 16 * NZ)

            @block.vector
            def _(dve):
                link, at, count = linker(dve, a_dve)
                nc.vector.memset(zero, 0.0).then_inc(zeroed, 1)
                dve.sem_inc(v_out, 1)
                dve.sem_inc(h_out, 1)

                def norm(b, s):
                    wait_apart(dve, x_in[s], b * 8 + (16 - 8 * s))
                    layer_norm(nc, link, stats, mv, rstd, var_ready, lambda: dve.wait_ge(rstd_ready, b + 1),
                               lambda t: b_tiles(X, b)[:, t, :], lambda t: XN[:, s, t, :]).then_inc(xn_ready, 1)
                norm(0, 0)
                dve.wait_ge(weights_in, 16 * NWA)
                link(nc.vector.memset(C2[:, :], 0.0))
                nc.vector.tensor_scalar(C2[:, :], C2[:, :], bias_cols[:, 5:6], 2.0, ALU.add, ALU.mult)\
                    .then_inc(c_ready, 1)

                first, per = count(), 3

                def body(b, s, last):
                    at(b * per + first)
                    if not last:
                        norm(b + 1, 1 - s)
                    dve.wait_ge(v_ps, b + 1)
                    for t in range(NST):
                        ins = nc.vector.tensor_tensor(V_all[:, bass.ds(b * NG, NG), t, :],
                                                      psV[:, t, :].rearrange("p (g c) -> p g c", g=NG),
                                                      bv_row.rearrange("p (g c) -> p g c", g=NG), ALU.add)
                    ins.then_inc(v_out, 1)
                    dve.wait_ge(h_ps, b + 1)
                    nc.vector.tensor_tensor(b_tiles(HX, b), psH[:, :, :],
                                            bo_row.unsqueeze(1).to_broadcast([P, NST, D]), ALU.add).then_inc(h_out, 1)
                    dve.wait_ge(gates_ready, b + 2)
                    nc.vector.scalar_tensor_tensor(CA[:, 0, :], TG[:, 0, :], 1.0, C2[:, :], ALU.add, ALU.mult)
                    link(nc.vector.scalar_tensor_tensor(CA[:, 1, :], TG[:, 1, :], 1.0, TG[:, 2, :], ALU.add, ALU.mult))
                    nc.vector.scalar_tensor_tensor(C2[:, :], CA[:, 0, :], 0.5, CA[:, 1, :], ALU.mult, ALU.add)\
                        .then_inc(c_ready, 1)
                    dve.wait_ge(c_ready, b + 2)
                    assert last or count() == per
                two_steps(dve, body)

            @block.gpsimd
            def _(pool):
                pool.sem_inc(parts_ready, 4)
                pool.sem_inc(parts_stored[0], 128)
                pool.sem_inc(parts_stored[1], 128)

                nc.gpsimd.memset(rstd[:, 2, :], -0.5).then_inc(a_pool, 1)
                pool.wait_ge(a_pool, 1)
                power(pool, 0)

                def body(b, s, last):
                    for n in range(2):
                        pool.wait_ge(qk_sb, b * 2 + (n + 3))
                        pool.wait_ge(parts_ready, b * 2 + (n + 3))
                        nc.gpsimd.tensor_tensor(RES[:, n, :], QK[:, s, n, :], PARTS[:, s, n, 0, :], ALU.subtract)\
                            .then_inc(a_pool, 1)
                        if n == 0 and not last:
                            power(pool, b + 1)
                    for n in range(2):
                        pool.wait_ge(second_ready, b * 2 + (n + 1))
                        nc.gpsimd.tensor_tensor(PARTS[:, s, n, 2, :], RES[:, n, :], PARTS[:, s, n, 1, :], ALU.subtract)\
                            .then_inc(parts_ready, 1)
                two_steps(pool, body)

            @block.tensor
            def _(pe):
                pe.wait_ge(weights_in, 16 * NWA)
                pe.wait_ge(halved, 1)

                def transposes(n, s):
                    pe.wait_ge(xn_ready, n + 1)
                    pe.wait_ge(xnT_ready, n)
                    for t in range(4):
                        ins = nc.tensor.transpose(psT[:, t * P:(t + 1) * P], XN[:, s, t, :], ident[:, :])
                    ins.then_inc(xnT_ps, 1)
                transposes(0, 0)

                def body(b, s, last):
                    pe.wait_ge(xnT_ready, b + 1)
                    xT = XNT[:, s, :]
                    pe.wait_ge(qk_sb, b * 2 + 2)
                    nc.tensor.matmul(psQ[:, 0, :], W["wq"], xT, start=True, stop=True).then_inc(q_ps, 1)
                    nc.tensor.matmul(psQ[:, 1, :], W["wk"], xT, start=True, stop=True).then_inc(k_ps, 1)
                    pe.wait_ge(v_out, b + 1)
                    for t in range(4):
                        ins = nc.tensor.matmul(psV[:, t, :], xT[:, t * P:(t + 1) * P], W["wv"], start=True, stop=True)
                    ins.then_inc(v_ps, 1)
                    pe.wait_ge(h_out, b + 1)
                    for t in range(4):
                        ins = nc.tensor.matmul(psH[:, t, :], xT[:, t * P:(t + 1) * P], W["wo"], start=True, stop=True)
                    ins.then_inc(h_ps, 1)
                    pe.wait_ge(gates_ready, b + 1)
                    for n, w in enumerate(("wf", "wi", "wc")):
                        nc.tensor.matmul(psG[:, n, :], W[w], xT, start=True, stop=False)
                    if not last:
                        transposes(b + 1, 1 - s)
                    pe.wait_ge(c_ready, b + 1)
                    for n in range(3):
                        ins = nc.tensor.matmul(psG[:, n, :], U2[:, n, :], C2[:, :], start=False, stop=True)
                    ins.then_inc(g_ps, 1)
                two_steps(pe, body)
        pa.close()

        pb = ExitStack()
        carved[0] = B * S
        maskb, identb = carve([P, P], BF16), carve([P, P], BF16)
        QS, KS = carve([P, NG, HG, S], BF16), carve([P, NG, HG, S], BF16)
        PR = carve([P, RING, S])
        P1, P2 = carve([P, RING, S], F16), carve([P, RING, S], F16)
        VG = carve([P, 2, NST, HG * (P + GW)], BF16)
        VG_heads = VG.rearrange("p g k (h x) -> p g k h x", h=HG)
        V1 = 3 * HD
        NROW = 6 * HD
        OS = sb(pb, "OS", [P, 2, S])
        maskf, pick = sb(pb, "maskf", [P, P]), sb(pb, "pick", [P, HG * (HD + 1)])
        NM = sb(pb, "NM", [P, 2, HG * NST])
        NR = sb(pb, "NR", [HG * NST, P])
        NP = sb(pb, "NP", [HG * NST, 3, P], BF16)
        VR = sb(pb, "VR", [P, NST, GW])
        RI = sb(pb, "RI", [P, 2, NST * HG])
        psS = ps(pb, "psS", [P, 2, S])
        psST = ps(pb, "psST", [P, 3, S])
        psO = ps(pb, "psO", [P, 2, S])
        psM = ps(pb, "psM", [P, S])
        psN = psM[0:HG * NST, 0:P]
        psF = psM[:, P:P + NST * HG * (HD + 1)].rearrange("p (q x) -> p q x", q=NST)

        mask_in, b_const, stack_clear = sem("mask_in"), sem("b_const"), sem("stack_clear")
        stack_in = [sem(f"stack_in{g}") for g in range(NG)]
        max_in = [sem(f"max_in{g}") for g in range(NG)]
        s_done, max_done, nt_done, n_split, v_split = (sem(n) for n in ("s_done", "max_done", "nt_done", "n_split", "v_split"))
        st_done, exp_done, p1_act, p1_dve, p2_done, p2_dve, pv_done = (sem(n) for n in (
            "st_done", "exp_done", "p1_act", "p1_dve", "p2_done", "p2_dve", "pv_done"))
        BY_DVE = 6
        o_evac, post_done, b_dve, norm_done = sem("o_evac"), sem("post_done"), sem("b_dve"), sem("norm_done")

        def keys_of(v):
            return {0: [(0, 0, 0, S)], 1: [(1, P, 0, 3 * P), (3, 3 * P, 3 * P, S)], 2: [(2, 2 * P, 0, 2 * P)]}[v % 3]

        def second_parts(i, v):
            j, w = i + v // NU, v % NU
            if w % GU == BY_DVE:
                return p2_dve, j * NG + (w // GU + 1)
            return p2_done, j * (NU - NG) + sum(x % GU != BY_DVE for x in range(w + 1))

        def width(v):
            return 2 * P if v % 3 == 2 else S

        def skewed(eng, body):
            for u in range(NU):
                body(0, u, lambda lag, u=u: u - lag >= 0)
            with eng.Fori(1, B) as i:
                for u in range(NU):
                    body(i, u, lambda lag: True)
            for u in range(LAG_NORM + 1):
                body(B, u, lambda lag, u=u: u - lag < 0 and lag > 0)

        def group(i, v):
            return i * NG + v // GU

        with nc.Block() as block:
            @block.sync
            def _(sp):
                sp.dma_start(maskf[:, :], a["mask"]).then_inc(mask_in, 16)
                sp.dma_start(pick[:, :], a["pick"]).then_inc(mask_in, 16)
                sp.wait_ge(stack_clear, 1)

                def load(j, g):
                    rows = q_parts[bass.ds(j, 1)].rearrange("a t (d h) s -> (a t) d (h s)", d=HD)
                    for r, t in enumerate((0, 0, 0, 1, 1, 2)):
                        sp.dma_start(QS[r * HD:(r + 1) * HD, g].rearrange("p h s -> p (h s)"),
                                     rows[t]).then_inc(stack_in[g], 16)
                    rows = k_parts[bass.ds(j, 1)].rearrange("a t (d h) s -> (a t d) (h s)", d=HD)
                    for r, n in ((0, 3), (3, 2), (5, 1)):
                        sp.dma_start(KS[r * HD:(r + n) * HD, g].rearrange("p h s -> p (h s)"),
                                     rows[0:n * HD]).then_inc(stack_in[g], 16)

                def put_maxima(j, g):
                    sp.wait_ge(n_split, j * 4 + 4)
                    for t in range(3):
                        sp.dma_start(QS[NROW + t:NROW + t + 1, g].rearrange("p h (q s) -> p (h q) s", q=NST),
                                     NP[:, t, :]).then_inc(max_in[g], 16)
                for g in range(3):
                    load(g, g)
                with sp.Fori(0, B - 1) as i:
                    for g in range(NG):
                        put_maxima(i * NG + g, g)
                        wait_apart(sp, exp_done, i * NU + (g * GU + 3))
                        load(i * NG + (g + 3), (g + 3) % NG)
                for g in range(NG):
                    put_maxima((B - 1) * NG + g, g)
                    if g == 0:
                        sp.wait_ge(exp_done, (B - 1) * NU + 3)
                        load(B * NG - 1, NG - 1)

            @block.gpsimd
            def _(pool):
                nc.gpsimd.memset(KS[0:2 * GW], 1.0).then_inc(stack_clear, 1)
                pool.wait_ge(mask_in, 32)
                nc.gpsimd.tensor_copy(maskb, maskf[:, :])
                nc.gpsimd.tensor_copy(identb, ident[:, :])
                nc.gpsimd.memset(VG, 0.0).then_inc(b_const, 1)
                pool.wait_ge(b_const, 1)
                for g in range(2):
                    ins = nc.gpsimd.memset(VG_heads[:, g, :, :, V1:V1 + 1], 1.0)
                ins.then_inc(b_const, 1)
                with pool.Fori(0, B * NG) as j:
                    for v in range(GU):
                        if v == BY_DVE:
                            continue
                        n = v // 3
                        if v % 3 == 1:
                            pool.wait_ge(p1_dve, j * HG + (n + 1))
                        else:
                            pool.wait_ge(p1_act, j * 2 * HG + (2 * n + 1 + v % 3 // 2))
                        w = width(v)
                        nc.gpsimd.tensor_tensor(P2[:, v % RING, 0:w], PR[:, v % RING, 0:w], P1[:, v % RING, 0:w],
                                                ALU.subtract).then_inc(p2_done, 1)

            @block.tensor
            def _(pe):
                pe.wait_ge(b_const, 2)
                pe.wait_ge(mask_in, 32)
                pe.sem_inc(pv_done, RING)

                def body(i, u, has):
                    if has(0):
                        g, h = u // GU, u % GU // 3
                        if u % GU == 0:
                            pe.wait_ge(stack_in[g], i * 144 + 144)
                        pe.wait_ge(max_done, i * NU + (u + 1))
                        bank = psS[:, u % 2, :]
                        for qb, c0 in UNITS[u % 3]:
                            nc.tensor.matmul(bank[:, c0:c0 + (qb + 1) * P], QS[0:NROW, g, h, qb * P:(qb + 1) * P],
                                             KS[0:NROW, g, h, 0:(qb + 1) * P], start=True, stop=False)
                            ins = nc.tensor.matmul(bank[:, c0 + qb * P:c0 + (qb + 1) * P], identb, maskb,
                                                   start=False, stop=True)
                        ins.then_inc(s_done, 1)
                    if has(LAG_T) and (u - LAG_T) % GU == GU - 1:
                        v = u - LAG_T
                        pe.wait_ge(max_done, i * NU + (v + 3))
                        pe.wait_ge(norm_done, group(i, v))
                        nc.tensor.transpose(psN, NM[:, v // GU % 2, :], ident[:, :]).then_inc(nt_done, 1)
                    if has(LAG_S):
                        v = u - LAG_S
                        g, h = v // GU % NG, v % GU // 3
                        if v % GU == 0:
                            pe.wait_ge(max_in[g], (i + v // NU) * 48 + 48)
                        pe.wait_ge(exp_done, i * NU + (v + 1))
                        bank = psST[:, v % 3, :]
                        for kb, q0, c0, c1 in keys_of(v):
                            nc.tensor.matmul(bank[:, c0:c1], KS[0:NROW + 3, g, h, kb * P:(kb + 1) * P],
                                             QS[0:NROW + 3, g, h, q0:S], start=True, stop=False)
                            ins = nc.tensor.matmul(bank[:, c0:c0 + P], maskb, identb, start=False, stop=True)
                        ins.then_inc(st_done, 1)
                    if has(LAG_V):
                        v = u - LAG_V
                        g, h = v // GU % 2, v % GU // 3
                        if v % GU == 0:
                            pe.wait_ge(v_split, group(i, v) * 4 + 4)
                            pe.wait_ge(o_evac, group(i, v) + 1)
                        pe.wait_ge(*second_parts(i, v))
                        for kb, q0, c0, c1 in keys_of(v):
                            for n, part in enumerate((P1, P2)):
                                ins = nc.tensor.matmul(psO[:, g, q0:S], VG[:, g, kb, h * P:(h + 1) * P],
                                                       part[:, v % RING, c0:c1], start=(v % GU == 0 and n == 0),
                                                       stop=(v % GU == GU - 1 and n == 1))
                        ins.then_inc(pv_done, 1)
                    if has(LAG_F) and (u - LAG_F) % GU == GU - 1:
                        v = u - LAG_F
                        pe.wait_ge(o_evac, group(i, v) + 3)
                        n = group(i, v) + 3
                        pe.wait_ge(n_split, (min(n, B * NG) if isinstance(n, int) else n) * 4 - 2)
                        for qb in range(NST):
                            ins = nc.tensor.matmul(psF[:, qb, :], OS[:, v // GU % 2, qb * P:(qb + 1) * P], pick[:, :],
                                                   start=True, stop=True)
                        ins.then_inc(post_done, 1)
                skewed(pe, body)

            @block.scalar
            def _(act):
                act.sem_inc(exp_done, 3)
                act.sem_inc(o_evac, 2)

                def body(i, u, has):
                    if has(LAG_S):
                        v = u - LAG_S
                        w = width(v)
                        act.wait_ge(st_done, i * NU + (v + 1))
                        if has(LAG_S + RING):
                            act.wait_ge(*second_parts(i, v - RING))
                        nc.scalar.activation(PR[:, v % RING, 0:w], psST[:, v % 3, 0:w], ACT.Exp).then_inc(exp_done, 1)
                    if has(LAG_S + 1) and (u - LAG_S - 1) % 3 != 1:
                        v = u - LAG_S - 1
                        w = width(v)
                        act.wait_ge(exp_done, i * NU + (v + 4))
                        act.wait_ge(pv_done, i * NU + (v + 1))
                        nc.scalar.copy(P1[:, v % RING, 0:w], PR[:, v % RING, 0:w]).then_inc(p1_act, 1)
                    if has(LAG_V + 1) and (u - LAG_V - 1) % GU == GU - 1:
                        v = u - LAG_V - 1
                        act.wait_ge(pv_done, i * NU + (v + (1 + RING)))
                        act.wait_ge(post_done, group(i, v) + 1)
                        nc.scalar.copy(OS[:, v // GU % 2, :], psO[:, v // GU % 2, :]).then_inc(o_evac, 1)
                skewed(act, body)

            @block.vector
            def _(dve):
                dve.sem_inc(max_done, 2)
                dve.sem_inc(norm_done, 2)
                dve.sem_inc(post_done, 2)
                dve.wait_ge(b_const, 2)

                def body(i, u, has):
                    if has(0):
                        g, h = u // GU, u % GU // 3
                        dve.wait_ge(s_done, i * NU + (u + 1))
                        for qb, c0 in UNITS[u % 3]:
                            ins = nc.vector.tensor_reduce(NM[:, g % 2, h * NST + qb:h * NST + qb + 1],
                                                          psS[:, u % 2, c0:c0 + (qb + 1) * P], AX.X, ALU.max, negate=True)
                        ins.then_inc(max_done, 1)
                    if has(LAG_S + 1) and (u - LAG_S - 1) % 3 == 1:
                        v = u - LAG_S - 1
                        dve.wait_ge(exp_done, i * NU + (v + 4))
                        dve.wait_ge(pv_done, i * NU + (v + 1))
                        nc.vector.tensor_copy(P1[:, v % RING, :], PR[:, v % RING, :]).then_inc(p1_dve, 1)
                    if has(LAG_S + 2) and (u - LAG_S - 2) % GU == BY_DVE:
                        v = u - LAG_S - 2
                        w, n = width(v), v // 3
                        dve.wait_ge(p1_act, i * (2 * NU // 3) + (2 * n + 1 + v % 3 // 2))
                        nc.vector.tensor_tensor(P2[:, v % RING, 0:w], PR[:, v % RING, 0:w], P1[:, v % RING, 0:w],
                                                ALU.subtract).then_inc(p2_dve, 1)
                    if has(GU) and (u - GU) % GU in (2, 3):
                        v = u - GU
                        j, n, g = group(i, v), v % GU, v // GU % NG
                        if n == 2:
                            dve.wait_ge(nt_done, j + 1)
                            if has(2 * GU):
                                dve.wait_ge(max_in[(g - 1) % NG], (i + v // NU) * 48 + (48 if g else 0))
                            nc.vector.tensor_scalar(NP[:, 0, :], psN, GAIN, None, ALU.add).then_inc(n_split, 1)
                            dve.wait_ge(n_split, j * 4 + 1)
                            nc.vector.scalar_tensor_tensor(NR[:, :], psN, GAIN, NP[:, 0, :],
                                                           ALU.add, ALU.subtract).then_inc(n_split, 1)
                        else:
                            dve.wait_ge(n_split, j * 4 + 2)
                            nc.vector.tensor_copy(NP[:, 1, :], NR[:, :]).then_inc(n_split, 1)
                            dve.wait_ge(n_split, j * 4 + 3)
                            nc.vector.tensor_tensor(NP[:, 2, :], NR[:, :], NP[:, 1, :], ALU.subtract).then_inc(n_split, 1)
                    if has(GU) and (u - GU) % GU in (4, 5, 6, 7):
                        v = u - GU
                        j, n, g = group(i, v), v % GU - 4, v // GU % 2
                        rest = VR[:, :, :].rearrange("p k (h e) -> p k h e", e=HD)
                        part = [VG_heads[:, g, :, :, t * HD:(t + 1) * HD] for t in range(3)]
                        if n == 0:
                            if has(2 * GU):
                                dve.wait_ge(pv_done, i * NU + (v // GU * GU - GU + RING))
                            src = V_all[:, bass.ds(j, 1)].rearrange("p a k (h e) -> p (a k) h e", e=HD)
                            nc.vector.tensor_copy(part[0], src).then_inc(v_split, 1)
                        elif n == 1:
                            dve.wait_ge(v_split, j * 4 + 1)
                            src = V_all[:, bass.ds(j, 1)].rearrange("p a k (h e) -> p (a k) h e", e=HD)
                            nc.vector.tensor_tensor(rest, src, part[0], ALU.subtract).then_inc(v_split, 1)
                        elif n == 2:
                            dve.wait_ge(v_split, j * 4 + 2)
                            nc.vector.tensor_copy(part[1], rest).then_inc(v_split, 1)
                        else:
                            dve.wait_ge(v_split, j * 4 + 3)
                            nc.vector.tensor_tensor(part[2], rest, part[1], ALU.subtract).then_inc(v_split, 1)
                    if has(LAG_NORM) and (u - LAG_NORM) % GU == GU - 1:
                        v = u - LAG_NORM
                        j, g = group(i, v), v // GU % 2
                        heads = psF.rearrange("p q (h x) -> p (q h) x", x=HD + 1)
                        dve.wait_ge(post_done, j + 3)
                        nc.vector.reciprocal(RI[:, g], heads[:, :, HD:HD + 1].rearrange("p n a -> p (n a)")).then_inc(b_dve, 1)
                        dve.wait_ge(b_dve, j + 1)
                        nc.vector.tensor_tensor(
                            O_all[:, bass.ds(j, 1)].rearrange("p a q (h e) -> p (a q h) e", e=HD), heads[:, :, 0:HD],
                            RI[:, g].unsqueeze(2).to_broadcast([P, NST * HG, HD]), ALU.mult).then_inc(norm_done, 1)
                skewed(dve, body)
        pb.close()

        pc = ExitStack()
        XB1 = BIG[:, 0, :].rearrange("p (k t s) -> p k t s", t=B, s=BS)
        WC = sb(pc, "WC", [P, D])
        rw = sb(pc, "rw", [P, NE])
        ab_row = sb(pc, "ab_row", [P, D])
        CU = C2[:, :].rearrange("p (n d) -> p n d", n=NST)
        carved[0] = B * S
        OST, OT = carve([P, 4, D]), carve([P, 2, S])
        HS, XS, XT = carve([P, 2, 4, D]), carve([P, 2, 4, D]), carve([P, 2, S])
        c_in, cu_ps = sem("c_in"), sem("cu_ps")
        ost_ready, oT_ps, oT_sb, y_ps, x1_ready, hs_pre, hs_ready, xs_ready, xT_ps, xT_sb = (sem(n) for n in (
            "ost_ready", "oT_ps", "oT_sb", "y_ps", "x1_ready", "hs_pre", "hs_ready", "xs_ready", "xT_ps", "xT_sb"))
        r_ps, log_sb, xs_copied, c_dve, c_pool = (sem(n) for n in ("r_ps", "log_sb", "xs_copied", "c_dve", "c_pool"))
        xb1_ready = sem("xb1_ready")
        psA, psA2 = ps(pc, "psA", [P, 4, D]), ps(pc, "psA2", [P, 4, D])
        psB = ps(pc, "psB", [P, 2, 4, D])
        psR = ps(pc, "psR", [P, S])[:, 0:4 * NE]
        psCU = ps(pc, "psCU", [P, NST, D])

        def flat(t):
            return t.rearrange("p t d -> p (t d)")

        with nc.Block() as block:
            @block.sync
            def _(sp):
                sp.dma_start(WC[:, :], a["attn_wo"]).then_inc(c_in, 16)
                sp.dma_start(rw[:, :], a["router"]).then_inc(c_in, 16)
                sp.dma_start(ab_row[:, :], a["attn_bo"].to_broadcast([P, D])).then_inc(c_in, 16)

            @block.gpsimd
            def _(pool):
                pool.sem_inc(xs_copied, 2)
                pool.wait_ge(c_in, 48)

                def add_bias(n):
                    nc.gpsimd.tensor_tensor(b_tiles(X, n), b_tiles(X, n),
                                            ab_row[:, :].unsqueeze(1).to_broadcast([P, NST, D]), ALU.add).then_inc(c_pool, 1)
                add_bias(0)

                def body(b, s, last):
                    if not last:
                        add_bias(b + 1)
                    power(pool, b + B)
                    wait_apart(pool, xs_ready, b + 1)
                    nc.gpsimd.tensor_copy(b_tiles(HX, b), XS[:, s]).then_inc(xs_copied, 1)
                two_steps(pool, body)

            @block.tensor
            def _(pe):
                pe.wait_ge(c_in, 48)
                for t in range(NST):
                    ins = nc.tensor.matmul(psCU[:, t, :], C2[:, t * P:(t + 1) * P], uo_h[:, :], start=True, stop=True)
                ins.then_inc(cu_ps, 1)
                pe.sem_inc(xT_ps, 2)
                pe.sem_inc(y_ps, 2)
                pe.sem_inc(r_ps, 2)

                def output(n, s):
                    pe.wait_ge(ost_ready, n + 1)
                    pe.wait_ge(oT_sb, n + 1)
                    for t in range(4):
                        ins = nc.tensor.transpose(psA[:, t, :], OST[:, t, :], ident[:, :])
                    ins.then_inc(oT_ps, 1)
                    pe.wait_ge(oT_sb, n + 2)
                    pe.wait_ge(x1_ready, n + 1)
                    for t in range(4):
                        ins = nc.tensor.matmul(psB[:, s, t, :], OT[:, s, t * P:(t + 1) * P], WC[:, :], start=True, stop=True)
                    ins.then_inc(y_ps, 1)
                output(0, 0)

                def body(b, s, last):
                    if not last:
                        output(b + 1, 1 - s)
                    pe.wait_ge(xs_ready, b + 1)
                    pe.wait_ge(xT_sb, b + 1)
                    for t in range(4):
                        ins = nc.tensor.transpose(psA2[:, t, :], XS[:, s, t, :], ident[:, :])
                    ins.then_inc(xT_ps, 1)
                    pe.wait_ge(xT_sb, b + 2)
                    pe.wait_ge(log_sb, b + 1)
                    for t in range(4):
                        ins = nc.tensor.matmul(psR[:, t * NE:(t + 1) * NE], XT[:, s, t * P:(t + 1) * P], rw[:, :],
                                               start=True, stop=True)
                    ins.then_inc(r_ps, 1)
                two_steps(pe, body)

            @block.scalar
            def _(act):
                act.sem_inc(oT_sb, 1)
                act.sem_inc(xT_sb, 1)
                act.sem_inc(log_sb, 1)
                act.sem_inc(xb1_ready, 2)

                def output(n, s):
                    act.wait_ge(oT_ps, n)
                    for g in range(NG):
                        ins = nc.scalar.copy(OST[:, :, g * GW:(g + 1) * GW],
                                             O_all[:, bass.ds(n * NG + g, 1)].rearrange("p a q c -> p (a q) c"))
                    ins.then_inc(ost_ready, 1)
                    act.wait_ge(hs_pre, n + 1)
                    nc.scalar.activation(HS[:, s], HS[:, s], ACT.Tanh).then_inc(hs_ready, 1)
                    act.wait_ge(oT_ps, n + 1)
                    act.wait_ge(y_ps, n + 1)
                    nc.scalar.copy(OT[:, s, :], flat(psA[:, :, :])).then_inc(oT_sb, 1)
                output(0, 0)

                def body(b, s, last):
                    if not last:
                        output(b + 1, 1 - s)
                    act.wait_ge(xT_ps, b + 3)
                    act.wait_ge(r_ps, b + 1)
                    act.wait_ge(xb1_ready, b + 1)
                    nc.scalar.copy(XT[:, s, :], flat(psA2[:, :, :])).then_inc(xT_sb, 1)
                    act.wait_ge(xT_sb, b + 2)
                    nc.scalar.copy(XB1[:, :, bass.ds(b, 1), :].rearrange("p k a s -> p k (a s)"),
                                   XT[:, s, :].rearrange("p (k s) -> p k s", s=BS)).then_inc(xb1_ready, 1)
                    act.wait_ge(r_ps, b + 3)
                    nc.scalar.copy(LOG[:, bass.ds(b * NST, NST), :].rearrange("p n e -> p (n e)"), psR).then_inc(log_sb, 1)
                two_steps(act, body)

            @block.vector
            def _(dve):
                link, at, count = linker(dve, c_dve)
                dve.sem_inc(x1_ready, 2)
                dve.wait_ge(c_in, 48)
                dve.wait_ge(cu_ps, 1)
                link(nc.vector.tensor_copy(CU[:, :, :], psCU[:, :, :]))

                def tanh_argument(n, s):
                    dve.wait_ge(x1_ready, n + 1)
                    nc.vector.tensor_tensor(HS[:, s], b_tiles(HX, n), CU[:, :, :], ALU.add).then_inc(hs_pre, 1)
                tanh_argument(0, 0)
                per = 4

                def body(b, s, last):
                    at(b * per + 1)
                    if not last:
                        tanh_argument(b + 1, 1 - s)
                    dve.wait_ge(c_pool, b + 1)
                    dve.wait_ge(y_ps, b + 3)
                    link(nc.vector.tensor_tensor(b_tiles(X, b), psB[:, s], b_tiles(X, b), ALU.add))
                    dve.wait_ge(hs_ready, b + 1)
                    link(nc.vector.tensor_tensor(b_tiles(X, b), b_tiles(X, b), HS[:, s], ALU.add))
                    dve.sem_inc(x1_ready, 1)
                    dve.wait_ge(xs_copied, b + 1)
                    wait_apart(dve, xT_ps, b + 1)
                    layer_norm(nc, link, stats, mv, rstd, var_ready, lambda: dve.wait_ge(rstd_ready, b + (B + 1)),
                               lambda t: b_tiles(X, b)[:, t, :], lambda t: XS[:, s, t, :]).then_inc(xs_ready, 1)
                    dve.wait_ge(xs_ready, b + 1)
                    assert count() == per
                two_steps(dve, body)
        pc.close()
        attn_space.close()

        pr = ExitStack()

        def rsb(shape, dt=F32):
            rsb.n += 1
            return sb(pr, f"r{rsb.n}", shape, dt)[:]
        rsb.n = 0
        OH, ET = rsb([P, NTILE, NE]), rsb([P, NTILE, NE])
        TOT, INC = rsb([P, NE, NTILE]), rsb([P, NE, NTILE])
        ones64, iota64 = rsb([P, NTILE]), rsb([P, NTILE])
        mxl, idx, posf = rsb([P, NTILE]), rsb([P, NTILE]), rsb([P, NTILE])
        iota8 = rsb([P, NE])
        nblk, incb, baseb = rsb([P, NE]), rsb([P, NE]), rsb([P, NE])
        onesm, before = rsb([P, P]), rsb([P, P])
        iotab, ebf, ebc = rsb([P, NBLK]), rsb([P, NBLK]), rsb([P, NBLK, NE])
        psRT = ps(pr, "psRT", [P, 2, NTILE * NE])

        VT = BIG[:, 2, :].rearrange("p (j x) -> p j x", j=NG1)
        carved[0], limit = B * S, 2 * B * S
        XTS, Q32 = carve([P, 2, 4, P]), carve([P, NBT, P])
        REST = carve([P, 4, S])
        QKP = carve([P, 4, 3, S], BF16)
        WP = rsb([P, 3, D])
        relk, relrow, sel = rsb([P, NREL, NH]), rsb([P, NREL]), rsb([P, NH])
        bq1, bv1 = rsb([P, 3]), rsb([P, D])
        assert carved[0] <= limit
        RP = rsb([P, 2, 3, NBT, B, BS], BF16)
        psC = ps(pr, "psC", [P, 4, S])
        p_in, p_const, p_act, p_ps = sem("p_in"), sem("p_const"), sem("p_act"), sem("p_ps")
        first_done, rest_done, second_done, third_done, vt_done = (sem(n) for n in (
            "first_done", "rest_done", "second_done", "third_done", "vt_done"))
        qk_out, rel_out = [sem(f"qk_out{n}") for n in range(4)], sem("rel_out")
        NIT = 20
        SPLIT = [j for j in range(NIT) if not 8 <= j < 12]
        NSP = len(SPLIT)
        psRank, psTot = (psRT[:, n, :].rearrange("p (j e) -> p j e", e=NE) for n in range(2))
        e_const, e_oh, e_rank, pos_ready, scattered, e_dve = (sem(n) for n in (
            "e_const", "e_oh", "e_rank", "pos_ready", "scattered", "e_dve"))

        with nc.Block() as block:
            @block.sync
            def _(sp):
                sp.dma_start(onesm, a["ones"]).then_inc(e_const, 16)
                sp.dma_start(before, a["before"]).then_inc(e_const, 16)
                sp.dma_start(iota8, a["iota8"].to_broadcast([P, NE])).then_inc(e_const, 16)
                sp.dma_start(iota64, a["iota64"].to_broadcast([P, NTILE])).then_inc(e_const, 16)
                sp.dma_start(iotab, a["iotab"].to_broadcast([P, NBLK])).then_inc(e_const, 16)
                sp.dma_start(WP, a["in_proj"].rearrange("p (n d) -> p n d", n=3)).then_inc(p_in, 16)
                sp.dma_start(bq1[:, 0:2], a["in_bias_qk"]).then_inc(p_in, 16)
                sp.dma_start(bv1, a["in_bias_v"].to_broadcast([P, D])).then_inc(p_in, 16)
                sp.dma_start(relrow, a["relk"]).then_inc(p_in, 16)
                sp.dma_start(sel, a["sel"]).then_inc(p_in, 16)
                for s in range(4):
                    sp.sem_inc(qk_out[s], 16)
                sp.sem_inc(rel_out, 96)

                with sp.Fori(0, NST) as st:
                    for n, parts in enumerate((q1_parts, k1_parts)):
                        for c in range(4):
                            k = n * 4 + c
                            sp.wait_ge(third_done, st * NSP + (k + 5))
                            sp.dma_start(parts[bass.ds(st, 1), :, :, c * S:(c + 1) * S].rearrange("a t p s -> p (a t) s"),
                                         QKP[:, k % 4]).then_inc(qk_out[k % 4], 16)
                    for half in range(2):
                        sp.wait_ge(third_done, st * NSP + (8 + 4 * half + 8))
                        for t in range(3):
                            sp.dma_start(r1_parts[bass.ds(st, 1), t, half].rearrange("a p s -> (a p) s"),
                                         RP[:, half, t].rearrange("p k t s -> p (k t s)")).then_inc(rel_out, 16)
                for s in range(4):
                    sp.wait_ge(qk_out[s], 16 + NST * 32)
                sp.wait_ge(rel_out, 96 + NST * 96)

            @block.scalar
            def _(act):
                act.wait_ge(p_in, 80)
                nc.scalar.mul(bq1[:, 2:3], bq1[:, 0:1], SCALE).then_inc(p_act, 1)
                act.wait_ge(p_act, 1)

                with act.Fori(0, NST) as st:
                    def second(k):
                        act.wait_ge(rest_done, st * NSP + (k + 5))
                        ring, j = k % 4, SPLIT[k]
                        if j < 8:
                            ins = nc.scalar.copy(QKP[:, ring, 1, :], REST[:, ring, :])
                        else:
                            half, c = (j - 12) // 4, j % 4
                            ins = nc.scalar.copy(RP[:, half, 1, :, 4 * c:4 * c + 4, :].rearrange("p k t s -> p k (t s)"),
                                                 REST[:, ring, :].rearrange("p (k x) -> p k x", k=NBT))
                        ins.then_inc(second_done, 1)
                    def v_operand(c):
                        nc.scalar.copy(XTS[:, c % 2], XB1[:, bass.ds(st * NBT + 4 * c, 4)].rearrange("p k t s -> p k (t s)"))\
                          .then_inc(p_act, 1)
                    v_operand(0)
                    v_operand(1)
                    for k, j in enumerate(SPLIT):
                        act.wait_ge(p_ps, st * NIT + (j + 1))
                        bank = psC[:, j % 4, :]
                        if j < 8:
                            c, isk = j % 4, j // 4
                            act.wait_ge(qk_out[k % 4], st * 32 + (k // 4 * 16 + 16))
                            if isk:
                                dst = REST[:, k % 4, :]
                                act.wait_ge(third_done, st * NSP + (k + 1))
                                args = dict(bias=bq1[:, 1:2])
                            else:
                                dst = Q32[:, 4 * c:4 * c + 4, :].rearrange("p k s -> p (k s)")
                                args = dict(bias=bq1[:, 2:3], scale=SCALE)
                            nc.scalar.activation(dst, bank, ACT.Identity, **args)
                            nc.scalar.activation(QKP[:, k % 4, 0, :], bank, ACT.Identity, **args).then_inc(first_done, 1)
                        else:
                            half, c = (j - 12) // 4, j % 4
                            if j == 12:
                                act.wait_ge(rel_out, st * 96 + 96)
                            nc.scalar.copy(RP[:, half, 0, :, 4 * c:4 * c + 4, :].rearrange("p k t s -> p k (t s)"),
                                           bank.rearrange("p (k x) -> p k x", k=NBT)).then_inc(first_done, 1)
                        if j == 7:
                            for c in (2, 3):
                                act.wait_ge(p_ps, st * NIT + (7 + c))
                                v_operand(c)
                        if k >= 2:
                            second(k - 2)
                    second(NSP - 2)
                    second(NSP - 1)

            @block.vector
            def _(dve):
                link, at, count = linker(dve, e_dve)
                link(nc.vector.memset(ones64, 1.0))
                dve.wait_ge(e_const, 80)
                link(nc.vector.tensor_reduce(mxl, LOG[:, :, :], AX.X, ALU.max))
                link(nc.vector.tensor_tensor(ET, LOG[:, :, :], mxl.unsqueeze(2).to_broadcast([P, NTILE, NE]), ALU.is_equal))
                io = iota8.unsqueeze(1).to_broadcast([P, NTILE, NE])
                link(nc.vector.tensor_tensor(ET, ET, io, ALU.mult))
                link(nc.vector.tensor_reduce(idx, ET, AX.X, ALU.min))
                nc.vector.tensor_tensor(OH, idx.unsqueeze(2).to_broadcast([P, NTILE, NE]), io, ALU.is_equal).then_inc(e_oh, 1)
                dve.wait_ge(e_rank, 1)
                link(nc.vector.tensor_copy(TOT, psTot.rearrange("p j e -> p e j")))
                for e in range(NE):
                    ins = nc.vector.tensor_tensor_scan(INC[:, e, :], ones64, TOT[:, e, :], 0.0, ALU.mult, ALU.add)
                link(ins)
                for e in range(NE):
                    ins = nc.vector.tensor_scalar(ET.rearrange("p j e -> p (j e)")[:, e * NTILE:(e + 1) * NTILE], iota64,
                                                  INC[:, e, NTILE - 1:NTILE], None, ALU.is_lt)
                link(ins)
                link(nc.vector.tensor_reduce(nblk, ET.rearrange("p j e -> p (j e)").rearrange("p (e n) -> p e n", e=NE),
                                             AX.X, ALU.add))
                link(nc.vector.tensor_tensor_scan(incb, ones64[:, 0:NE], nblk, 0.0, ALU.mult, ALU.add))
                link(nc.vector.tensor_tensor(baseb, incb, nblk, ALU.subtract))
                link(nc.vector.tensor_scalar(baseb, baseb, float(P), None, ALU.mult))
                link(nc.vector.tensor_tensor(INC, INC, TOT, ALU.subtract))
                link(nc.vector.tensor_tensor(INC, INC, baseb.unsqueeze(2).to_broadcast([P, NE, NTILE]), ALU.add))
                link(nc.vector.tensor_tensor(ET, psRank, INC.rearrange("p e j -> p j e"), ALU.add))
                link(nc.vector.tensor_tensor(ET, ET, OH, ALU.mult))
                link(nc.vector.tensor_reduce(posf, ET, AX.X, ALU.add))
                link(nc.vector.tensor_copy(pos[:, :], posf))
                link(nc.vector.tensor_tensor(ebc, incb.unsqueeze(1).to_broadcast([P, NBLK, NE]),
                                             iotab.unsqueeze(2).to_broadcast([P, NBLK, NE]), ALU.is_le))
                link(nc.vector.tensor_reduce(ebf, ebc, AX.X, ALU.add))
                link(nc.vector.tensor_scalar(ebf, ebf, float(NE - 1), None, ALU.min))
                nc.vector.tensor_copy(eb[0:1, :], ebf[0:1, :]).then_inc(pos_ready, 1)

                dve.sem_inc(rest_done, 4)
                dve.sem_inc(third_done, 4)
                dve.wait_ge(p_in, 80)
                with dve.Fori(0, NST) as st:
                    def third(k):
                        dve.wait_ge(second_done, st * NSP + (k + 1))
                        ring, j = k % 4, SPLIT[k]
                        if j < 8:
                            ins = nc.vector.tensor_tensor(QKP[:, ring, 2, :], REST[:, ring, :], QKP[:, ring, 1, :], ALU.subtract)
                        else:
                            rp = RP[:, (j - 12) // 4, :, :, 4 * (j % 4):4 * (j % 4) + 4, :].rearrange("p a k t s -> p a k (t s)")
                            ins = nc.vector.tensor_tensor(rp[:, 2], REST[:, ring, :].rearrange("p (k x) -> p k x", k=NBT),
                                                          rp[:, 1], ALU.subtract)
                        ins.then_inc(third_done, 1)
                    for k, j in enumerate(SPLIT):
                        dve.wait_ge(first_done, st * NSP + (k + 1))
                        dve.wait_ge(third_done, st * NSP + (k + 1))
                        ring, c = k % 4, j % 4
                        if j < 4:
                            ins = nc.vector.tensor_tensor(REST[:, ring, :], Q32[:, 4 * c:4 * c + 4, :].rearrange("p k s -> p (k s)"),
                                                          QKP[:, ring, 0, :], ALU.subtract)
                        elif j < 8:
                            ins = nc.vector.tensor_tensor(REST[:, ring, :], REST[:, ring, :], QKP[:, ring, 0, :], ALU.subtract)
                        else:
                            rp = RP[:, (j - 12) // 4, 0, :, 4 * c:4 * c + 4, :].rearrange("p k t s -> p k (t s)")
                            ins = nc.vector.tensor_tensor(REST[:, ring, :].rearrange("p (k x) -> p k x", k=NBT),
                                                          psC[:, j % 4, :].rearrange("p (k x) -> p k x", k=NBT), rp, ALU.subtract)
                        ins.then_inc(rest_done, 1)
                        if k >= 2:
                            third(k - 2)
                        if j == 7:
                            for c in range(4):
                                dve.wait_ge(p_ps, st * NIT + (9 + c))
                                for n in range(4):
                                    ins = nc.vector.tensor_tensor(
                                        VT[:, bass.ds(st * NPAIR, NPAIR), (4 * c + n) * GW1:(4 * c + n + 1) * GW1],
                                        psC[:, c, n * P:(n + 1) * P].rearrange("p (g x) -> p g x", g=NPAIR),
                                        bv1.rearrange("p (g x) -> p g x", g=NPAIR), ALU.add)
                                ins.then_inc(vt_done, 1)
                    third(NSP - 2)
                    third(NSP - 1)

            @block.tensor
            def _(pe):
                pe.wait_ge(e_const, 80)
                pe.wait_ge(e_oh, 1)
                oh = OH.rearrange("p j e -> p (j e)")
                nc.tensor.matmul(psRT[:, 0, :], before, oh, start=True, stop=True)
                nc.tensor.matmul(psRT[:, 1, :], onesm, oh, start=True, stop=True).then_inc(e_rank, 1)

                pe.wait_ge(p_in, 80)
                with pe.Fori(0, NST) as st:
                    for j in range(NIT):
                        if j < 4:
                            pe.wait_ge(rest_done, st * NSP + (j + 1))
                        elif j < 12:
                            pe.wait_ge(first_done, st * NSP + (j - 3))
                        elif j < 16:
                            pe.wait_ge(vt_done, st * 4 + (j - 11))
                        else:
                            pe.wait_ge(rest_done, st * NSP + (j - 16 + 8 + 5))
                        bank = psC[:, j % 4, :]
                        if j < 8:
                            x = XB1[:, bass.ds(st * NBT + 4 * (j % 4), 4)].rearrange("p k t s -> p (k t s)")
                            ins = nc.tensor.matmul(bank, WP[:, j // 4, :], x, start=True, stop=True)
                        elif j < 12:
                            pe.wait_ge(p_act, st * 4 + (j - 6))
                            for n in range(4):
                                ins = nc.tensor.matmul(bank[:, n * P:(n + 1) * P], XTS[:, j % 2, n, :], WP[:, 2, :],
                                                       start=True, stop=True)
                        else:
                            if j == 12:
                                pe.wait_ge(first_done, st * NSP + 4)
                                pe.wait_ge(p_const, 1)
                            for n in range(4):
                                t, half = j % 4 * 4 + n, (j - 12) // 4
                                r = MAXREL - t + 8 * half
                                ins = nc.tensor.matmul(
                                    bank.rearrange("p (k n s) -> p k n s", k=NBT, n=4)[:, :, n, :],
                                    relk[:, r:r + 8, :].rearrange("p r h -> p (r h)"),
                                    Q32.rearrange("p k (t s) -> p k t s", t=B)[:, :, t, :], start=True, stop=True)
                        ins.then_inc(p_ps, 1)

            @block.gpsimd
            def _(pool):
                pool.wait_ge(p_in, 80)
                nc.gpsimd.tensor_tensor(relk, relrow.unsqueeze(2).to_broadcast([P, NREL, NH]),
                                        sel.unsqueeze(1).to_broadcast([P, NREL, NH]), ALU.mult).then_inc(p_const, 1)
                pool.wait_ge(pos_ready, 1)
                for b in range(B):
                    for st in range(NST):
                        j = b * NST + st
                        pool.indirect_dma_start(sorted_x, bass.IndirectOffsetOnAxis(pos[:, j:j + 1], 0),
                                                HX[:, b, st, :], None).then_inc(scattered, 16)
                pool.wait_ge(scattered, 16 * NTILE)
        pr.close()

        pd = ExitStack()
        carved[0] = 0
        QS1, KS1 = carve([P, 4, 2, NBT, P], BF16), carve([P, 4, 2, NBT, P], BF16)
        hx = HX[:, :, :, :].rearrange("p a n d -> p (a n d)")
        PR1 = hx[:, 0:RING * S].rearrange("p (r x) -> p r x", r=RING)
        P11, P21 = (hx[:, (4 + n) * RING * S // 4:][:, 0:RING * S // 2].bitcast(F16).rearrange("p (r x) -> p r x", r=RING)
                    for n in (0, 2))
        OS1 = hx[:, 2 * RING * S:4 * RING * S].rearrange("p (g t k s) -> p g t k s", g=2, t=B, s=BS)
        VG1 = sb(pd, "VG1", [P, 2, NBT, 2 * P], BF16)
        VG1_heads = VG1[:, :, :, :].rearrange("p g k (h x) -> p g k h x", h=2)
        rows1 = sb(pd, "rows1", [P, 3, P])
        rows1b = sb(pd, "rows1b", [P, 2, P], BF16)
        RV1 = sb(pd, "RV1", [P, B, 2 * (HD + 1)])
        wout = sb(pd, "wout", [P, D])
        bout_row = sb(pd, "bout_row", [P, D])
        NM1, NR1 = sb(pd, "NM1", [P, 2, 2 * NBT]), sb(pd, "NR1", [2 * NBT, P])
        NP1 = sb(pd, "NP1", [2 * NBT, 3, P], BF16)
        VR1, RI1 = sb(pd, "VR1", [P, NBT, GW1]), sb(pd, "RI1", [P, 2, 2 * B])
        OST1, OT1 = sb(pd, "OST1", [P, 2, NST, D]), sb(pd, "OT1", [P, 2, S])
        psS1, psST1, psO1 = ps(pd, "psS1", [P, 2, S]), ps(pd, "psST1", [P, 2, S]), ps(pd, "psO1", [P, 2, S])
        psN1 = ps(pd, "psN1", [P, S])[0:2 * NBT, 0:P]
        psF1 = ps(pd, "psF1", [P, S])[:, 0:B * 2 * (HD + 1)].rearrange("p (t x) -> p t x", t=B)
        d_in, rv_in, d_const, d_vg = sem("d_in"), sem("rv_in"), sem("d_const"), sem("d_vg")
        d_rows = sem("d_rows")
        stack1_in = [sem(f"stack1_in{g}") for g in range(4)]
        max1_in = [sem(f"max1_in{g}") for g in range(4)]
        s1_done, max1_done, nt1_done, n1_split, v1_split = (sem(n) for n in (
            "s1_done", "max1_done", "nt1_done", "n1_split", "v1_split"))
        st1_done, exp1_done, p11_done, p21_done, pv1_done = (sem(n) for n in (
            "st1_done", "exp1_done", "p11_done", "p21_done", "pv1_done"))
        xb2_done = sem("xb2_done")
        o1_evac, post1_done, d_dve, norm1_done = sem("o1_evac"), sem("post1_done"), sem("d_dve"), sem("norm1_done")
        ost1_ready, o1T_ps, o1T_sb, y1_ps, x2_done = (sem(n) for n in (
            "ost1_ready", "o1T_ps", "o1T_sb", "y1_ps", "x2_done"))
        GU1, NU1, STEPS1 = 8, 32, NG1 // 4
        L_T, L_S, L_V, L_E, L_F, L_N = 2, 16, 20, 22, 31, 37
        MROW = 104

        def skewed1(eng, body):
            for u in range(NU1):
                body(0, u, lambda lag, u=u: u - lag >= 0)
            with eng.Fori(1, STEPS1) as i:
                for u in range(NU1):
                    body(i, u, lambda lag: True)
            for u in range(L_N - GU1 + 1):
                body(STEPS1, u, lambda lag, u=u: u - lag < 0 and lag > 0)

        def group1(i, v):
            return i * 4 + v // GU1

        def blocks1(v):
            return v % 2, range(v % GU1 // 2 * 4, v % GU1 // 2 * 4 + 4)

        with nc.Block() as block:
            @block.sync
            def _(sp):
                sp.dma_start(rows1[:, :, :], a["rows1"].rearrange("p (n x) -> p n x", n=3)).then_inc(d_in, 16)
                sp.dma_start(RV1[:, :, :], a["pick1"].unsqueeze(1).to_broadcast([P, B, 2 * (HD + 1)])).then_inc(rv_in, 16)
                sp.dma_start(wout[:, :], a["out_w"]).then_inc(d_in, 16)
                sp.dma_start(bout_row[:, :], a["out_b"].to_broadcast([P, D])).then_inc(d_in, 16)
                def load(st, pair, g):
                    rows = q1_parts[bass.ds(st, 1), :, pair * GW1:(pair + 1) * GW1, :]\
                        .rearrange("a t (d h) s -> (a t) d (h s)", d=HD)
                    for r, t in enumerate((0, 0, 0, 1, 1, 2)):
                        sp.dma_start(QS1[r * HD:(r + 1) * HD, g].rearrange("p h k s -> p (h k s)"),
                                     rows[t]).then_inc(stack1_in[g], 16)
                    rows = k1_parts[bass.ds(st, 1), :, pair * GW1:(pair + 1) * GW1, :]\
                        .rearrange("a t (d h) s -> (a t) d (h s)", d=HD)
                    for r, t in enumerate((0, 1, 2, 0, 1, 0)):
                        sp.dma_start(KS1[r * HD:(r + 1) * HD, g].rearrange("p h k s -> p (h k s)"),
                                     rows[t]).then_inc(stack1_in[g], 16)
                    rows = r1_parts[bass.ds(st, 1)].rearrange("a t f (k g h) s -> g (a t f k) (h s)", g=NPAIR, h=2)
                    sp.dma_start(QS1[NROW:NROW + 3 * B, g].rearrange("p h k s -> p (h k s)"),
                                 rows[pair]).then_inc(stack1_in[g], 16)

                def put_maxima(j, g):
                    sp.wait_ge(n1_split, j * 4 + 4)
                    for t in range(3):
                        sp.dma_start(QS1[MROW + t:MROW + t + 1, g].rearrange("p h k s -> p (h k) s"),
                                     NP1[:, t, :]).then_inc(max1_in[g], 16)
                for g in range(3):
                    sp.wait_ge(d_rows, g + 1)
                    load(0, g, g)
                sp.wait_ge(d_rows, 4)
                sp.wait_ge(rv_in, 16)
                for t in range(B):
                    for h in range(2):
                        sp.dma_start(RV1[64 * h + 32:64 * h + 32 + B, t, h * (HD + 1):h * (HD + 1) + HD],
                                     a["relv"][MAXREL - t:MAXREL - t + B, :]).then_inc(rv_in, 16)
                with sp.Fori(0, NST - 1) as st:
                    for pair in range(NPAIR):
                        g = pair % 4
                        put_maxima(st * NPAIR + pair, g)
                        wait_apart(sp, exp1_done, st * (2 * NU1) + (pair * GU1 + 2))
                        load(st + (pair + 3) // NPAIR, (pair + 3) % NPAIR, (g + 3) % 4)
                for pair in range(NPAIR):
                    g = pair % 4
                    put_maxima((NST - 1) * NPAIR + pair, g)
                    if pair + 3 < NPAIR:
                        sp.wait_ge(exp1_done, (NST - 1) * 2 * NU1 + pair * GU1 + 2)
                        load(NST - 1, pair + 3, (g + 3) % 4)

            @block.gpsimd
            def _(pool):
                nc.gpsimd.memset(VG1[:, :, :, :], 0.0).then_inc(d_vg, 1)
                pool.wait_ge(d_in, 48)
                pool.wait_ge(d_vg, 1)
                for g in range(2):
                    for h in range(2):
                        c0 = 3 * HD
                        ins = nc.gpsimd.tensor_copy(VG1_heads[:, g, :, h, c0:c0 + 24],
                                                    rows1[:, 2, 0:24].unsqueeze(1).to_broadcast([P, NBT, 24]))
                ins.then_inc(d_vg, 1)
                pool.sem_inc(p21_done, RING)

                with pool.Fori(0, NG1) as j:
                    for v in range(GU1):
                        pool.wait_ge(p11_done, j * GU1 + (v + 1))
                        nc.gpsimd.tensor_tensor(P21[:, v % RING, :], PR1[:, v % RING, :], P11[:, v % RING, :],
                                                ALU.subtract).then_inc(p21_done, 1)

                with pool.Fori(0, B) as b:
                    nc.gpsimd.tensor_tensor(b_tiles(X, b), b_tiles(X, b),
                                            bout_row[:, :].unsqueeze(1).to_broadcast([P, NST, D]), ALU.add).then_inc(xb2_done, 1)

            @block.tensor
            def _(pe):
                pe.wait_ge(d_vg, 2)
                pe.wait_ge(d_in, 48)
                pe.sem_inc(pv1_done, RING)

                def body(i, u, has):
                    if has(0):
                        g = u // GU1
                        h, ks = blocks1(u)
                        if u % GU1 == 0:
                            pe.wait_ge(stack1_in[g], i * 208 + 208)
                        pe.wait_ge(max1_done, i * NU1 + (u + 1))
                        for n, k in enumerate(ks):
                            ins = nc.tensor.matmul(psS1[:, u % 2, n * P:(n + 1) * P], QS1[0:MROW, g, h, k, :],
                                                   KS1[0:MROW, g, h, k, :], start=True, stop=True)
                        ins.then_inc(s1_done, 1)
                    if has(L_T) and (u - L_T) % GU1 == GU1 - 1:
                        v = u - L_T
                        pe.wait_ge(max1_done, i * NU1 + (v + 3))
                        if has(L_T + GU1):
                            pe.wait_ge(n1_split, group1(i, v) * 4 - 2)
                        nc.tensor.transpose(psN1, NM1[:, v // GU1 % 2, :], ident[:, :]).then_inc(nt1_done, 1)
                    if has(L_S):
                        v = u - L_S
                        g = v // GU1 % 4
                        h, ks = blocks1(v)
                        if v % GU1 == 0:
                            pe.wait_ge(max1_in[g], (i + v // NU1) * 48 + 48)
                        pe.wait_ge(exp1_done, i * NU1 + (v + 1))
                        for n, k in enumerate(ks):
                            ins = nc.tensor.matmul(psST1[:, v % 2, n * P:(n + 1) * P],
                                                   KS1[0:MROW + 3, g, h, k, :], QS1[0:MROW + 3, g, h, k, :], start=True, stop=True)
                        ins.then_inc(st1_done, 1)
                    if has(L_V):
                        v = u - L_V
                        g = v // GU1 % 2
                        h, ks = blocks1(v)
                        if v % GU1 == 0:
                            pe.wait_ge(v1_split, group1(i, v) * 4 + 4)
                        if h == 0:
                            pe.wait_ge(o1_evac, i * (NU1 // 2) + (v // 2 + 1))
                        pe.wait_ge(p21_done, i * NU1 + (v + (1 + RING)))
                        for n, k in enumerate(ks):
                            for m, part in enumerate((P11, P21)):
                                ins = nc.tensor.matmul(psO1[:, v // 2 % 2, n * P:(n + 1) * P], VG1[:, g, k, 64 * h:64 * h + P],
                                                       part[:, v % RING, n * P:(n + 1) * P], start=(h == n == m == 0),
                                                       stop=(h == m == 1 and n == 3))
                        ins.then_inc(pv1_done, 1)
                    if has(L_F) and (u - L_F) % GU1 < 6:
                        v = u - L_F
                        r = v % GU1
                        if r == 0:
                            if isinstance(i, int) and i == 0:
                                pe.wait_ge(rv_in, 16 + 32 * 16)
                            pe.wait_ge(o1_evac, group1(i, v) * 4 + 6)
                            pe.wait_ge(norm1_done, group1(i, v) + 2)
                        for t in ((0, 3, 6, 9, 12, 14, 16)[r] + m for m in range((3, 3, 3, 3, 2, 2)[r])):
                            ins = nc.tensor.matmul(psF1[:, t, :], OS1[:, v // GU1 % 2, t].rearrange("p k s -> p (k s)"),
                                                   RV1[:, t, :], start=True, stop=True)
                        if r == 5:
                            ins.then_inc(post1_done, 1)
                skewed1(pe, body)

                def transposes(n, s):
                    pe.wait_ge(ost1_ready, n + 1)
                    pe.wait_ge(o1T_sb, n + 1)
                    for k in range(NST):
                        ins = nc.tensor.transpose(psS1[:, s, k * P:(k + 1) * P], OST1[:, s, k, :], ident[:, :])
                    ins.then_inc(o1T_ps, 1)

                def products(n, s):
                    pe.wait_ge(o1T_sb, n + 3)
                    pe.wait_ge(x2_done, n + 1)
                    for k in range(NST):
                        ins = nc.tensor.matmul(psO1[:, s, k * P:(k + 1) * P], OT1[:, s, k * P:(k + 1) * P], wout[:, :],
                                               start=True, stop=True)
                    ins.then_inc(y1_ps, 1)
                transposes(0, 0)
                with pe.Fori(0, B // 2 - 1) as i:
                    for s in range(2):
                        transposes(i * 2 + (s + 1), 1 - s)
                        products(i * 2 + s, s)
                transposes(B - 1, 1)
                products(B - 2, 0)
                products(B - 1, 1)

            @block.scalar
            def _(act):
                act.sem_inc(exp1_done, 2)

                def body(i, u, has):
                    if has(L_S):
                        v = u - L_S
                        act.wait_ge(st1_done, i * NU1 + (v + 1))
                        act.wait_ge(p21_done, i * NU1 + (v + 1))
                        nc.scalar.activation(PR1[:, v % RING, :], psST1[:, v % 2, :], ACT.Exp).then_inc(exp1_done, 1)
                    if has(L_S + 1):
                        v = u - L_S - 1
                        act.wait_ge(exp1_done, i * NU1 + (v + 3))
                        act.wait_ge(pv1_done, i * NU1 + (v + 1))
                        nc.scalar.copy(P11[:, v % RING, :], PR1[:, v % RING, :]).then_inc(p11_done, 1)
                skewed1(act, body)
                act.sem_inc(o1T_sb, 2)
                act.sem_inc(o1T_ps, 2)

                def token_major(n, s):
                    act.wait_ge(o1T_ps, n + 1)
                    src = VT.rearrange("p j (t x) -> p j t x", t=B)[:, :, bass.ds(n, 1), :]
                    nc.scalar.copy(OST1[:, s].rearrange("p n (g x) -> p (n g) x", g=NPAIR),
                                   src.rearrange("p j a x -> p j (a x)")).then_inc(ost1_ready, 1)
                act.wait_ge(norm1_done, NG1 + 2)
                token_major(0, 0)

                def step(b, s, last):
                    if not last:
                        token_major(b + 1, 1 - s)
                    act.wait_ge(o1T_ps, b + 3)
                    act.wait_ge(y1_ps, b + 1)
                    nc.scalar.copy(OT1[:, s, :], psS1[:, s, :]).then_inc(o1T_sb, 1)
                two_steps(act, step)

            @block.vector
            def _(dve):
                dve.sem_inc(max1_done, 2)
                dve.sem_inc(norm1_done, 2)
                dve.sem_inc(post1_done, 2)
                dve.sem_inc(o1_evac, 2)
                dve.sem_inc(y1_ps, 2)
                dve.sem_inc(x2_done, 2)
                dve.wait_ge(d_in, 48)
                nc.vector.tensor_copy(rows1b[:, :, :], rows1[:, 0:2, :]).then_inc(d_const, 1)
                dve.wait_ge(d_const, 1)
                for g in range(4):
                    for n, stack in enumerate((QS1, KS1)):
                        ins = nc.vector.tensor_copy(stack[:, g].rearrange("p h k s -> p (h k) s"),
                                                    rows1b[:, n:n + 1, :].to_broadcast([P, 2 * NBT, P]))
                    ins.then_inc(d_rows, 1)
                dve.wait_ge(d_vg, 2)

                def body(i, u, has):
                    if has(0):
                        g, h, c = u // GU1, u % 2, u % GU1 // 2
                        dve.wait_ge(s1_done, i * NU1 + (u + 1))
                        nc.vector.tensor_reduce(NM1[:, g % 2, h * NBT + 4 * c:h * NBT + 4 * c + 4],
                                                psS1[:, u % 2, :].rearrange("p (k s) -> p k s", k=4), AX.X, ALU.max,
                                                negate=True).then_inc(max1_done, 1)
                    if has(L_E) and (u - L_E) % 2 == 1:
                        v = u - L_E
                        c = v % GU1 // 2
                        dve.wait_ge(pv1_done, i * NU1 + (v + (1 + RING)))
                        if c == 0:
                            dve.wait_ge(post1_done, group1(i, v) + 1)
                        nc.vector.tensor_copy(OS1[:, v // GU1 % 2, :, 4 * c:4 * c + 4, :],
                                              psO1[:, v // 2 % 2, :].rearrange("p (k t s) -> p t k s", k=4, t=B))\
                            .then_inc(o1_evac, 1)
                    if has(GU1) and (u - GU1) % GU1 in (2, 3):
                        v = u - GU1
                        j, n, g = group1(i, v), v % GU1, v // GU1 % 4
                        if n == 2:
                            dve.wait_ge(nt1_done, j + 1)
                            if has(2 * GU1):
                                dve.wait_ge(max1_in[(g - 1) % 4], (i + v // NU1) * 48 + (48 if g else 0))
                            nc.vector.tensor_scalar(NP1[:, 0, :], psN1, GAIN, None, ALU.add).then_inc(n1_split, 1)
                            dve.wait_ge(n1_split, j * 4 + 1)
                            nc.vector.scalar_tensor_tensor(NR1[:, :], psN1, GAIN, NP1[:, 0, :],
                                                           ALU.add, ALU.subtract).then_inc(n1_split, 1)
                        else:
                            dve.wait_ge(n1_split, j * 4 + 2)
                            nc.vector.tensor_copy(NP1[:, 1, :], NR1[:, :]).then_inc(n1_split, 1)
                            dve.wait_ge(n1_split, j * 4 + 3)
                            nc.vector.tensor_tensor(NP1[:, 2, :], NR1[:, :], NP1[:, 1, :], ALU.subtract).then_inc(n1_split, 1)
                    if has(GU1) and (u - GU1) % GU1 in (4, 5, 6, 7):
                        v = u - GU1
                        j, n, g = group1(i, v), v % GU1 - 4, v // GU1 % 2
                        rest = VR1[:, :, :].rearrange("p k (h e) -> p k h e", e=HD)
                        part = [VG1_heads[:, g, :, :, t * HD:(t + 1) * HD] for t in range(3)]
                        src = VT[:, bass.ds(j, 1)].rearrange("p a (k h e) -> p (a k) h e", k=NBT, e=HD)
                        if n == 0:
                            if has(2 * GU1):
                                dve.wait_ge(pv1_done, i * NU1 + (v // GU1 * GU1 - GU1 + RING))
                            nc.vector.tensor_copy(part[0], src).then_inc(v1_split, 1)
                        elif n == 1:
                            dve.wait_ge(v1_split, j * 4 + 1)
                            nc.vector.tensor_tensor(rest, src, part[0], ALU.subtract).then_inc(v1_split, 1)
                        elif n == 2:
                            dve.wait_ge(v1_split, j * 4 + 2)
                            nc.vector.tensor_copy(part[1], rest).then_inc(v1_split, 1)
                        else:
                            dve.wait_ge(v1_split, j * 4 + 3)
                            nc.vector.tensor_tensor(part[2], rest, part[1], ALU.subtract).then_inc(v1_split, 1)
                    if has(L_N) and (u - L_N) % GU1 == 0:
                        v = u - L_N
                        j, g = group1(i, v), v // GU1 % 2
                        heads = psF1.rearrange("p t (h x) -> p (t h) x", x=HD + 1)
                        dve.wait_ge(post1_done, j + 3)
                        nc.vector.reciprocal(RI1[:, g], heads[:, :, HD:HD + 1].rearrange("p n a -> p (n a)")).then_inc(d_dve, 1)
                        dve.wait_ge(d_dve, j + 1)
                        nc.vector.tensor_tensor(
                            VT[:, bass.ds(j, 1)].rearrange("p a (n e) -> p (a n) e", e=HD), heads[:, :, 0:HD],
                            RI1[:, g].unsqueeze(2).to_broadcast([P, 2 * B, HD]), ALU.mult).then_inc(norm1_done, 1)
                skewed1(dve, body)
                with dve.Fori(0, B // 2) as i:
                    for s in range(2):
                        dve.wait_ge(xb2_done, i * 2 + (s + 1))
                        dve.wait_ge(y1_ps, i * 2 + (s + 3))
                        x = b_tiles(X, i * 2 + s)
                        nc.vector.tensor_tensor(x, psO1[:, s, :].rearrange("p (n d) -> p n d", n=NST), x, ALU.add)\
                            .then_inc(x2_done, 1)
        pd.close()

        pe_ = ExitStack()
        carved[0] = 0
        GUW = carve([P, NE, 2 * FI])
        DW = carve([P, NE, len(FC), D])
        GUWf, DWf = GUW.rearrange("p e f -> p (e f)"), DW.rearrange("p e c d -> p (e c d)")
        XB, XBT = carve([P, 4, P]), carve([P, 2, P])
        TH, HH = carve([P, 2, FI]), carve([P, 2, FI])
        HT, YB = carve([P, 2, 3 * P]), carve([P, 4, D])
        psGU = ps(pe_, "psGU", [P, 2, 2, S])
        psXB = ps(pe_, "psXB", [P, S])
        psHT = ps(pe_, "psHT", [P, 3, P])
        psY = ps(pe_, "psY", [P, 2, S])
        ew_in = sem("ew_in")
        xb_in = [sem(f"xb_in{n}") for n in range(4)]
        y2_out = [sem(f"y2_out{n}") for n in range(4)]
        e_silu = sem("e_silu")
        xb_ps, xb_sb, gu_ps, th_sb, hh_sb, ht_ps, ht_sb, y2_ps, y2_sb = (sem(n) for n in (
            "xb_ps", "xb_sb", "gu_ps", "th_sb", "hh_sb", "ht_ps", "ht_sb", "y2_ps", "y2_sb"))
        a_add, out_done = sem("a_add"), sem("out_done")
        gathered = [sem(f"gathered{b}") for b in range(0, B, 2)]

        def staged(eng, body):
            for u in range(4):
                body(0, u, lambda lag, u=u: u - lag >= 0)
            with eng.Fori(1, NBLK // 4) as i:
                for u in range(4):
                    body(i, u, lambda lag: True)
            for u in range(3):
                body(NBLK // 4, u, lambda lag, u=u: u - lag < 0)

        with nc.Block() as block:
            @block.sync
            def _(sp):
                sp.dma_start(GUW, a["gate_up"].rearrange("p (e f) -> p e f", e=NE)).then_inc(ew_in, 16)
                for c, w in enumerate(FC):
                    sp.dma_start(DW[0:w, :, c, :], a["down"][c * P:c * P + w, :].rearrange("p (e d) -> p e d", e=NE))\
                      .then_inc(ew_in, 16)
                sp.sem_inc(xb_ps, 4)
                for s in range(4):
                    sp.sem_inc(y2_out[s], 16)

                def load(n, s):
                    sp.wait_ge(xb_ps, n + 1)
                    sp.dma_start(XB[:, s, :], sorted_x[bass.ds(n * P, P), :]).then_inc(xb_in[s], 16)

                def store(n, s):
                    sp.wait_ge(y2_sb, n + 3)
                    sp.dma_start(sorted_y[bass.ds(n * P, P), :], YB[:, s, :]).then_inc(y2_out[s], 16)
                for n in range(8):
                    load(n, n % 4)
                with sp.Fori(1, NBLK // 4 - 1) as i:
                    for s in range(4):
                        load(i * 4 + (s + 4), s)
                        store(i * 4 + (s - 4), s)
                for n in range(NBLK - 8, NBLK):
                    store(n, n % 4)
                for b in range(B):
                    sp.wait_ge(a_add, b + 1)
                    sp.dma_start(out[b].rearrange("(n p) d -> p n d", p=P), X[:, b]).then_inc(out_done, 16)
                sp.wait_ge(out_done, 16 * B)

            @block.vector
            def _(dve):
                dve.sem_inc(y2_sb, 2)
                dve.sem_inc(hh_sb, 2)

                def body(i, u, has):
                    n = i * 4 + u
                    if has(1):
                        s = (u - 1) % 2
                        dve.wait_ge(th_sb, n)
                        nc.vector.scalar_tensor_tensor(TH[:, s, :], TH[:, s, :], 1.0, psGU[:, s, 0, 0:FI],
                                                       ALU.add, ALU.mult).then_inc(e_silu, 1)
                        dve.wait_ge(e_silu, n)
                        dve.wait_ge(ht_ps, n)
                        nc.vector.scalar_tensor_tensor(HH[:, s, :], TH[:, s, :], 0.5, psGU[:, s, 1, 0:FI],
                                                       ALU.mult, ALU.mult).then_inc(hh_sb, 1)
                    if has(3):
                        s = (u - 3) % 4
                        dve.wait_ge(y2_ps, n)
                        dve.wait_ge(y2_out[s], (i + (u - 3) // 4) * 16 + 16)
                        nc.vector.tensor_copy(YB[:, s, :], psY[:, s % 2, 0:D]).then_inc(y2_sb, 1)
                staged(dve, body)
                for b in range(B):
                    dve.wait_ge(gathered[b // 2], 16 * NST * 2)
                    nc.vector.tensor_tensor(X[:, b], X[:, b], HX[:, b], ALU.add).then_inc(a_add, 1)

            @block.scalar
            def _(act):
                act.sem_inc(xb_sb, 1)
                act.sem_inc(ht_sb, 1)

                def body(i, u, has):
                    n = i * 4 + u
                    if has(0):
                        act.wait_ge(xb_ps, n + 5)
                        act.wait_ge(gu_ps, n + 1)
                        nc.scalar.copy(XBT[:, u % 2, :], psXB[:, 0:P]).then_inc(xb_sb, 1)
                    if has(1):
                        s = (u - 1) % 2
                        act.wait_ge(gu_ps, n + 2)
                        nc.scalar.activation(TH[:, s, :], psGU[:, s, 0, 0:FI], ACT.Tanh, scale=0.5).then_inc(th_sb, 1)
                    if has(2):
                        act.wait_ge(ht_ps, n + 1)
                        act.wait_ge(y2_ps, n - 1)
                        nc.scalar.copy(HT[:, u % 2, 0:2 * P], psHT[:, 0:2, :].rearrange("p c s -> p (c s)"))
                        nc.scalar.copy(HT[0:FC[2], u % 2, 2 * P:3 * P], psHT[0:FC[2], 2, :]).then_inc(ht_sb, 1)
                staged(act, body)

            @block.tensor
            def _(pe):
                pe.wait_ge(ew_in, 64)

                def expert(n):
                    return pe.value_load(eb[0:1, bass.ds(n, 1)], min_val=0, max_val=NE - 1)

                pe.sem_inc(gu_ps, 2)
                pe.sem_inc(ht_ps, 2)
                pe.sem_inc(y2_ps, 2)

                def body(i, u, has):
                    n = i * 4 + u
                    if has(0):
                        pe.wait_ge(xb_in[u], i * 16 + 16)
                        pe.wait_ge(xb_sb, n + 1)
                        nc.tensor.transpose(psXB[:, 0:P], XB[:, u, :], ident[:, :]).then_inc(xb_ps, 1)
                    if has(1):
                        s = (u - 1) % 2
                        pe.wait_ge(xb_sb, n + 1)
                        wait_apart(pe, hh_sb, n)
                        e = expert(n - 1)
                        for c in range(2):
                            ins = nc.tensor.matmul(psGU[:, s, c, 0:FI], XBT[:, s, :],
                                                   GUWf[:, bass.ds(e * (2 * FI) + c * FI, FI)], start=True, stop=True)
                        ins.then_inc(gu_ps, 1)
                    if has(2):
                        pe.wait_ge(hh_sb, n + 1)
                        pe.wait_ge(ht_sb, n - 1)
                        for c, w in enumerate(FC):
                            ins = nc.tensor.transpose(psHT[0:w, c, :], HH[:, u % 2, c * P:c * P + w], ident[:, :])
                        ins.then_inc(ht_ps, 1)
                    if has(3):
                        s = (u - 3) % 2
                        pe.wait_ge(ht_sb, n - 1)
                        wait_apart(pe, y2_sb, n - 2)
                        e = expert(n - 3)
                        for c, w in enumerate(FC):
                            ins = nc.tensor.matmul(psY[:, s, 0:D], HT[0:w, s, c * P:(c + 1) * P],
                                                   DWf[0:w, bass.ds(e * (3 * D) + c * D, D)], start=(c == 0), stop=(c == 2))
                        ins.then_inc(y2_ps, 1)
                staged(pe, body)

            @block.gpsimd
            def _(pool):
                for s in range(4):
                    pool.wait_ge(y2_out[s], 16 * (NBLK // 4 + 1))
                for b in range(B):
                    for st in range(NST):
                        j = b * NST + st
                        pool.indirect_dma_start(HX[:, b, st, :], None, sorted_y,
                                                bass.IndirectOffsetOnAxis(pos[:, j:j + 1], 0)).then_inc(gathered[b // 2], 16)
        pe_.close()


def kernel(**inputs):
    import numpy as _np
    import concourse.bacc as _bacc
    from concourse import mybir as _mybir
    from concourse.bass_utils import run_bass_kernel_spmd as _run

    v = {k: _np.asarray(x) for k, x in inputs.items()}

    def heads_inner(w):
        w = _np.moveaxis(w, 0, -2)
        w = w.reshape(w.shape[:-2] + (NG, HG, HD))
        return _np.swapaxes(w, -1, -2).reshape(w.shape[:-3] + (D,))

    def pairs_inner(w):
        return _np.swapaxes(w.reshape(w.shape[:-1] + (NPAIR, 2, HD)), -1, -2).reshape(w.shape)

    in_w = [w.T for w in v["L1_attn_in_proj_weight"].reshape(3, D, D)]
    in_b = v["L1_attn_in_proj_bias"].reshape(3, D)
    eye = _np.eye(P, dtype=_np.float32)
    n = _np.arange(P)
    rows1 = _np.zeros((P, 3, P), _np.float32)
    for r in range(3 * B):
        rows1[6 * HD + r, 1] = n // BS == r % B
    for r in range(BS):
        rows1[6 * HD + 3 * B + r, 0] = _np.where(n % BS == r, 0.0, NEG)
        rows1[6 * HD + 3 * B + r, 1] = n % BS == r
    rows1[6 * HD + 3 * B + BS:6 * HD + 3 * B + BS + 3, 1] = 1.0
    rows1[:, 2, 0] = 1.0
    rows1[:, 2, HD:HD + B] = n[:, None] // BS == _np.arange(B)[None, :]
    pick1 = _np.stack([(n // 64 == h) & ((n % 64 == 3 * HD) if e == HD else (n % 64 < 3 * HD) & (n % HD == e))
                       for h in range(2) for e in range(HD + 1)], axis=1).astype(_np.float32)
    arrays = {
        "x": v["L0_attn_inputs"],
        "weights": _np.concatenate([heads_inner(v["L0_attn_W_q"]), heads_inner(v["L0_attn_W_k"]),
                                    v["L0_attn_W_v"].transpose(1, 0, 2).reshape(D, D)]
                                   + [v["L0_ffn_" + w].T for w in ("wf", "wi", "wc", "wo", "uf", "ui", "uc", "uo")], axis=1),
        "bias_cols": _np.stack([heads_inner(v["L0_attn_b_q"]).reshape(D), heads_inner(v["L0_attn_b_k"]).reshape(D)]
                               + [v["L0_ffn_" + b] for b in ("bf", "bi", "bc", "in_c")], axis=1),
        "bv": v["L0_attn_b_v"].reshape(1, D),
        "attn_wo": v["L0_attn_W_o"].T, "attn_bo": v["L0_attn_b_o"].reshape(1, D),
        "ffn_bo": v["L0_ffn_bo"].reshape(1, D),
        "in_proj": _np.concatenate([pairs_inner(in_w[0]), pairs_inner(in_w[1]), in_w[2]], axis=1),
        "in_bias_qk": _np.stack([pairs_inner(in_b[0]), pairs_inner(in_b[1])], axis=1), "in_bias_v": in_b[2].reshape(1, D),
        "relk": _np.tile(_np.repeat(v["L1_attn_rel_k_table"].T, 2, axis=0), (NPAIR, 1)),
        "relv": v["L1_attn_rel_v_table"],
        "out_w": v["L1_attn_out_w"].T, "out_b": v["L1_attn_out_b"].reshape(1, D),
        "router": v["L1_ffn_router_w"].T,
        "gate_up": _np.concatenate([v["L1_ffn_gate_w"], v["L1_ffn_up_w"]], axis=1).transpose(2, 0, 1).reshape(D, NE * 2 * FI),
        "down": v["L1_ffn_down_w"].transpose(2, 0, 1).reshape(FI, NE * D),
        "ident": eye, "ones": _np.ones((P, P), _np.float32),
        "before": (n[:, None] < n[None, :]).astype(_np.float32),
        "mask": _np.where(n[None, :] > n[:, None], NEG, 0.0).astype(_np.float32),
        "sel": (n[:, None] // GW1 * 2 + n[:, None] % 2 == _np.arange(NH)[None, :]).astype(_np.float32),
        "rows1": rows1.reshape(P, 3 * P), "pick1": pick1,
        "pick": _np.stack([(n // GW == h) & ((n % GW == 3 * HD) if e == HD else (n % GW < 3 * HD) & (n % HD == e))
                           for h in range(HG) for e in range(HD + 1)], axis=1).astype(_np.float32),
        "iota8": _np.arange(NE, dtype=_np.float32).reshape(1, NE) - NE,
        "iota64": _np.arange(NTILE, dtype=_np.float32).reshape(1, NTILE) * P,
        "iotab": _np.arange(NBLK, dtype=_np.float32).reshape(1, NBLK),
    }

    nc = _bacc.Bacc("TRN2", target_bir_lowering=False, num_devices=1)
    aps = {}
    arrays = {k: _np.ascontiguousarray(x) for k, x in arrays.items()}
    for k, x in arrays.items():
        aps[k] = nc.dram_tensor(f"in_{k}", x.shape, _mybir.dt.from_np(x.dtype), kind="ExternalInput").ap()
    out = nc.dram_tensor("out", (B, S, D), F32, kind="ExternalOutput").ap()
    program(nc, aps, out)
    r = _run(nc, [{f"in_{k}": x for k, x in arrays.items()}], core_ids=[0])
    return r.results[0]["out"]
```
